# Optimizing a Trainium2 kernel written in Bass

```python
import numpy as np
import jax
import jax.numpy as jnp

def _softmax(x, axis=-1):
    return jax.nn.softmax(x, axis=axis)

def _gelu(x):
    return jax.nn.gelu(x, approximate=True)

def _silu(x):
    return jax.nn.silu(x)

def _sigmoid(x):
    return jax.nn.sigmoid(x)

def _layernorm(x, axis=-1, eps=1e-05):
    m = jnp.mean(x, axis=axis, keepdims=True)
    v = jnp.var(x, axis=axis, keepdims=True)
    return (x - m) / jnp.sqrt(v + eps)

def _scatter_add(tgt, idx, src, axis=0):
    return tgt.at[idx].add(src)

def _segment_sum(src, seg, n):
    return jax.ops.segment_sum(src, seg, n)
kernel_name = 'mk_gnn_ffn_d4_gnn_r16_3650dd'

def setup_inputs(seed: int=0):
    np.random.seed(seed)
    _w = jnp.asarray

    def _rec_inputs():
        import jax
        import jax.numpy as jnp
        _gk = jax.random.key(seed)
        x = -0.0003713 + 1 * jax.random.normal(jax.random.fold_in(_gk, 1), (3125, 256), jnp.float32)
        _s = jax.random.randint(jax.random.fold_in(_gk, 2), (25000,), 0, 3125, jnp.int32)
        _d = jax.random.randint(jax.random.fold_in(_gk, 3), (25000,), 0, 3125, jnp.int32)
        _loop = jnp.arange(3125, dtype=jnp.int32)
        src = jnp.concatenate([_s, _d, _loop])
        dst = jnp.concatenate([_d, _s, _loop])
        _o = jnp.argsort(dst, stable=True)
        src = src[_o]
        dst = dst[_o]
        edge_attr_3 = -1.09012e-05 + 0.99985 * jax.random.normal(jax.random.fold_in(_gk, 11), (53125, 3), jnp.float32)
        edge_type_8 = jax.random.randint(jax.random.fold_in(_gk, 13), (53125,), 0, 8, jnp.int32)
        return (x, src, dst, edge_attr_3, edge_type_8)
    x, src, dst, edge_attr_3, edge_type_8 = _rec_inputs()

    def _L0_gnn_setup():
        import jax, jax.numpy as jnp
        import numpy as np
        NEG_SLOPE = 0.2

        def gatv2_layer(x, Wl, Wr, att, bias, src, dst, n_nodes, heads, ch, concat):
            xl = (x @ Wl).reshape(n_nodes, heads, ch)
            xr = (x @ Wr).reshape(n_nodes, heads, ch)
            m = xl[src] + xr[dst]
            e = jax.nn.leaky_relu(m, NEG_SLOPE)
            logits = jnp.einsum('ehc,hc->eh', e, att)
            mx = jax.ops.segment_max(logits, dst, num_segments=n_nodes)
            ex = jnp.exp(logits - mx[dst])
            denom = jax.ops.segment_sum(ex, dst, num_segments=n_nodes)
            alpha = ex / denom[dst]
            out = jax.ops.segment_sum(alpha[:, :, None] * xl[src], dst, num_segments=n_nodes)
            if concat:
                out = out.reshape(n_nodes, heads * ch)
            else:
                out = out.mean(axis=1)
            return out + bias
        N, E = (3125, 50000)
        IN, HID, OUT, H = (256, 64, 256, 4)
        key = jax.random.key(seed)
        ks = jax.random.split(key, 12)
        s = lambda fan_in: 1.0 / np.sqrt(fan_in)
        return {'x': jax.random.normal(ks[0], (N, IN), dtype=jnp.float32), 'edge_index': jax.random.randint(ks[1], (2, E), 0, N, dtype=jnp.int64), 'Wl1': jax.random.normal(ks[2], (IN, H * HID), jnp.float32) * s(IN), 'Wr1': jax.random.normal(ks[3], (IN, H * HID), jnp.float32) * s(IN), 'att1': jax.random.normal(ks[4], (H, HID), jnp.float32) * s(HID), 'b1': jnp.zeros((H * HID,), jnp.float32), 'Wl2': jax.random.normal(ks[5], (H * HID, OUT), jnp.float32) * s(H * HID), 'Wr2': jax.random.normal(ks[6], (H * HID, OUT), jnp.float32) * s(H * HID), 'att2': jax.random.normal(ks[7], (1, OUT), jnp.float32) * s(OUT), 'b2': jnp.zeros((OUT,), jnp.float32)}
    _L0_gnn_all = _L0_gnn_setup()
    _L0_gnn_in = {k: v for k, v in _L0_gnn_all.items() if k in ('Wl1', 'Wr1', 'att1', 'b1', 'Wl2', 'Wr2', 'att2', 'b2')}
    del _L0_gnn_all

    def _L0_ffn_setup():
        import jax, jax.numpy as jnp
        import numpy as np
        DIM = 256
        H = 8
        D = 64
        G = 64
        INNER = H * D
        SCALE = D ** (-0.5)
        key = jax.random.key(seed)
        ks = jax.random.split(key, 12)
        B, N = (4, 1024)
        x = jax.random.normal(ks[0], (B, N, DIM), dtype=jnp.float32)
        s = lambda fan_in: 1.0 / np.sqrt(fan_in)
        W_fx = jax.random.normal(ks[1], (DIM, INNER), dtype=jnp.float32) * s(DIM)
        b_fx = jnp.zeros((INNER,), dtype=jnp.float32)
        W_x = jax.random.normal(ks[2], (DIM, INNER), dtype=jnp.float32) * s(DIM)
        b_x = jnp.zeros((INNER,), dtype=jnp.float32)
        A = jax.random.normal(ks[3], (G, D), dtype=jnp.float32)
        Q, _ = jnp.linalg.qr(A.T)
        W_slice = Q[:, :G].astype(jnp.float32)
        b_slice = jnp.zeros((G,), dtype=jnp.float32)
        W_q = jax.random.normal(ks[4], (D, D), dtype=jnp.float32) * s(D)
        W_k = jax.random.normal(ks[5], (D, D), dtype=jnp.float32) * s(D)
        W_v = jax.random.normal(ks[6], (D, D), dtype=jnp.float32) * s(D)
        W_out = jax.random.normal(ks[7], (INNER, DIM), dtype=jnp.float32) * s(INNER)
        b_out = jnp.zeros((DIM,), dtype=jnp.float32)
        temperature = jnp.ones((1, H, 1, 1), dtype=jnp.float32) * 0.5
        return {'x': x, 'W_fx': W_fx, 'b_fx': b_fx, 'W_x': W_x, 'b_x': b_x, 'W_slice': W_slice, 'b_slice': b_slice, 'W_q': W_q, 'W_k': W_k, 'W_v': W_v, 'W_out': W_out, 'b_out': b_out, 'temperature': temperature}
    _L0_ffn_all = _L0_ffn_setup()
    _L0_ffn_in = {k: v for k, v in _L0_ffn_all.items() if k in ('W_fx', 'b_fx', 'W_x', 'b_x', 'W_slice', 'b_slice', 'W_q', 'W_k', 'W_v', 'W_out', 'b_out', 'temperature')}
    del _L0_ffn_all

    def _L1_gnn_setup():
        import jax, jax.numpy as jnp
        import numpy as np
        N_NODES = 3125
        N_EDGES = 50000
        IN_FEAT = 256
        OUT_FEAT = 256
        NUM_RELS = 8
        ALPHA = 0.5
        key = jax.random.key(seed)
        k1, k2, k3, k4, k5, k6 = jax.random.split(key, 6)
        x = jax.random.normal(k1, (N_NODES, IN_FEAT), dtype=jnp.float32)
        edge_index = jax.random.randint(k2, (2, N_EDGES), 0, N_NODES, dtype=jnp.int64)
        edge_type = jax.random.randint(k3, (N_EDGES,), 0, NUM_RELS, dtype=jnp.int64)
        gain = float(np.sqrt(2.0))
        lim_w = gain * float(np.sqrt(6.0 / (IN_FEAT + OUT_FEAT)))
        weight = jax.random.uniform(k4, (NUM_RELS, IN_FEAT, OUT_FEAT), dtype=jnp.float32, minval=-lim_w, maxval=lim_w)
        loop_weight = jax.random.uniform(k5, (IN_FEAT, OUT_FEAT), dtype=jnp.float32, minval=-lim_w, maxval=lim_w)
        h_bias = jnp.zeros((OUT_FEAT,), dtype=jnp.float32)
        return {'edge_index': edge_index, 'x': x, 'edge_type': edge_type, 'weight': weight, 'h_bias': h_bias, 'loop_weight': loop_weight}
    _L1_gnn_all = _L1_gnn_setup()
    _L1_gnn_in = {k: v for k, v in _L1_gnn_all.items() if k in ('weight', 'h_bias', 'loop_weight')}
    del _L1_gnn_all

    def _L1_ffn_setup():
        import jax, jax.numpy as jnp
        import numpy as np
        B, N, D = (16, 256, 256)
        NUM_EXPERTS, TOP_K, HEADS = (4, 2, 4)
        N_EDGES = 65536
        LN_EPS = 1e-05

        def _layernorm(x, g, b):
            mu = x.mean(-1, keepdims=True)
            var = ((x - mu) ** 2).mean(-1, keepdims=True)
            return (x - mu) * jax.lax.rsqrt(var + LN_EPS) * g + b

        def _forward(x, edge_index, W_gat, att_src, att_dst, b_gat, ln_gamma, ln_beta, W1, b1, W2, b2):
            Bc, Nc, Dc = x.shape
            M = Bc * Nc
            x_flat = x.reshape(M, Dc)
            h = (x_flat @ W_gat).reshape(M, HEADS, NUM_EXPERTS)
            loops = jnp.arange(M, dtype=edge_index.dtype)
            src = jnp.concatenate([edge_index[0], loops])
            dst = jnp.concatenate([edge_index[1], loops])
            a_src = (h * att_src).sum(-1)
            a_dst = (h * att_dst).sum(-1)
            e = jax.nn.leaky_relu(a_src[src] + a_dst[dst], negative_slope=0.2)
            e_max = jax.ops.segment_max(e, dst, num_segments=M)
            ee = jnp.exp(e - e_max[dst])
            denom = jax.ops.segment_sum(ee, dst, num_segments=M)
            alpha = ee / (denom[dst] + 1e-16)
            msg = h[src] * alpha[:, :, None]
            agg = jax.ops.segment_sum(msg, dst, num_segments=M).reshape(M, HEADS * NUM_EXPERTS) + b_gat
            scores = _layernorm(agg, ln_gamma, ln_beta).reshape(M, HEADS, NUM_EXPERTS).mean(1)
            scores = scores.reshape(Bc, Nc, NUM_EXPERTS)
            topk_s, topk_i = jax.lax.top_k(scores, TOP_K)
            w = jax.nn.softmax(topk_s, axis=-1)
            out = jnp.zeros_like(x)
            for ei in range(NUM_EXPERTS):
                g = jnp.where(topk_i == ei, w, 0.0).sum(-1)
                hh = jax.nn.gelu(x @ W1[ei] + b1[ei], approximate=False)
                out = out + g[..., None] * (hh @ W2[ei] + b2[ei])
            return out
        key = jax.random.key(seed)
        ks = jax.random.split(key, 8)
        s = 0.05
        return {'x': jax.random.normal(ks[0], (B, N, D), jnp.float32), 'W_gat': jax.random.normal(ks[1], (D, HEADS * NUM_EXPERTS), jnp.float32) * s, 'att_src': jax.random.normal(ks[2], (HEADS, NUM_EXPERTS), jnp.float32) * s, 'att_dst': jax.random.normal(ks[3], (HEADS, NUM_EXPERTS), jnp.float32) * s, 'b_gat': jnp.zeros((HEADS * NUM_EXPERTS,), jnp.float32), 'ln_gamma': jnp.ones((HEADS * NUM_EXPERTS,), jnp.float32), 'ln_beta': jnp.zeros((HEADS * NUM_EXPERTS,), jnp.float32), 'W1': jax.random.normal(ks[4], (NUM_EXPERTS, D, 2 * D), jnp.float32) * s, 'b1': jnp.zeros((NUM_EXPERTS, 2 * D), jnp.float32), 'W2': jax.random.normal(ks[5], (NUM_EXPERTS, 2 * D, D), jnp.float32) * s, 'b2': jnp.zeros((NUM_EXPERTS, D), jnp.float32), 'edge_index': jax.random.randint(ks[6], (2, N_EDGES), 0, B * N, jnp.int32)}
    _L1_ffn_all = _L1_ffn_setup()
    _L1_ffn_in = {k: v for k, v in _L1_ffn_all.items() if k in ('W_gat', 'att_src', 'att_dst', 'b_gat', 'ln_gamma', 'ln_beta', 'W1', 'b1', 'W2', 'b2', 'edge_index')}
    del _L1_ffn_all

    def _L2_gnn_setup():
        import jax, jax.numpy as jnp
        import numpy as np
        N = 625
        E = 18750
        D = 256
        key = jax.random.key(seed)
        k1, k2, k3, k4 = jax.random.split(key, 4)
        x = jax.random.normal(k1, (N, D), dtype=jnp.float32)
        edge_index = jax.random.randint(k2, (2, E), 0, N, dtype=jnp.int32)
        s = 1.0 / np.sqrt(D)
        W1 = jax.random.uniform(k3, (D, D), jnp.float32, -s, s)
        b1 = jnp.zeros((D,), jnp.float32)
        W2 = jax.random.uniform(k4, (D, D), jnp.float32, -s, s)
        b2 = jnp.zeros((D,), jnp.float32)
        return {'x': x, 'W1': W1, 'b1': b1, 'W2': W2, 'b2': b2, 'edge_index': edge_index}
    _L2_gnn_all = _L2_gnn_setup()
    _L2_gnn_in = {k: v for k, v in _L2_gnn_all.items() if k in ('W1', 'b1', 'W2', 'b2')}
    del _L2_gnn_all

    def _L2_ffn_setup():
        import jax, jax.numpy as jnp
        import numpy as np
        B, K, D = (512, 16, 256)
        E = 32
        H = int(D * 0.25)
        key = jax.random.key(seed)
        ks = jax.random.split(key, 7)
        d_rs = D ** (-0.5)
        h_rs = H ** (-0.5)
        x = jax.random.normal(ks[0], (B, K, D), dtype=jnp.float32)
        router_w = jax.random.uniform(ks[1], (E, D), jnp.float32, -d_rs, d_rs)
        router_b = jax.random.uniform(ks[2], (E,), jnp.float32, -d_rs, d_rs)
        W1 = jax.random.uniform(ks[3], (E, D, H), jnp.float32, -h_rs, h_rs)
        b1 = jax.random.uniform(ks[4], (E, H), jnp.float32, -h_rs, h_rs)
        W2 = jax.random.uniform(ks[5], (E, H, D), jnp.float32, -d_rs, d_rs)
        b2 = jax.random.uniform(ks[6], (E, D), jnp.float32, -d_rs, d_rs)
        return {'x': x, 'router_w': router_w, 'router_b': router_b, 'W1': W1, 'b1': b1, 'W2': W2, 'b2': b2}
    _L2_ffn_all = _L2_ffn_setup()
    _L2_ffn_in = {k: v for k, v in _L2_ffn_all.items() if k in ('router_w', 'router_b', 'W1', 'b1', 'W2', 'b2')}
    del _L2_ffn_all

    def _L3_gnn_setup():
        import jax, jax.numpy as jnp
        import numpy as np
        N = 3125
        E = 25000
        IN = 256
        H = 8
        D = 32
        EF = 3
        key = jax.random.key(seed)
        ks = jax.random.split(key, 8)
        x = jax.random.normal(ks[0], (N, IN), dtype=jnp.float32)
        edge_index = jax.random.randint(ks[1], (2, E), 0, N, dtype=jnp.int64)
        edge_attr = jax.random.normal(ks[2], (E, EF), dtype=jnp.float32)
        W = jax.random.normal(ks[3], (H * D, IN), dtype=jnp.float32) * np.float32(np.sqrt(2.0 / (IN + H * D)))
        a_src = jax.random.normal(ks[4], (H, D), dtype=jnp.float32) * np.float32(np.sqrt(2.0 / (H + D)))
        a_dst = jax.random.normal(ks[5], (H, D), dtype=jnp.float32) * np.float32(np.sqrt(2.0 / (H + D)))
        edge_W = jax.random.normal(ks[6], (H * D, EF), dtype=jnp.float32) * np.float32(np.sqrt(2.0 / (EF + H * D)))
        edge_b = jnp.zeros((H * D,), dtype=jnp.float32)
        bias = jnp.zeros((H * D,), dtype=jnp.float32)
        return {'x': x, 'W': W, 'a_src': a_src, 'a_dst': a_dst, 'edge_W': edge_W, 'edge_b': edge_b, 'bias': bias, 'edge_attr': edge_attr, 'edge_index': edge_index}
    _L3_gnn_all = _L3_gnn_setup()
    _L3_gnn_in = {k: v for k, v in _L3_gnn_all.items() if k in ('W', 'a_src', 'a_dst', 'edge_W', 'edge_b', 'bias')}
    del _L3_gnn_all

    def _L3_ffn_setup():
        import jax, jax.numpy as jnp
        import numpy as np
        TOP_K = 2
        key = jax.random.key(seed)
        ks = jax.random.split(key, 4)
        B, L, D, H, E = (8, 256, 256, 1024, 8)
        s = 0.02
        return {'x': jax.random.normal(ks[0], (B, L, D), jnp.float32), 'Wg': jax.random.normal(ks[1], (D, E), jnp.float32) * s, 'bg': jnp.zeros((E,), jnp.float32), 'W1': jax.random.normal(ks[2], (E, D, H), jnp.float32) * s, 'b1': jnp.zeros((E, H), jnp.float32), 'W2': jax.random.normal(ks[3], (E, H, D), jnp.float32) * s, 'b2': jnp.zeros((E, D), jnp.float32)}
    _L3_ffn_all = _L3_ffn_setup()
    _L3_ffn_in = {k: v for k, v in _L3_ffn_all.items() if k in ('Wg', 'bg', 'W1', 'b1', 'W2', 'b2')}
    del _L3_ffn_all
    return {'x': x, 'src': src, 'dst': dst, 'edge_attr_3': edge_attr_3, 'edge_type_8': edge_type_8, 'L0_gnn_Wl1': _L0_gnn_in['Wl1'], 'L0_gnn_Wr1': _L0_gnn_in['Wr1'], 'L0_gnn_att1': _L0_gnn_in['att1'], 'L0_gnn_b1': _L0_gnn_in['b1'], 'L0_gnn_Wl2': _L0_gnn_in['Wl2'], 'L0_gnn_Wr2': _L0_gnn_in['Wr2'], 'L0_gnn_att2': _L0_gnn_in['att2'], 'L0_gnn_b2': _L0_gnn_in['b2'], 'L0_ffn_W_fx': _L0_ffn_in['W_fx'], 'L0_ffn_b_fx': _L0_ffn_in['b_fx'], 'L0_ffn_W_x': _L0_ffn_in['W_x'], 'L0_ffn_b_x': _L0_ffn_in['b_x'], 'L0_ffn_W_slice': _L0_ffn_in['W_slice'], 'L0_ffn_b_slice': _L0_ffn_in['b_slice'], 'L0_ffn_W_q': _L0_ffn_in['W_q'], 'L0_ffn_W_k': _L0_ffn_in['W_k'], 'L0_ffn_W_v': _L0_ffn_in['W_v'], 'L0_ffn_W_out': _L0_ffn_in['W_out'], 'L0_ffn_b_out': _L0_ffn_in['b_out'], 'L0_ffn_temperature': _L0_ffn_in['temperature'], 'L1_gnn_weight': _L1_gnn_in['weight'], 'L1_gnn_h_bias': _L1_gnn_in['h_bias'], 'L1_gnn_loop_weight': _L1_gnn_in['loop_weight'], 'L1_ffn_W_gat': _L1_ffn_in['W_gat'], 'L1_ffn_att_src': _L1_ffn_in['att_src'], 'L1_ffn_att_dst': _L1_ffn_in['att_dst'], 'L1_ffn_b_gat': _L1_ffn_in['b_gat'], 'L1_ffn_ln_gamma': _L1_ffn_in['ln_gamma'], 'L1_ffn_ln_beta': _L1_ffn_in['ln_beta'], 'L1_ffn_W1': _L1_ffn_in['W1'], 'L1_ffn_b1': _L1_ffn_in['b1'], 'L1_ffn_W2': _L1_ffn_in['W2'], 'L1_ffn_b2': _L1_ffn_in['b2'], 'L1_ffn_edge_index': _L1_ffn_in['edge_index'], 'L2_gnn_W1': _L2_gnn_in['W1'], 'L2_gnn_b1': _L2_gnn_in['b1'], 'L2_gnn_W2': _L2_gnn_in['W2'], 'L2_gnn_b2': _L2_gnn_in['b2'], 'L2_ffn_router_w': _L2_ffn_in['router_w'], 'L2_ffn_router_b': _L2_ffn_in['router_b'], 'L2_ffn_W1': _L2_ffn_in['W1'], 'L2_ffn_b1': _L2_ffn_in['b1'], 'L2_ffn_W2': _L2_ffn_in['W2'], 'L2_ffn_b2': _L2_ffn_in['b2'], 'L3_gnn_W': _L3_gnn_in['W'], 'L3_gnn_a_src': _L3_gnn_in['a_src'], 'L3_gnn_a_dst': _L3_gnn_in['a_dst'], 'L3_gnn_edge_W': _L3_gnn_in['edge_W'], 'L3_gnn_edge_b': _L3_gnn_in['edge_b'], 'L3_gnn_bias': _L3_gnn_in['bias'], 'L3_ffn_Wg': _L3_ffn_in['Wg'], 'L3_ffn_bg': _L3_ffn_in['bg'], 'L3_ffn_W1': _L3_ffn_in['W1'], 'L3_ffn_b1': _L3_ffn_in['b1'], 'L3_ffn_W2': _L3_ffn_in['W2'], 'L3_ffn_b2': _L3_ffn_in['b2']}

def reference(x, src, dst, edge_attr_3, edge_type_8, L0_gnn_Wl1, L0_gnn_Wr1, L0_gnn_att1, L0_gnn_b1, L0_gnn_Wl2, L0_gnn_Wr2, L0_gnn_att2, L0_gnn_b2, L0_ffn_W_fx, L0_ffn_b_fx, L0_ffn_W_x, L0_ffn_b_x, L0_ffn_W_slice, L0_ffn_b_slice, L0_ffn_W_q, L0_ffn_W_k, L0_ffn_W_v, L0_ffn_W_out, L0_ffn_b_out, L0_ffn_temperature, L1_gnn_weight, L1_gnn_h_bias, L1_gnn_loop_weight, L1_ffn_W_gat, L1_ffn_att_src, L1_ffn_att_dst, L1_ffn_b_gat, L1_ffn_ln_gamma, L1_ffn_ln_beta, L1_ffn_W1, L1_ffn_b1, L1_ffn_W2, L1_ffn_b2, L1_ffn_edge_index, L2_gnn_W1, L2_gnn_b1, L2_gnn_W2, L2_gnn_b2, L2_ffn_router_w, L2_ffn_router_b, L2_ffn_W1, L2_ffn_b1, L2_ffn_W2, L2_ffn_b2, L3_gnn_W, L3_gnn_a_src, L3_gnn_a_dst, L3_gnn_edge_W, L3_gnn_edge_b, L3_gnn_bias, L3_ffn_Wg, L3_ffn_bg, L3_ffn_W1, L3_ffn_b1, L3_ffn_W2, L3_ffn_b2):
    import jax
    import jax.numpy as jnp

    def _L0_gnn_ref(x, edge_index, Wl1, Wr1, att1, b1, Wl2, Wr2, att2, b2):
        import jax, jax.numpy as jnp
        import numpy as np
        NEG_SLOPE = 0.2

        def gatv2_layer(x, Wl, Wr, att, bias, src, dst, n_nodes, heads, ch, concat):
            xl = (x @ Wl).reshape(n_nodes, heads, ch)
            xr = (x @ Wr).reshape(n_nodes, heads, ch)
            m = xl[src] + xr[dst]
            e = jax.nn.leaky_relu(m, NEG_SLOPE)
            logits = jnp.einsum('ehc,hc->eh', e, att)
            mx = jax.ops.segment_max(logits, dst, num_segments=n_nodes)
            ex = jnp.exp(logits - mx[dst])
            denom = jax.ops.segment_sum(ex, dst, num_segments=n_nodes)
            alpha = ex / denom[dst]
            out = jax.ops.segment_sum(alpha[:, :, None] * xl[src], dst, num_segments=n_nodes)
            if concat:
                out = out.reshape(n_nodes, heads * ch)
            else:
                out = out.mean(axis=1)
            return out + bias
        N = x.shape[0]
        loops = jnp.arange(N, dtype=edge_index.dtype)
        src = jnp.concatenate([edge_index[0], loops])
        dst = jnp.concatenate([edge_index[1], loops])
        h = gatv2_layer(x, Wl1, Wr1, att1, b1, src, dst, N, 4, 64, concat=True)
        h = jax.nn.elu(h)
        out = gatv2_layer(h, Wl2, Wr2, att2, b2, src, dst, N, 1, 256, concat=False)
        return out

    def _L0_ffn_ref(x, W_fx, b_fx, W_x, b_x, W_slice, b_slice, W_q, W_k, W_v, W_out, b_out, temperature):
        import jax, jax.numpy as jnp
        import numpy as np
        DIM = 256
        H = 8
        D = 64
        G = 64
        INNER = H * D
        SCALE = D ** (-0.5)
        B, N, _ = x.shape
        fx_mid = (x @ W_fx + b_fx).reshape(B, N, H, D).transpose(0, 2, 1, 3)
        x_mid = (x @ W_x + b_x).reshape(B, N, H, D).transpose(0, 2, 1, 3)
        temp = jnp.clip(temperature, 0.1, 5.0)
        slice_weights = jax.nn.softmax((x_mid @ W_slice + b_slice) / temp, axis=-1)
        slice_norm = slice_weights.sum(axis=2)
        slice_token = jnp.einsum('bhnc,bhng->bhgc', fx_mid, slice_weights)
        slice_token = slice_token / (slice_norm[..., None] + 1e-05)
        q = slice_token @ W_q
        k = slice_token @ W_k
        v = slice_token @ W_v
        attn = jax.nn.softmax(jnp.einsum('bhgc,bhkc->bhgk', q, k) * SCALE, axis=-1)
        out_slice = jnp.einsum('bhgk,bhkc->bhgc', attn, v)
        out_x = jnp.einsum('bhgc,bhng->bhnc', out_slice, slice_weights)
        out_x = out_x.transpose(0, 2, 1, 3).reshape(B, N, INNER)
        return out_x @ W_out + b_out

    def _L1_gnn_ref(edge_index, x, edge_type, weight, h_bias, loop_weight):
        import jax, jax.numpy as jnp
        import numpy as np
        N_NODES = 3125
        N_EDGES = 50000
        IN_FEAT = 256
        OUT_FEAT = 256
        NUM_RELS = 8
        ALPHA = 0.5
        num_nodes = x.shape[0]
        src, dst = (edge_index[0], edge_index[1])
        hx = jnp.einsum('ni,rio->rno', x, weight)
        msg = hx[edge_type, src]
        agg = jax.ops.segment_sum(msg, dst, num_segments=num_nodes)
        node_repr = agg * jnp.asarray(ALPHA, x.dtype) ** 0.5
        node_repr = node_repr + h_bias
        loop_message = x @ loop_weight
        node_repr = node_repr + loop_message * jnp.asarray(1.0 - ALPHA, x.dtype) ** 0.5
        return node_repr

    def _L1_ffn_ref(x, W_gat, att_src, att_dst, b_gat, ln_gamma, ln_beta, W1, b1, W2, b2, edge_index):
        import jax, jax.numpy as jnp
        import numpy as np
        B, N, D = (16, 256, 256)
        NUM_EXPERTS, TOP_K, HEADS = (4, 2, 4)
        N_EDGES = 65536
        LN_EPS = 1e-05

        def _layernorm(x, g, b):
            mu = x.mean(-1, keepdims=True)
            var = ((x - mu) ** 2).mean(-1, keepdims=True)
            return (x - mu) * jax.lax.rsqrt(var + LN_EPS) * g + b

        def _forward(x, edge_index, W_gat, att_src, att_dst, b_gat, ln_gamma, ln_beta, W1, b1, W2, b2):
            Bc, Nc, Dc = x.shape
            M = Bc * Nc
            x_flat = x.reshape(M, Dc)
            h = (x_flat @ W_gat).reshape(M, HEADS, NUM_EXPERTS)
            loops = jnp.arange(M, dtype=edge_index.dtype)
            src = jnp.concatenate([edge_index[0], loops])
            dst = jnp.concatenate([edge_index[1], loops])
            a_src = (h * att_src).sum(-1)
            a_dst = (h * att_dst).sum(-1)
            e = jax.nn.leaky_relu(a_src[src] + a_dst[dst], negative_slope=0.2)
            e_max = jax.ops.segment_max(e, dst, num_segments=M)
            ee = jnp.exp(e - e_max[dst])
            denom = jax.ops.segment_sum(ee, dst, num_segments=M)
            alpha = ee / (denom[dst] + 1e-16)
            msg = h[src] * alpha[:, :, None]
            agg = jax.ops.segment_sum(msg, dst, num_segments=M).reshape(M, HEADS * NUM_EXPERTS) + b_gat
            scores = _layernorm(agg, ln_gamma, ln_beta).reshape(M, HEADS, NUM_EXPERTS).mean(1)
            scores = scores.reshape(Bc, Nc, NUM_EXPERTS)
            topk_s, topk_i = jax.lax.top_k(scores, TOP_K)
            w = jax.nn.softmax(topk_s, axis=-1)
            out = jnp.zeros_like(x)
            for ei in range(NUM_EXPERTS):
                g = jnp.where(topk_i == ei, w, 0.0).sum(-1)
                hh = jax.nn.gelu(x @ W1[ei] + b1[ei], approximate=False)
                out = out + g[..., None] * (hh @ W2[ei] + b2[ei])
            return out
        return _forward(x, edge_index, W_gat, att_src, att_dst, b_gat, ln_gamma, ln_beta, W1, b1, W2, b2)

    def _L2_gnn_ref(x, W1, b1, W2, b2, edge_index):
        import jax, jax.numpy as jnp
        import numpy as np
        N = 625
        E = 18750
        D = 256
        n = x.shape[0]
        loops = jnp.arange(n, dtype=edge_index.dtype)
        src = jnp.concatenate([edge_index[0], loops])
        dst = jnp.concatenate([edge_index[1], loops])
        deg = jax.ops.segment_sum(jnp.ones(src.shape[0], x.dtype), dst, num_segments=n)
        dinv = jnp.where(deg > 0, jax.lax.rsqrt(jnp.maximum(deg, 1e-12)), 0.0)
        norm = dinv[src] * dinv[dst]

        def gcn_conv(h, W, b):
            m = (h @ W)[src] * norm[:, None]
            return jax.ops.segment_sum(m, dst, num_segments=n) + b
        x1 = gcn_conv(x, W1, b1)
        x1 = x1 / jnp.maximum(jnp.linalg.norm(x1, axis=-1, keepdims=True), 1e-12)
        x2 = gcn_conv(x1, W2, b2)
        return x2 + x

    def _L2_ffn_ref(x, router_w, router_b, W1, b1, W2, b2):
        import jax, jax.numpy as jnp
        import numpy as np
        B, K, D = (512, 16, 256)
        E = 32
        H = int(D * 0.25)
        xf = x.reshape(-1, D)
        logits = xf @ router_w.T + router_b
        idx = jnp.argmax(logits, axis=-1)
        w1t = jnp.take(W1, idx, axis=0)
        h = jnp.einsum('nd,ndh->nh', xf, w1t) + jnp.take(b1, idx, axis=0)
        h = jax.nn.relu(h)
        w2t = jnp.take(W2, idx, axis=0)
        out = jnp.einsum('nh,nhd->nd', h, w2t) + jnp.take(b2, idx, axis=0)
        out = jax.nn.relu(out)
        return out.reshape(x.shape)

    def _L3_gnn_ref(x, W, a_src, a_dst, edge_W, edge_b, bias, edge_attr, edge_index):
        import jax, jax.numpy as jnp
        import numpy as np
        N = 3125
        E = 25000
        IN = 256
        H = 8
        D = 32
        EF = 3
        n = x.shape[0]
        h = (x @ W.T).reshape(n, H, D)
        src, dst = (edge_index[0], edge_index[1])
        h_src = h[src]
        h_dst = h[dst]
        alpha = jnp.einsum('ehd,hd->eh', h_src, a_src) + jnp.einsum('ehd,hd->eh', h_dst, a_dst)
        enc = jax.nn.relu(edge_attr @ edge_W.T + edge_b).reshape(-1, H, D)
        alpha = alpha + jnp.sum(enc * h_dst, axis=-1)
        alpha = jnp.where(alpha >= 0, alpha, 0.2 * alpha)
        amax = jax.ops.segment_max(alpha, dst, num_segments=n)
        ex = jnp.exp(alpha - amax[dst])
        denom = jax.ops.segment_sum(ex, dst, num_segments=n)
        attn = ex / jnp.maximum(denom[dst], 1e-10)
        out = jax.ops.segment_sum(h_src * attn[..., None], dst, num_segments=n)
        return out.reshape(n, H * D) + bias

    def _L3_ffn_ref(x, Wg, bg, W1, b1, W2, b2):
        import jax, jax.numpy as jnp
        import numpy as np
        TOP_K = 2
        B, L, D = x.shape
        E = W1.shape[0]
        xf = x.reshape(-1, D)
        gate_logits = xf @ Wg + bg
        top_w, top_i = jax.lax.top_k(gate_logits, TOP_K)
        top_w = jax.nn.softmax(top_w, axis=-1)
        w_dense = jnp.sum(jax.nn.one_hot(top_i, E, dtype=xf.dtype) * top_w[..., None], axis=1)
        out = jnp.zeros_like(xf)
        for e in range(E):
            h = jax.nn.gelu(xf @ W1[e] + b1[e], approximate=False)
            out = out + w_dense[:, e:e + 1] * (h @ W2[e] + b2[e])
        return out.reshape(B, L, D)
    edge_index = jnp.stack([src, dst])
    x = x + _L0_gnn_ref(_layernorm(x, axis=-1), edge_index, L0_gnn_Wl1, L0_gnn_Wr1, L0_gnn_att1, L0_gnn_b1, L0_gnn_Wl2, L0_gnn_Wr2, L0_gnn_att2, L0_gnn_b2)
    x = x + _L0_ffn_ref(_layernorm(x, axis=-1)[None], L0_ffn_W_fx, L0_ffn_b_fx, L0_ffn_W_x, L0_ffn_b_x, L0_ffn_W_slice, L0_ffn_b_slice, L0_ffn_W_q, L0_ffn_W_k, L0_ffn_W_v, L0_ffn_W_out, L0_ffn_b_out, L0_ffn_temperature)[0]
    x = x + _L1_gnn_ref(edge_index, _layernorm(x, axis=-1), edge_type_8, L1_gnn_weight, L1_gnn_h_bias, L1_gnn_loop_weight)
    x = x + _L1_ffn_ref(_layernorm(x, axis=-1)[None], L1_ffn_W_gat, L1_ffn_att_src, L1_ffn_att_dst, L1_ffn_b_gat, L1_ffn_ln_gamma, L1_ffn_ln_beta, L1_ffn_W1, L1_ffn_b1, L1_ffn_W2, L1_ffn_b2, L1_ffn_edge_index)[0]
    x = x + _L2_gnn_ref(_layernorm(x, axis=-1), L2_gnn_W1, L2_gnn_b1, L2_gnn_W2, L2_gnn_b2, edge_index)
    x = x + _L2_ffn_ref(_layernorm(x, axis=-1)[None], L2_ffn_router_w, L2_ffn_router_b, L2_ffn_W1, L2_ffn_b1, L2_ffn_W2, L2_ffn_b2)[0]
    x = x + _L3_gnn_ref(_layernorm(x, axis=-1), L3_gnn_W, L3_gnn_a_src, L3_gnn_a_dst, L3_gnn_edge_W, L3_gnn_edge_b, L3_gnn_bias, edge_attr_3, edge_index)
    x = x + _L3_ffn_ref(_layernorm(x, axis=-1)[None], L3_ffn_Wg, L3_ffn_bg, L3_ffn_W1, L3_ffn_b1, L3_ffn_W2, L3_ffn_b2)[0]
    return x

_drawn_inputs = setup_inputs


def setup_inputs(seed=0):
    import zlib

    import numpy as np

    out = dict(_drawn_inputs(seed))
    spreads = {'L0_gnn_b1': (0.0, 0.1),
     'L0_gnn_b2': (0.0, 0.1),
     'L0_ffn_b_fx': (0.0, 0.1),
     'L0_ffn_b_x': (0.0, 0.8),
     'L0_ffn_b_slice': (0.0, 0.8),
     'L0_ffn_b_out': (0.0, 0.1),
     'L0_ffn_temperature': (0.5, 0.6),
     'L1_gnn_h_bias': (0.0, 0.308),
     'L1_ffn_b_gat': (0.0, 0.1),
     'L1_ffn_ln_gamma': (1.0, 0.6),
     'L1_ffn_ln_beta': (0.0, 0.583),
     'L1_ffn_b1': (0.0, 0.55),
     'L1_ffn_b2': (0.0, 0.441),
     'L2_gnn_b1': (0.0, 0.8),
     'L2_gnn_b2': (0.0, 0.47),
     'L3_gnn_edge_b': (0.0, 0.679),
     'L3_gnn_bias': (0.0, 0.462),
     'L3_ffn_bg': (0.0, 0.696),
     'L3_ffn_b1': (0.0, 0.8),
     'L3_ffn_b2': (0.0, 0.646)}
    factors = {'L0_gnn_Wr1': 3.202,
     'L0_gnn_Wr2': 8.0,
     'L0_gnn_att2': 3.601,
     'L0_ffn_W_x': 5.052,
     'L0_ffn_W_slice': 7.461,
     'L0_ffn_W_q': 8.0,
     'L0_ffn_W_k': 8.0,
     'L1_ffn_att_src': 6.401,
     'L1_ffn_att_dst': 8.0,
     'L2_gnn_W1': 8.0,
     'L2_gnn_W2': 8.0,
     'L2_ffn_router_b': 6.584,
     'L2_ffn_W1': 2.676,
     'L2_ffn_b1': 8.0,
     'L2_ffn_b2': 8.0,
     'L3_gnn_a_dst': 3.136,
     'L3_ffn_Wg': 3.458,
     'L3_ffn_W1': 4.157,
     'L3_ffn_W2': 3.876}
    for name, (base, spread) in spreads.items():
        noise = np.random.default_rng([zlib.crc32(name.encode()), seed]).standard_normal(out[name].shape)
        drawn = base * np.exp(spread * noise) if base else spread * noise
        out[name] = jnp.asarray(drawn.astype(out[name].dtype))
    for name, factor in factors.items():
        out[name] = (out[name] * factor).astype(out[name].dtype)
    return out
```

```python
from contextlib import ExitStack

import numpy as np

import concourse.bass as bass
from concourse import mybir

F = mybir.dt.float32
BF = mybir.dt.bfloat16
I32 = mybir.dt.int32
U32 = mybir.dt.uint32
ALU = mybir.AluOpType
ACT = mybir.ActivationFunctionType
AX = mybir.AxisListType.X

N = 3125
NB = 25
D = 256
LASTP = N - 24 * 128
NEG = -1.0e30
FILL = -1000.0


class Queue:

    def __init__(self, nc, eng, name):
        self.nc, self.eng, self.sem, self.n = nc, eng, nc.alloc_semaphore(name), 0
        self.name = name
        self.seen = {}

    def wait(self, *tokens):
        for tok in tokens:
            if tok is None:
                continue
            if isinstance(tok, list):
                self.wait(*tok)
                continue
            name, sem, value = tok
            if self.seen.get(name, 0) < value:
                self.eng.wait_ge(sem, value)
                self.seen[name] = value

    def do(self, ins):
        ins.then_inc(self.sem, 1)
        self.n += 1
        return (self.name, self.sem, self.n)

    def now(self):
        return (self.name, self.sem, self.n) if self.n else None


class Dmas:

    def __init__(self, nc, queue, name, ring):
        self.q, self.name = queue, name
        self.sems = [nc.alloc_semaphore(f"{name}{i}") for i in range(ring)]
        self.count = [0] * ring
        self.k = 0

    def slot(self):
        i = self.k % len(self.sems)
        self.k += 1
        self.q.wait(self.token(i))
        return i

    def token(self, i):
        return (f"{self.name}{i}", self.sems[i], 16 * self.count[i]) if self.count[i] else None

    def start(self, out, in_, small=False):
        i = self.slot()
        self.q.eng.dma_start(out, in_, allow_slow_non_contiguous=small).then_inc(self.sems[i], 16)
        self.count[i] += 1
        return self.token(i)

    def gather(self, out, table, index, rows):
        i = self.slot()
        self.q.eng.indirect_dma_start(
            out=out, out_offset=None, in_=table,
            in_offset=bass.IndirectOffsetOnAxis(ap=index, axis=0),
            bounds_check=rows - 1, oob_is_err=False).then_inc(self.sems[i], 16)
        self.count[i] += 1
        return self.token(i)

    def scatter(self, table, index, in_, rows):
        i = self.slot()
        self.q.eng.indirect_dma_start(
            out=table, out_offset=bass.IndirectOffsetOnAxis(ap=index, axis=0),
            in_=in_, in_offset=None,
            bounds_check=rows - 1, oob_is_err=False).then_inc(self.sems[i], 16)
        self.count[i] += 1
        return self.token(i)

    def all(self):
        return [self.token(i) for i in range(len(self.sems))]


class Ctx:
    pass


def bc(ap, shape):
    return ap.to_broadcast(shape)


def make_ctx(nc):
    k = Ctx()
    k.nc = nc
    k.V = Queue(nc, nc.vector, "qv")
    k.A = Queue(nc, nc.scalar, "qa")
    k.P = Queue(nc, nc.tensor, "qp")
    k.G = Queue(nc, nc.gpsimd, "qg")
    k.S = Queue(nc, nc.sync, "qs")
    k.ld = Dmas(nc, k.S, "dl", 12)
    k.st = Dmas(nc, k.A, "da", 8)
    k.ind = Dmas(nc, k.G, "dg", 24)
    k.ps = [nc.alloc_psum_tensor(f"ps{i}", [128, 512], F) for i in range(8)]
    k.pst = [None] * 8
    return k


def fence(k):
    toks = [q.now() for q in (k.V, k.A, k.P, k.G)] + k.ld.all() + k.st.all() + k.ind.all()
    for q in (k.V, k.A, k.P, k.G, k.S):
        q.wait(toks)
    k.pst = [None] * 8


def mm(k, out, lhsT, rhs, start=True, stop=True):
    return k.P.do(k.nc.tensor.matmul(out, lhsT, rhs, start=start, stop=stop, skip_group_check=True))


def constants(k):
    nc, V, G = k.nc, k.V, k.G
    al = nc.alloc_sbuf_tensor
    k.ident = al("ident", [128, 128], F)
    k.identb = al("identb", [128, 128], BF)
    k.ltri = al("ltri", [128, 128], F)
    k.lmask = al("lmask", [128, 128], F)
    k.ones = al("ones", [128, 128], F)
    k.iof = al("iof", [128, 128], F)
    k.iob = al("iob", [128, 128], BF)
    a = V.do(nc.vector.memset(k.ones[:, :], 1.0))
    V.do(nc.vector.memset(k.ident[:, :], 0.0))
    b = V.do(nc.vector.memset(k.identb[:, :], 0.0))
    G.wait(a, b)
    t0 = G.do(nc.gpsimd.affine_select(out=k.ident[:, :], in_=k.ident[:, :], compare_op=ALU.not_equal, fill=1.0,
                                      base=0, pattern=[[-1, 128]], channel_multiplier=1))
    G.do(nc.gpsimd.affine_select(out=k.ltri[:, :], in_=k.ones[:, :], compare_op=ALU.is_gt, fill=0.0,
                                 base=0, pattern=[[1, 128]], channel_multiplier=-1))
    G.do(nc.gpsimd.affine_select(out=k.lmask[:, :], in_=k.ones[:, :], compare_op=ALU.is_gt, fill=0.0,
                                 base=0, pattern=[[-1, 128]], channel_multiplier=1))
    t1 = G.do(nc.gpsimd.iota(k.iof[:, :], pattern=[[1, 128]], base=0, channel_multiplier=0,
                             allow_small_or_imprecise_dtypes=True))
    V.wait(t0, t1)
    V.do(nc.vector.tensor_copy(k.identb[:, :], k.ident[:, :]))
    V.do(nc.vector.tensor_copy(k.iob[:, :], k.iof[:, :]))
    fence(k)


def sort_edges(k, name, J, load, T, Wd):
    nc, V, A, P, G = k.nc, k.V, k.A, k.P, k.G
    vec = nc.vector
    rows = 128 * T
    tab = nc.dram_tensor(f"tab_{name}", (rows, Wd), F).ap()
    st = nc.alloc_sbuf_tensor(f"st_{name}", [128, 26], F)
    cnt = nc.alloc_sbuf_tensor(f"cnt_{name}", [128, NB], F)
    with ExitStack() as es:
        def sb(n, shape, dt):
            return es.enter_context(nc.sbuf_tensor(f"{name}_{n}", shape, dt))
        pay = sb("pay", [128, J, Wd], F)
        filla = sb("fill", [128, T, Wd], F)
        V.do(vec.memset(filla[:, :, :], 0.0))
        V.wait(V.now())
        V.do(vec.memset(filla[:, :, 0], FILL))
        k.S.wait(V.now())
        tfill = k.ld.start(tab.rearrange("(p r) w -> p (r w)", p=128), filla[:, :, :].rearrange("p a b -> p (a b)"))
        dst = load(sb, pay)
        lo = sb("lo", [128, J], F)
        hi = sb("hi", [128, J], F)
        inv = sb("inv", [128, J], F)
        ti = sb("ti", [128, J], I32)
        V.wait(V.now())
        V.do(vec.tensor_scalar(ti[:, :], dst[:, :], 127, None, ALU.bitwise_and))
        V.wait(V.now())
        V.do(vec.tensor_copy(lo[:, :], ti[:, :]))
        V.wait(V.now())
        V.do(vec.tensor_scalar(ti[:, :], dst[:, :], 7, None, ALU.arith_shift_right))
        V.wait(V.now())
        V.do(vec.tensor_copy(hi[:, :], ti[:, :]))
        V.do(vec.tensor_scalar(inv[:, :], pay[:, :, 0], float(N) - 0.5, 1.0e6, ALU.is_gt, ALU.mult))
        V.wait(V.now())
        V.do(vec.tensor_tensor(hi[:, :], hi[:, :], inv[:, :], ALU.add))
        V.wait(V.now())
        NG = (J + 15) // 16
        ohi = sb("ohi", [128, NG, 16, NB], BF)
        hist = sb("hist", [128, J, NB], F)
        cum = sb("cum", [128, NB, J + 1], F)
        olo = sb("olo", [128, 8, 128], BF)
        use = [None] * 8
        tko = []
        for g in range(NG):
            w = min(16, J - 16 * g)
            h = ohi[:, g, 0:w, :]
            tko.append(V.do(vec.tensor_tensor(h, bc(k.iof[:, 0:NB].unsqueeze(1), [128, w, NB]),
                                              bc(hi[:, 16 * g:16 * g + w].unsqueeze(2), [128, w, NB]), ALU.is_equal)))
        for g in range(NG):
            w = min(16, J - 16 * g)
            bank = g % 2
            for c in range(w):
                t = 16 * g + c
                b = t % 8
                V.wait(use[b])
                tv = V.do(vec.tensor_scalar(olo[:, b, :], k.iob[:, :], lo[:, t:t + 1], None, ALU.is_equal))
                P.wait(tv, tko[g])
                if c == 0:
                    P.wait(k.pst[bank])
                use[b] = mm(k, k.ps[bank][:, c * NB:(c + 1) * NB], olo[:, b, :], ohi[:, g, c, :])
            A.wait(P.now())
            k.pst[bank] = A.do(nc.scalar.copy(hist[:, 16 * g:16 * g + w, :],
                                              k.ps[bank][:, 0:w * NB].rearrange("p (a b) -> p a b", b=NB)))
        V.wait(A.now())
        hv = hist[:, :, :].rearrange("p t b -> p b t")
        V.do(vec.tensor_reduce(cnt[:, :], hv, AX, ALU.add))
        P.wait(V.now(), k.pst[2])
        mm(k, k.ps[2][:, 0:NB], k.ltri[:, :], cnt[:, :])
        mm(k, k.ps[2][:, 32:32 + NB], k.ones[:, :], cnt[:, :])
        V.wait(P.now())
        tot = sb("tot", [128, NB], F)
        toti = sb("toti", [128, NB], I32)
        V.do(vec.tensor_scalar(tot[:, :], k.ps[2][:, 32:32 + NB], 1.0, 127.0, ALU.max, ALU.add))
        V.wait(V.now())
        V.do(vec.tensor_copy(toti[:, :], tot[:, :]))
        V.wait(V.now())
        V.do(vec.tensor_scalar(toti[:, :], toti[:, :], 7, None, ALU.arith_shift_right))
        V.wait(V.now())
        V.do(vec.tensor_copy(tot[:, :], toti[:, :]))
        V.do(vec.memset(st[:, 0:1], 0.0))
        V.wait(V.now())
        V.do(vec.tensor_tensor_scan(st[:, 1:26], k.ones[:, 0:25], tot[:, :], 0.0, ALU.mult, ALU.add))
        V.wait(V.now())
        V.do(vec.scalar_tensor_tensor(out=cum[:, :, 0], in0=st[:, 0:25], scalar=128.0, in1=k.ps[2][:, 0:NB],
                                      op0=ALU.mult, op1=ALU.add))
        V.wait(V.now())
        k.pst[2] = V.now()
        one = sb("one", [128, J], F)
        V.do(vec.memset(one[:, :], 1.0))
        V.wait(V.now())
        for b in range(NB):
            V.do(vec.tensor_tensor_scan(cum[:, b, 1:J + 1], one[:, :], hist[:, :, b], cum[:, b, 0:1],
                                        ALU.mult, ALU.add))
        tcum = V.now()
        NT = (J + 127) // 128
        dT = sb("dT", [128, NT, 128], F)
        P.wait(k.pst[2])
        P.wait(V.now())
        for a in range(NT):
            w = min(128, J - 128 * a)
            P.wait(k.pst[2 + a % 2])
            P.do(nc.tensor.transpose(k.ps[2 + a % 2][0:w, 0:128], pay[:, 128 * a:128 * a + w, 0], k.ident[:, :]))
            A.wait(P.now())
            k.pst[2 + a % 2] = A.do(nc.scalar.copy(dT[0:w, a, :], k.ps[2 + a % 2][0:w, 0:128]))
        tdT = A.now()
        olt = sb("olt", [128, 4, 128], F)
        rank = sb("rank", [128, J], F)
        junk = sb("junk", [128, 2, 128], F)
        prod = sb("prod", [128, 2, 16, NB], F)
        addr = sb("addr", [128, J], U32)
        fa = sb("fa", [128, J], F)
        fi = sb("fi", [128, J], I32)
        fj = sb("fj", [128, J], I32)
        fb = sb("fb", [128, J], F)
        use = [None] * 8
        uselt = [None] * 4
        junkt = [None] * 2
        toks = []
        for g in range(NG):
            w = min(16, J - 16 * g)
            lb = 4 + g % 2
            for c in range(w):
                t = 16 * g + c
                b = t % 8
                V.wait(use[b])
                tv = V.do(vec.tensor_scalar(olo[:, b, :], k.iob[:, :], lo[:, t:t + 1], None, ALU.is_equal))
                P.wait(tv)
                pb = t % 2
                P.wait(k.pst[pb])
                pt = k.ps[pb][:, 0:64].bitcast(BF)
                use[b] = P.do(nc.tensor.transpose(pt, olo[:, b, :], k.identb[:, :]))
                A.wait(use[b], uselt[t % 4])
                k.pst[pb] = A.do(nc.scalar.copy(olt[:, t % 4, :], pt))
                P.wait(tdT, k.pst[2 + pb])
                kk = min(128, J - 128 * (t // 128))
                mm(k, k.ps[2 + pb][:, 0:128], bc(k.ident[0:kk, t % 128:t % 128 + 1], [kk, 128]),
                   dT[0:kk, t // 128, :])
                V.wait(P.now(), junkt[pb])
                k.pst[2 + pb] = junkt[pb] = V.do(vec.scalar_tensor_tensor(
                    out=junk[:, pb, :], in0=k.ps[2 + pb][:, 0:128], scalar=pay[:, t, 0:1], in1=k.lmask[:, :],
                    op0=ALU.is_equal, op1=ALU.mult, accum_out=rank[:, t:t + 1]))
                P.wait(k.pst[pb], tcum)
                if c == 0:
                    P.wait(k.pst[lb])
                uselt[t % 4] = mm(k, k.ps[lb][:, c * NB:(c + 1) * NB], olt[:, t % 4, :], cum[:, :, t])
            V.wait(P.now(), V.now())
            s = slice(16 * g, 16 * g + w)
            k.pst[lb] = V.do(vec.tensor_tensor(prod[:, g % 2, 0:w, :],
                                               k.ps[lb][:, 0:w * NB].rearrange("p (a b) -> p a b", b=NB),
                                               ohi[:, g, 0:w, :], ALU.mult))
            V.wait(V.now())
            V.do(vec.tensor_reduce(fa[:, s], prod[:, g % 2, 0:w, :], AX, ALU.add))
            V.wait(V.now())
            V.do(vec.tensor_tensor(fa[:, s], fa[:, s], rank[:, s], ALU.add))
            V.wait(V.now())
            V.do(vec.tensor_copy(fi[:, s], fa[:, s]))
            V.wait(V.now())
            V.do(vec.tensor_scalar(fj[:, s], fi[:, s], 7, None, ALU.arith_shift_right))
            V.do(vec.tensor_scalar(fi[:, s], fi[:, s], 127, None, ALU.bitwise_and))
            V.wait(V.now())
            V.do(vec.tensor_copy(fa[:, s], fi[:, s]))
            V.do(vec.tensor_copy(fb[:, s], fj[:, s]))
            V.wait(V.now())
            V.do(vec.scalar_tensor_tensor(out=fb[:, s], in0=fa[:, s], scalar=float(T), in1=fb[:, s],
                                          op0=ALU.mult, op1=ALU.add))
            V.wait(V.now())
            V.do(vec.tensor_tensor(fb[:, s], fb[:, s], inv[:, s], ALU.add))
            V.wait(V.now())
            tad = V.do(vec.tensor_copy(addr[:, s], fb[:, s]))
            G.wait(tad, tfill)
            for t in range(16 * g, 16 * g + w):
                k.ind.scatter(tab, addr[:, t:t + 1], pay[:, t, :], rows)
        fence(k)
    return tab, st, cnt


def tile_blocks(k, name, T, st, widths):
    nc, V = k.nc, k.V
    vec = nc.vector
    blk = nc.alloc_sbuf_tensor(f"blk_{name}", [128, T], F)
    offs = [nc.alloc_sbuf_tensor(f"off_{name}{w}", [1, T], I32) for w in widths]
    with ExitStack() as es:
        io = es.enter_context(nc.sbuf_tensor(f"io_{name}", [128, T], F))
        tmp = es.enter_context(nc.sbuf_tensor(f"tmp_{name}", [128, T], F))
        k.V.wait(k.G.do(nc.gpsimd.iota(io[:, :], pattern=[[1, T]], base=0, channel_multiplier=0,
                                       allow_small_or_imprecise_dtypes=True)))
        V.do(vec.memset(blk[:, :], 0.0))
        for b in range(1, 25):
            V.wait(V.now())
            V.do(vec.scalar_tensor_tensor(out=blk[:, :], in0=io[:, :], scalar=st[:, b:b + 1], in1=blk[:, :],
                                          op0=ALU.is_ge, op1=ALU.add))
        for w, o in zip(widths, offs):
            V.wait(V.now())
            V.do(vec.tensor_scalar(tmp[:, :], blk[:, :], float(w), None, ALU.mult))
            V.wait(V.now())
            V.do(vec.tensor_copy(o[:, :], tmp[0:1, :]))
        fence(k)
    return blk, offs


def load_int(k, sb, name, J, src, fill):
    nc, V = k.nc, k.V
    t = sb(name, [128, J], I32)
    V.do(nc.vector.memset(t[:, :], fill))
    k.S.wait(V.now())
    E = src.shape[0]
    c = (E + 127) // 128
    full = E // c
    toks = [k.ld.start(t[0:full, 0:c], src[0:full * c].rearrange("(p c) -> p c", c=c))]
    if E > full * c:
        toks.append(k.ld.start(t[full:full + 1, 0:E - full * c],
                               src[full * c:E].rearrange("(a c) -> a c", a=1)))
    return t, toks


def main_edges(k, src, dst, attr, typ):
    nc, V, G = k.nc, k.V, k.G
    vec = nc.vector
    J = 441
    T = 464
    k.T = T

    def load(sb, pay):
        d, t1 = load_int(k, sb, "d", J, dst, 4095)
        s, t2 = load_int(k, sb, "s", J, src, 0)
        y, t3 = load_int(k, sb, "y", J, typ, 0)
        at = sb("at", [128, 416, 3], F)
        V.do(vec.memset(at[:, :, :], 0.0))
        k.S.wait(V.now())
        t4 = [k.ld.start(at[0:127, :, :].rearrange("p a b -> p (a b)"),
                         attr[0:127 * 416, :].rearrange("(p c) w -> p (c w)", c=416)),
              k.ld.start(at[127:128, 0:293, :].rearrange("p a b -> p (a b)"),
                         attr[127 * 416:53125, :].rearrange("(p c) w -> p (c w)", p=1))]
        G.wait(t1, t2, V.now())
        lp = [G.do(nc.gpsimd.iota(x[:, 416:441], pattern=[[1, 25]], base=0, channel_multiplier=25)) for x in (d, s)]
        V.wait(lp, t1, t2, t3, t4)
        V.do(vec.tensor_copy(pay[:, :, 0], d[:, :]))
        V.do(vec.tensor_scalar(pay[:, :, 1], s[:, :], float(N - 1), None, ALU.min))
        V.wait(V.now())
        V.do(vec.scalar_tensor_tensor(out=pay[:, :, 2], in0=y[:, :], scalar=3200.0, in1=pay[:, :, 1],
                                      op0=ALU.mult, op1=ALU.add))
        V.do(vec.memset(pay[:, 0:416, 3], 1.0))
        V.do(vec.memset(pay[:, 416:441, 3:8], 0.0))
        V.do(vec.memset(pay[:, 0:416, 7], 0.0))
        V.do(vec.tensor_copy(pay[:, 0:416, 4:7], at[:, :, :]))
        return d

    tab, st, k.deg = sort_edges(k, "m", J, load, T, 8)
    k.blk, (k.off256, k.off264) = tile_blocks(k, "m", T, st, (256, 264))
    al = nc.alloc_sbuf_tensor
    k.dlA = al("dlA", [128, T], F)
    k.dlR = al("dlR", [128, T], F)
    k.xsrc = al("xsrc", [128, T], U32)
    k.xtyp = al("xtyp", [128, T], U32)
    k.attr = al("attr", [128, T, 4], F)
    k.loopneg = al("loopneg", [128, T], F)
    k.m_flags = edge_flags_dram(k, "m", T)
    with ExitStack() as es:
        p = es.enter_context(nc.sbuf_tensor("sorted_m", [128, T, 8], F))
        V.wait(k.ld.start(p[:, :, :].rearrange("p a b -> p (a b)"), tab.rearrange("(p r) w -> p (r w)", p=128)))
        V.do(vec.tensor_copy(k.xsrc[:, :], p[:, :, 1]))
        V.do(vec.tensor_copy(k.xtyp[:, :], p[:, :, 2]))
        V.do(vec.tensor_copy(k.attr[:, :, 0:3], p[:, :, 4:7]))
        V.do(vec.memset(k.attr[:, :, 3:4], 1.0))
        V.do(vec.scalar_tensor_tensor(out=k.dlA[:, :], in0=k.blk[:, :], scalar=-128.0, in1=p[:, :, 0],
                                      op0=ALU.mult, op1=ALU.add))
        V.do(vec.tensor_scalar(k.loopneg[:, :], p[:, :, 3], 1.0, -NEG, ALU.subtract, ALU.mult))
        V.wait(V.now())
        V.do(vec.tensor_tensor(k.dlR[:, :], k.dlA[:, :], k.loopneg[:, :], ALU.add))
        V.wait(V.now())
        to_rows(k, "mf", p[:, :, 0], T, k.m_flags[128:128 + T * 128])
        fence(k)


def edge_flags_dram(k, name, T):
    nc, V = k.nc, k.V
    d = nc.dram_tensor(f"dsts_{name}", (128 * (T + 2),), F).ap()
    with ExitStack() as es:
        s = es.enter_context(nc.sbuf_tensor(f"sent_{name}", [2, 128], F))
        V.do(nc.vector.memset(s[:, :], -7.0))
        k.S.wait(V.now())
        k.ld.start(d[0:128].rearrange("(a b) -> a b", a=1), s[0:1, :])
        k.ld.start(d[128 * (T + 1):128 * (T + 2)].rearrange("(a b) -> a b", a=1), s[1:2, :])
        fence(k)
    return d


def to_rows(k, name, src, C, dram):
    nc, P, A = k.nc, k.P, k.A
    with ExitStack() as es:
        buf = es.enter_context(nc.sbuf_tensor(f"rows_{name}", [128, 4, 128], F))
        free = [None] * 4
        P.wait(k.V.now())
        for a in range((C + 127) // 128):
            w = min(128, C - 128 * a)
            b = a % 2
            P.wait(k.pst[b])
            P.do(nc.tensor.transpose(k.ps[b][0:w, 0:128], src[:, 128 * a:128 * a + w], k.ident[:, :]))
            A.wait(P.now(), free[a % 4])
            k.pst[b] = A.do(nc.scalar.copy(buf[0:w, a % 4, :], k.ps[b][0:w, 0:128]))
            k.S.wait(A.now())
            free[a % 4] = k.ld.start(dram[128 * 128 * a:128 * (128 * a + w)].rearrange("(q e) -> q e", e=128),
                                     buf[0:w, a % 4, :])
        fence(k)


def from_rows(k, name, dram, C, dst):
    nc, P, A = k.nc, k.P, k.A
    with ExitStack() as es:
        buf = es.enter_context(nc.sbuf_tensor(f"fr_{name}", [128, 4, 128], F))
        free = [None] * 4
        for a in range((C + 127) // 128):
            w = min(128, C - 128 * a)
            b = a % 2
            k.S.wait(free[a % 4])
            t = k.ld.start(buf[0:w, a % 4, :],
                           dram[128 * 128 * a:128 * (128 * a + w)].rearrange("(q e) -> q e", e=128))
            P.wait(t, k.pst[b])
            free[a % 4] = P.do(nc.tensor.transpose(k.ps[b][:, 0:w], buf[0:w, a % 4, :], k.ident[0:w, 0:w]))
            A.wait(P.now())
            k.pst[b] = A.do(nc.scalar.copy(dst[:, 128 * a:128 * a + w], k.ps[b][:, 0:w]))
        fence(k)


def rev(ap):
    return ap[:, ::-1]


def seg_softmax(k, name, L, H, C, T, flags, eps_op, eps):
    nc, V, P, A = k.nc, k.V, k.P, k.A
    vec = nc.vector
    Q = H * C
    r = T // C
    n = r * 128
    dram = nc.dram_tensor(f"soft_{name}", (H * T * 128,), F).ap()
    dram2 = nc.dram_tensor(f"softo_{name}", (H * T * 128,), F).ap()
    to_rows(k, name + "i", L, H * T, dram)
    with ExitStack() as es:
        def sb(nm, shape, dt=F):
            return es.enter_context(nc.sbuf_tensor(f"{name}_{nm}", shape, dt))
        x = sb("x", [128, n])
        d = sb("d", [128, n + 2])
        ks = sb("ks", [128, n])
        ke = sb("ke", [128, n])
        a = sb("a", [128, n])
        b = sb("b", [128, n])
        row = sb("row", [1, 4, 128])
        col = sb("col", [128, 2])
        toks = [k.ld.start(x[0:Q, :], dram.rearrange("(q e) -> q e", q=Q))]
        for h in range(H):
            win = flags[127:127 + C * n].rearrange("(c e) -> c e", c=C)
            toks.append(k.ld.start(d[h * C:(h + 1) * C, 0:n], win))
            win = flags[129:129 + C * n].rearrange("(c e) -> c e", c=C)
            toks.append(k.ld.start(d[h * C:(h + 1) * C, n:n + 2], win[:, n - 2:n]))
        V.wait(toks)
        V.do(vec.tensor_tensor(ks[0:Q, :], d[0:Q, 1:n + 1], d[0:Q, 0:n], ALU.not_equal))
        V.do(vec.tensor_tensor(ke[0:Q, :], d[0:Q, 1:n + 1], d[0:Q, 2:n + 2], ALU.not_equal))
        V.wait(V.now())
        V.do(vec.tensor_reduce(col[0:Q, 0:1], ks[0:Q, :], AX, ALU.max))
        V.do(vec.tensor_reduce(col[0:Q, 1:2], ke[0:Q, :], AX, ALU.max))
        V.wait(V.now())
        anys = sb("anys", [1, 2, 128])
        cc = sb("cc", [128, 4])
        for i in range(2):
            P.wait(V.now(), k.pst[0])
            P.do(nc.tensor.transpose(k.ps[0][0:1, 128 * i:128 * i + Q], col[0:Q, i:i + 1], k.ident[0:Q, 0:Q]))
        V.wait(P.now())
        V.do(vec.tensor_copy(anys[0:1, :, 0:Q], k.ps[0][0:1, 0:256].rearrange("p (a b) -> p a b", a=2)[:, :, 0:Q]))
        V.wait(V.now())
        k.pst[0] = V.now()

        def scans(out, gate, inp, back, op_gate, op_in, init, any_row):
            o, g, i_ = out[0:Q, 0:n], gate[0:Q, 0:n], inp[0:Q, 0:n]
            if back:
                o, g, i_ = rev(o), rev(g), rev(i_)
            V.wait(V.now())
            V.do(vec.tensor_tensor_scan(o, g, i_, init, op_gate, op_in))
            V.wait(V.now())
            last = out[0:Q, 0:1] if back else out[0:Q, n - 1:n]
            P.wait(V.now(), k.pst[0])
            P.do(nc.tensor.transpose(k.ps[0][0:1, 0:Q], last, k.ident[0:Q, 0:Q]))
            V.wait(P.now())
            v = row[0:1, 0, 0:Q]
            V.do(vec.tensor_copy(v, k.ps[0][0:1, 0:Q]))
            gt = row[0:1, 1, 0:Q]
            if op_gate == ALU.add:
                V.do(vec.tensor_scalar(gt, any_row, NEG, None, ALU.mult))
            else:
                V.do(vec.tensor_scalar(gt, any_row, -1.0, 1.0, ALU.mult, ALU.add))
            V.wait(V.now())
            res = row[0:1, 2, 0:Q]
            V.do(vec.memset(res, init))
            V.wait(V.now())
            for h in range(H):
                s = slice(h * C, (h + 1) * C)
                vo, vg, vi = row[0:1, 3, s], row[0:1, 1, s], row[0:1, 0, s]
                if back:
                    vo, vg, vi = rev(vo), rev(vg), rev(vi)
                V.do(vec.tensor_tensor_scan(vo, vg, vi, init, op_gate, op_in))
            V.wait(V.now())
            for h in range(H):
                if back:
                    V.do(vec.tensor_copy(row[0:1, 2, h * C:(h + 1) * C - 1], row[0:1, 3, h * C + 1:(h + 1) * C]))
                else:
                    V.do(vec.tensor_copy(row[0:1, 2, h * C + 1:(h + 1) * C], row[0:1, 3, h * C:(h + 1) * C - 1]))
            P.wait(V.now())
            P.do(nc.tensor.transpose(k.ps[0][0:Q, 0:1], res, k.ident[0:1, 0:1]))
            V.wait(P.now(), V.now())
            V.do(vec.tensor_copy(cc[0:Q, 0:1], k.ps[0][0:Q, 0:1]))
            k.pst[0] = V.now()
            V.wait(V.now())
            V.do(vec.tensor_tensor_scan(o, g, i_, cc[0:Q, 0:1], op_gate, op_in))
            V.wait(V.now())

        aS, aE = anys[0:1, 0, 0:Q], anys[0:1, 1, 0:Q]
        V.do(vec.tensor_scalar(b[0:Q, :], ks[0:Q, :], NEG, None, ALU.mult))
        scans(a, b, x, False, ALU.add, ALU.max, NEG, aS)
        V.do(vec.tensor_scalar(b[0:Q, :], ke[0:Q, :], NEG, None, ALU.mult))
        V.wait(V.now())
        g2 = d
        scans(g2, b, a, True, ALU.add, ALU.max, NEG, aE)
        V.do(vec.tensor_tensor(x[0:Q, :], x[0:Q, :], g2[0:Q, 0:n], ALU.subtract))
        A.wait(V.now())
        V.wait(A.do(nc.scalar.activation(x[0:Q, :], x[0:Q, :], ACT.Exp)))
        V.do(vec.tensor_scalar(b[0:Q, :], ks[0:Q, :], -1.0, 1.0, ALU.mult, ALU.add))
        scans(a, b, x, False, ALU.mult, ALU.add, 0.0, aS)
        V.do(vec.tensor_tensor(a[0:Q, :], a[0:Q, :], ke[0:Q, :], ALU.mult))
        V.do(vec.tensor_scalar(b[0:Q, :], ke[0:Q, :], -1.0, 1.0, ALU.mult, ALU.add))
        scans(g2, b, a, True, ALU.mult, ALU.add, 0.0, aE)
        if eps_op is not None:
            V.do(vec.tensor_scalar(g2[0:Q, 0:n], g2[0:Q, 0:n], eps, None, eps_op))
            V.wait(V.now())
        V.do(vec.reciprocal(g2[0:Q, 0:n], g2[0:Q, 0:n]))
        V.wait(V.now())
        V.do(vec.tensor_tensor(x[0:Q, :], x[0:Q, :], g2[0:Q, 0:n], ALU.mult))
        k.S.wait(V.now())
        k.ld.start(dram2.rearrange("(q e) -> q e", q=Q), x[0:Q, :])
        fence(k)
    from_rows(k, name + "o", dram2, H * T, L)


def rows_of(ap):
    return ap[:].rearrange("(a c) -> a c", a=1)


def layernorm(k, x, out):
    nc, V, A = k.nc, k.V, k.A
    vec = nc.vector
    x3 = x.rearrange("p (b c) -> p b c", b=NB)
    o3 = out.rearrange("p (b c) -> p b c", b=NB)
    with ExitStack() as es:
        mu = es.enter_context(nc.sbuf_tensor(k.nm("mu"), [128, NB], F))
        va = es.enter_context(nc.sbuf_tensor(k.nm("va"), [128, NB], F))
        junk = es.enter_context(nc.sbuf_tensor(k.nm("junk"), [128, 2, D], F))
        V.do(vec.tensor_reduce(mu[:, :], x3, AX, ALU.add))
        V.wait(V.now())
        V.do(vec.tensor_scalar(mu[:, :], mu[:, :], 1.0 / D, None, ALU.mult))
        V.wait(V.now())
        for b in range(NB):
            t = V.do(vec.tensor_scalar(o3[:, b, :], x3[:, b, :], mu[:, b:b + 1], None, ALU.subtract))
            A.wait(t)
            A.wait(A.now())
            A.do(nc.scalar.activation(junk[:, b % 2, :], o3[:, b, :], ACT.Square, accum_out=va[:, b:b + 1]))
        V.wait(A.now())
        V.do(vec.tensor_scalar(va[:, :], va[:, :], 1.0 / D, 1e-5, ALU.mult, ALU.add))
        A.wait(V.now())
        A.do(nc.scalar.activation(va[:, :], va[:, :], ACT.Sqrt))
        V.wait(A.now())
        V.do(vec.reciprocal(va[:, :], va[:, :]))
        V.wait(V.now())
        for b in range(NB):
            V.do(vec.tensor_scalar(o3[:, b, :], o3[:, b, :], va[:, b:b + 1], None, ALU.mult))
        fence(k)


def transpose_rows(k, x, xT, banks=(0, 1)):
    nc, P, A, V = k.nc, k.P, k.A, k.V
    P.wait(V.now(), A.now())
    i = 0
    for c in range(2):
        for b0 in range(0, NB, 4):
            w = min(4, NB - b0)
            bk = banks[i % len(banks)]
            P.wait(k.pst[bk])
            for j in range(w):
                b = b0 + j
                P.do(nc.tensor.transpose(k.ps[bk][:, 128 * j:128 * (j + 1)],
                                         x[:, b * D + c * 128:b * D + c * 128 + 128], k.ident[:, :]))
            E, f = (A, nc.scalar.copy) if i % 2 else (V, nc.vector.tensor_copy)
            E.wait(P.now())
            k.pst[bk] = E.do(f(xT[:, c, 128 * b0:128 * (b0 + w)], k.ps[bk][:, 0:128 * w]))
            i += 1
    P.wait(A.now(), V.now())


def load_w(k, dst, src):
    for c in range(2):
        k.ld.start(dst[:, c, :], src[128 * c:128 * (c + 1), :])
    return k.ld.all()


def project(k, xT, w, M, sink, banks=(2, 3, 4, 5)):
    i = 0
    for b in range(NB):
        for m0 in range(0, M, 512):
            mw = min(512, M - m0)
            bk = banks[i % len(banks)]
            i += 1
            k.P.wait(k.pst[bk])
            for c in range(2):
                mm(k, k.ps[bk][:, 0:mw], xT[:, c, 128 * b:128 * (b + 1)], w[:, c, m0:m0 + mw],
                   start=(c == 0), stop=(c == 1))
            k.pst[bk] = sink(b, m0, mw, k.ps[bk][:, 0:mw])


def copy_sink(k, dst, M):
    n = [0]

    def sink(b, m0, mw, ps):
        E, f = (k.A, k.nc.scalar.copy) if n[0] % 2 else (k.V, k.nc.vector.tensor_copy)
        n[0] += 1
        E.wait(k.P.now())
        return E.do(f(dst[:, b * M + m0:b * M + m0 + mw], ps))
    return sink


def dram_sink(k, es, dram, M):
    buf = es.enter_context(k.nc.sbuf_tensor(k.nm("tb"), [128, 6, 512], F))
    free = [None] * 6
    n = [0]

    def sink(b, m0, mw, ps):
        i = n[0] % 6
        E, f = (k.A, k.nc.scalar.copy) if n[0] % 2 else (k.V, k.nc.vector.tensor_copy)
        n[0] += 1
        E.wait(k.P.now(), free[i])
        t = E.do(f(buf[:, i, 0:mw], ps))
        k.S.wait(t)
        free[i] = []
        for j in range(0, mw, D):
            r = 3200 * ((m0 + j) // D) + 128 * b
            free[i].append(k.ld.start(dram[r:r + 128, :], buf[:, i, j:j + min(D, mw)]))
        return t
    return sink


def bcast_row(k, es, vecap, M):
    t = es.enter_context(k.nc.sbuf_tensor(k.nm("bc"), [128, M], F))
    k.ld.start(t[:, :], vecap.partition_broadcast(128))
    return t


def onehot(k, buf, dl, t, weight=None):
    if weight is None:
        return k.V.do(k.nc.vector.tensor_scalar(buf, k.iof[:, :], dl[:, t:t + 1], None, ALU.is_equal))
    return k.V.do(k.nc.vector.tensor_scalar(buf, k.iof[:, :], dl[:, t:t + 1], weight, ALU.is_equal, ALU.mult))


def seg_sum(k, T, table, rows, idx, dl, offs, acc, Wd=D, alpha=None, H=1):
    nc, V, P, G = k.nc, k.V, k.P, k.G
    vec = nc.vector
    R = 12
    with ExitStack() as es:
        g = es.enter_context(nc.sbuf_tensor(k.nm("g"), [128, R, Wd], F))
        oh = es.enter_context(nc.sbuf_tensor(k.nm("oh"), [128, 6, 128], F))
        V.do(vec.memset(acc[:, :], 0.0))
        freeg = [None] * R
        freeo = [None] * 6
        last = V.now()
        pend = []

        def add(t, tp):
            V.wait(tp, V.now())
            off = vec.value_load(offs[0:1, t:t + 1], min_val=0, max_val=24 * Wd)
            d = acc[:, bass.ds(off, Wd)]
            k.pst[t % 4] = V.do(vec.tensor_tensor(d, d, k.ps[t % 4][:, 0:Wd], ALU.add))

        for t in range(T):
            G.wait(freeg[t % R])
            tg = k.ind.gather(g[:, t % R, :], table, idx[:, t:t + 1], rows)
            V.wait(freeo[t % 6])
            if H == 1:
                to = onehot(k, oh[:, t % 6, :], dl, t, None if alpha is None else alpha[:, t:t + 1])
                tw = tg
            else:
                to = onehot(k, oh[:, t % 6, :], dl, t)
                V.wait(tg)
                gv = g[:, t % R, :].rearrange("p (h c) -> p h c", h=H)
                av = alpha.rearrange("p (h t) -> p h t", h=H)[:, :, t:t + 1]
                tw = V.do(vec.tensor_tensor(gv, gv, bc(av, [128, H, Wd // H]), ALU.mult))
            P.wait(to, tw, k.pst[t % 4])
            tp = mm(k, k.ps[t % 4][:, 0:Wd], oh[:, t % 6, :], g[:, t % R, :])
            freeg[t % R] = freeo[t % 6] = tp
            pend.append((t, tp))
            if len(pend) > 2:
                add(*pend.pop(0))
        for x in pend:
            add(*x)
        fence(k)


class DstRows:

    def __init__(self, k, es, dl, offs, src, width, ohbank=0, banks=(2, 3, 4)):
        nc = k.nc
        self.k, self.dl, self.offs, self.src, self.width, self.banks, self.ob = k, dl, offs, src, width, banks, ohbank
        self.oh = es.enter_context(nc.sbuf_tensor(k.nm("oh"), [128, 4, 128], F))
        self.ot = es.enter_context(nc.sbuf_tensor(k.nm("ot"), [128, 4, 128], F))
        self.fo = [None] * 4
        self.ft = [None] * 4

    def __call__(self, t):
        k, nc = self.k, self.k.nc
        i = t % 4
        k.V.wait(self.fo[i])
        to = onehot(k, self.oh[:, i, :], self.dl, t)
        b0 = self.ob + t % 2
        k.P.wait(to, k.pst[b0])
        self.fo[i] = k.P.do(nc.tensor.transpose(k.ps[b0][:, 0:128], self.oh[:, i, :], k.ident[:, :]))
        k.A.wait(self.fo[i], self.ft[i])
        k.pst[b0] = tc = k.A.do(nc.scalar.copy(self.ot[:, i, :], k.ps[b0][:, 0:128]))
        bk = self.banks[t % len(self.banks)]
        k.P.wait(tc, k.pst[bk])
        off = nc.tensor.value_load(self.offs[0:1, t:t + 1], min_val=0, max_val=24 * self.width)
        self.ft[i] = mm(k, k.ps[bk][:, 0:self.width], self.ot[:, i, :], self.src[:, bass.ds(off, self.width)])
        return bk, self.ft[i]


def gatv2_logits(k, T, table, xr, att, H, L):
    nc, V, P, G, A = k.nc, k.V, k.P, k.G, k.A
    vec = nc.vector
    R = 12
    with ExitStack() as es:
        g = es.enter_context(nc.sbuf_tensor(k.nm("g"), [128, R, D], F))
        attb = bcast_row(k, es, att, D)
        rows = DstRows(k, es, k.dlA, k.off256, xr, D)
        V.wait(k.ld.all())
        free = [None] * R
        Lv = L.rearrange("p (h t) -> p h t", h=H)
        pend = []

        def finish(t, ta):
            gt = g[:, t % R, :]
            V.wait(ta)
            if H == 1:
                free[t % R] = V.do(vec.tensor_tensor_reduce(gt, gt, attb[:, :], 1.0, 0.0, ALU.mult, ALU.add,
                                                            L[:, t:t + 1]))
            else:
                V.do(vec.tensor_tensor(gt, gt, attb[:, :], ALU.mult))
                V.wait(V.now())
                free[t % R] = V.do(vec.tensor_reduce(Lv[:, :, t], gt.rearrange("p (h c) -> p h c", h=H), AX, ALU.add))

        for t in range(T):
            G.wait(free[t % R])
            tg = k.ind.gather(g[:, t % R, :], table, k.xsrc[:, t:t + 1], 3200)
            bk, tp = rows(t)
            V.wait(tg, tp)
            gt = g[:, t % R, :]
            k.pst[bk] = V.do(vec.tensor_tensor(gt, gt, k.ps[bk][:, 0:D], ALU.add))
            V.wait(V.now())
            ta = V.do(vec.scalar_tensor_tensor(out=gt, in0=gt, scalar=0.2, in1=gt, op0=ALU.mult, op1=ALU.max))
            pend.append((t, ta))
            if len(pend) > 2:
                finish(*pend.pop(0))
        for x in pend:
            finish(*x)
        fence(k)


def gat_layer(k, name, xT, Wl, Wr, att, H, acc):
    nc = k.nc
    T = k.T
    table = nc.dram_tensor("xl_" + name, (3200, D), F).ap()
    with ExitStack() as es:
        def sb(n, shape, dt=F):
            return es.enter_context(nc.sbuf_tensor(k.nm(n), shape, dt))
        L = sb("L", [128, H * T])
        with ExitStack() as e2:
            xr = e2.enter_context(nc.sbuf_tensor(k.nm("xr"), [128, NB * D], F))
            wl = e2.enter_context(nc.sbuf_tensor(k.nm("wl"), [128, 2, D], F))
            wr = e2.enter_context(nc.sbuf_tensor(k.nm("wr"), [128, 2, D], F))
            load_w(k, wl, Wl)
            k.P.wait(load_w(k, wr, Wr))
            project(k, xT, wl, D, dram_sink(k, e2, table, D))
            project(k, xT, wr, D, copy_sink(k, xr, D))
            fence(k)
            gatv2_logits(k, T, table, xr, att, H, L[:, :])
        seg_softmax(k, name, L[:, :], H, 29 if H == 4 else 116, T, k.m_flags, None, 0)
        seg_sum(k, T, table, 3200, k.xsrc, k.dlA, k.off256, acc, alpha=L[:, :], H=H)


def add_bias(k, acc, bias_ap):
    with ExitStack() as es:
        b = bcast_row(k, es, bias_ap, D)
        k.V.wait(k.ld.all(), k.V.now())
        a3 = acc.rearrange("p (b c) -> p b c", b=NB)
        k.V.do(k.nc.vector.tensor_tensor(a3, a3, bc(b[:, :].unsqueeze(1), [128, NB, D]), ALU.add))
        fence(k)


def stage_l0_gnn(k, x, a):
    nc, V, A = k.nc, k.V, k.A
    vec = nc.vector
    with ExitStack() as es:
        def sb(n, shape, dt=F):
            return es.enter_context(nc.sbuf_tensor(k.nm(n), shape, dt))
        h = sb("h", [128, NB * D])
        xT = sb("xT", [128, 2, 3200])
        layernorm(k, x, h[:, :])
        transpose_rows(k, h, xT)
        fence(k)
        gat_layer(k, "g1", xT, a['L0_gnn_Wl1'], a['L0_gnn_Wr1'],
                  a['L0_gnn_att1'].rearrange("h c -> (h c)"), 4, h)
        add_bias(k, h[:, :], a['L0_gnn_b1'])
        with ExitStack() as e2:
            t = e2.enter_context(nc.sbuf_tensor(k.nm("t"), [128, NB * D], F))
            V.do(vec.tensor_scalar(t[:, :], h[:, :], 0.0, None, ALU.min))
            A.wait(V.now())
            A.do(nc.scalar.activation(t[:, :], t[:, :], ACT.Exp))
            V.wait(A.now())
            V.do(vec.tensor_scalar(t[:, :], t[:, :], -1.0, None, ALU.add))
            V.wait(V.now())
            V.do(vec.scalar_tensor_tensor(out=h[:, :], in0=h[:, :], scalar=0.0, in1=t[:, :],
                                          op0=ALU.max, op1=ALU.add))
            fence(k)
        transpose_rows(k, h, xT)
        fence(k)
        gat_layer(k, "g2", xT, a['L0_gnn_Wl2'], a['L0_gnn_Wr2'],
                  a['L0_gnn_att2'].rearrange("h c -> (h c)"), 1, h)
        add_bias(k, h[:, :], a['L0_gnn_b2'])
        V.do(vec.tensor_tensor(x, x, h[:, :], ALU.add))
        fence(k)


def stage_l0_ffn(k, x, a):
    nc, V, A, P = k.nc, k.V, k.A, k.P
    vec = nc.vector
    with ExitStack() as es:
        def sb(n, shape, dt=F):
            return es.enter_context(nc.sbuf_tensor(k.nm(n), shape, dt))
        sw = sb("sw", [128, NB, 512])
        Pm = sb("Pm", [128, 4, D])
        with ExitStack() as e2:
            def s2(n, shape, dt=F):
                return e2.enter_context(nc.sbuf_tensor(k.nm(n), shape, dt))
            xT = s2("xT", [128, 2, 3200])
            with ExitStack() as e3:
                xn = e3.enter_context(nc.sbuf_tensor(k.nm("xn"), [128, NB * D], F))
                layernorm(k, x, xn[:, :])
                transpose_rows(k, xn, xT)
                fence(k)
            wfx = s2("wfx", [128, 2, 512])
            wx = s2("wx", [128, 2, 512])
            load_w(k, wfx, a['L0_ffn_W_fx'])
            load_w(k, wx, a['L0_ffn_W_x'])
            bfx = bcast_row(k, e2, a['L0_ffn_b_fx'], 512)
            bxc = s2("bxc", [128, 4])
            k.ld.start(bxc[:, :], a['L0_ffn_b_x'].rearrange("(c p) -> p c", p=128), small=True)
            ws = s2("ws", [128, 128])
            V.do(vec.memset(ws[:, :], 0.0))
            k.S.wait(V.now())
            k.ld.start(ws[0:64, 0:64], a['L0_ffn_W_slice'])
            k.ld.start(ws[64:128, 64:128], a['L0_ffn_W_slice'])
            bs = bcast_row(k, e2, a['L0_ffn_b_slice'], 64)
            tp = bcast_row(k, e2, a['L0_ffn_temperature'].rearrange("a h b c -> (a h b c)"), 8)
            V.wait(k.ld.all())
            P.wait(k.ld.all())
            A.wait(k.ld.all())
            V.do(vec.tensor_scalar(tp[:, :], tp[:, :], 0.1, 5.0, ALU.max, ALU.min))
            V.wait(V.now())
            V.do(vec.reciprocal(tp[:, :], tp[:, :]))
            xm = s2("xm", [128, 2, 4, 512])
            fx = s2("fx", [128, 2, 8, 65])
            V.do(vec.memset(fx[:, :, :, :], 1.0))
            mx = s2("mx", [128, 2, 8])
            V.wait(V.now())
            pst = k.pst
            tok8 = [k.ps[6][0:64, :], k.ps[7][0:64, :]]
            fxfree = [None, None]
            for ch in range(7):
                t0, tw = 512 * ch, min(512, 3200 - 512 * ch)
                xb = ch % 2
                for i in range(4):
                    bk = i % 2
                    P.wait(pst[bk])
                    for c in range(2):
                        mm(k, k.ps[bk][:, 0:tw], wx[:, c, 128 * i:128 * (i + 1)], xT[:, c, t0:t0 + tw],
                           start=(c == 0), stop=(c == 1))
                    A.wait(P.now())
                    pst[bk] = A.do(nc.scalar.activation(xm[:, xb, i, 0:tw], k.ps[bk][:, 0:tw], ACT.Identity,
                                                        bias=bxc[:, i:i + 1]))
                txm = A.now()
                for j in range(tw // 128):
                    b = 4 * ch + j
                    bk = 2 + b % 2
                    P.wait(txm, pst[bk])
                    for i in range(4):
                        mm(k, k.ps[bk][:, 128 * i:128 * (i + 1)], xm[:, xb, i, 128 * j:128 * (j + 1)], ws[:, :])
                    w3 = sw[:, b, :].rearrange("p (h g) -> p h g", h=8)
                    V.wait(P.now())
                    pst[bk] = V.do(vec.tensor_tensor(w3, k.ps[bk][:, :].rearrange("p (h g) -> p h g", h=8),
                                                     bc(bs[:, :].unsqueeze(1), [128, 8, 64]), ALU.add))
                    m = mx[:, b % 2, :]

                    def step(ins):
                        V.do(ins)
                        V.wait(V.now())
                    V.wait(V.now())
                    step(vec.tensor_tensor(w3, w3, bc(tp[:, :].unsqueeze(2), [128, 8, 64]), ALU.mult))
                    step(vec.tensor_reduce(m, w3, AX, ALU.max))
                    step(vec.tensor_tensor(w3, w3, bc(m.unsqueeze(2), [128, 8, 64]), ALU.subtract))
                    A.wait(V.now())
                    A.do(nc.scalar.activation(sw[:, b, :], sw[:, b, :], ACT.Exp))
                    fk = 4 + b % 2
                    P.wait(pst[fk])
                    for c in range(2):
                        mm(k, k.ps[fk][:, :], xT[:, c, 128 * b:128 * (b + 1)], wfx[:, c, :],
                           start=(c == 0), stop=(c == 1))
                    V.wait(P.now(), fxfree[b % 2])
                    pst[fk] = V.do(vec.tensor_tensor(fx[:, b % 2, :, 0:64],
                                                     k.ps[fk][:, :].rearrange("p (h g) -> p h g", h=8),
                                                     bfx[:, :].rearrange("p (h g) -> p h g", h=8), ALU.add))
                    V.wait(A.now())
                    step(vec.tensor_reduce(m, w3, AX, ALU.add))
                    step(vec.reciprocal(m, m))
                    step(vec.tensor_tensor(w3, w3, bc(m.unsqueeze(2), [128, 8, 64]), ALU.mult))
                    P.wait(V.now())
                    kp = 128 if b < 24 else LASTP
                    for h in range(8):
                        fxfree[b % 2] = mm(k, tok8[h // 4][:, 65 * (h % 4):65 * (h % 4) + 65],
                                           sw[0:kp, b, 64 * h:64 * h + 64], fx[0:kp, b % 2, h, :],
                                           start=(b == 0 and h % 4 == 0), stop=(b == 24))
            fence(k)
            wq = s2("wq", [64, 64])
            wk = s2("wk", [64, 64])
            wv = s2("wv", [64, 64])
            wo = s2("wo", [64, 8, D])
            for t, n in ((wq, 'q'), (wk, 'k'), (wv, 'v')):
                k.ld.start(t[:, :], a['L0_ffn_W_' + n])
            k.ld.start(wo[:, :, :], a['L0_ffn_W_out'].rearrange("(h c) n -> c h n", c=64))
            P.wait(k.ld.all())
            st = s2("st", [64, 8, 65])
            nr = s2("nr", [64, 8])
            stT = s2("stT", [64, 8, 64])
            qT = s2("qT", [64, 8, 64])
            kT = s2("kT", [64, 8, 64])
            vv = s2("vv", [64, 8, 64])
            at = s2("at", [64, 8, 64])
            atT = s2("atT", [64, 8, 64])
            oT = s2("oT", [64, 8, 64])
            am = s2("am", [64, 8])

            def vs(op, *args, **kw):
                V.wait(V.now())
                V.do(op(*args, **kw))
                V.wait(V.now())
            for i in range(2):
                vs(vec.tensor_copy, st[:, 4 * i:4 * i + 4, :],
                                   tok8[i][:, 0:260].rearrange("p (h c) -> p h c", h=4))
            vs(vec.tensor_scalar, nr[:, :], st[:, :, 64], 1e-5, None, ALU.add)
            vs(vec.reciprocal, nr[:, :], nr[:, :])
            vs(vec.tensor_tensor, st[:, :, 0:64], st[:, :, 0:64], bc(nr[:, :].unsqueeze(2), [64, 8, 64]), ALU.mult)

            def heads(fn, dst, bank):
                P.wait(V.now(), A.now())
                for h in range(8):
                    fn(h, k.ps[bank][0:64, 64 * h:64 * h + 64])
                vs_wait = P.now()
                V.wait(vs_wait)
                vs(vec.tensor_copy, dst[:, :, :], k.ps[bank][0:64, :].rearrange("p (h c) -> p h c", h=8))
            i64 = k.ident[0:64, 0:64]
            heads(lambda h, o: P.do(nc.tensor.transpose(o, st[:, h, 0:64], i64)), stT, 0)
            heads(lambda h, o: mm(k, o, wq[:, :], stT[:, h, :]), qT, 1)
            heads(lambda h, o: mm(k, o, wk[:, :], stT[:, h, :]), kT, 2)
            heads(lambda h, o: mm(k, o, stT[:, h, :], wv[:, :]), vv, 3)
            heads(lambda h, o: mm(k, o, qT[:, h, :], kT[:, h, :]), at, 4)
            vs(vec.tensor_scalar, at[:, :, :], at[:, :, :], 0.125, None, ALU.mult)
            vs(vec.tensor_reduce, am[:, :], at[:, :, :], AX, ALU.max)
            vs(vec.tensor_tensor, at[:, :, :], at[:, :, :], bc(am[:, :].unsqueeze(2), [64, 8, 64]), ALU.subtract)
            A.wait(V.now())
            A.do(nc.scalar.activation(at[:, :, :], at[:, :, :], ACT.Exp))
            V.wait(A.now())
            vs(vec.tensor_reduce, am[:, :], at[:, :, :], AX, ALU.add)
            vs(vec.reciprocal, am[:, :], am[:, :])
            vs(vec.tensor_tensor, at[:, :, :], at[:, :, :], bc(am[:, :].unsqueeze(2), [64, 8, 64]), ALU.mult)
            heads(lambda h, o: P.do(nc.tensor.transpose(o, at[:, h, :], i64)), atT, 0)
            heads(lambda h, o: mm(k, o, vv[:, h, :], atT[:, h, :]), oT, 1)
            P.wait(V.now())
            pp = s2("pp", [64, 8, D])
            for h in range(8):
                bk = h % 2
                P.wait(k.pst[bk])
                mm(k, k.ps[bk][0:64, 0:D], oT[:, h, :], wo[:, h, :])
                V.wait(P.now())
                k.pst[bk] = V.do(vec.tensor_copy(pp[:, h, :], k.ps[bk][0:64, 0:D]))
            k.S.wait(V.now())
            for h in range(8):
                k.ld.start(Pm[64 * (h % 2):64 * (h % 2) + 64, h // 2, :], pp[:, h, :])
            fence(k)
        bo = bcast_row(k, es, a['L0_ffn_b_out'], D)
        V.wait(k.ld.all())
        wT = sb("wT", [128, 2, 4, 128])
        x3 = x.rearrange("p (b c) -> p b c", b=NB)
        for b in range(NB):
            bk = b % 2
            P.wait(k.pst[bk])
            for i in range(4):
                P.do(nc.tensor.transpose(k.ps[bk][:, 128 * i:128 * (i + 1)], sw[:, b, 128 * i:128 * (i + 1)],
                                         k.ident[:, :]))
            A.wait(P.now())
            k.pst[bk] = A.do(nc.scalar.copy(wT[:, bk, :, :].rearrange("p a b -> p (a b)"), k.ps[bk][:, :]))
            P.wait(A.now(), k.pst[2 + bk])
            for i in range(4):
                mm(k, k.ps[2 + bk][:, 0:D], wT[:, bk, i, :], Pm[:, i, :], start=(i == 0), stop=(i == 3))
            V.wait(P.now())
            k.pst[2 + bk] = V.do(vec.tensor_tensor(x3[:, b, :], x3[:, b, :], k.ps[2 + bk][:, 0:D], ALU.add))
            V.wait(V.now())
            V.do(vec.tensor_tensor(x3[:, b, :], x3[:, b, :], bo[:, :], ALU.add))
            A.wait(P.now())
        fence(k)


def stage_l1_gnn(k, x, a):
    nc, V, A, P = k.nc, k.V, k.A, k.P
    vec = nc.vector
    s = float(np.sqrt(np.float32(0.5)))
    table = nc.dram_tensor("hx_rel", (8 * 3200, D), F).ap()
    with ExitStack() as es:
        def sb(n, shape, dt=F):
            return es.enter_context(nc.sbuf_tensor(k.nm(n), shape, dt))
        h = sb("h", [128, NB * D])
        with ExitStack() as e2:
            xT = e2.enter_context(nc.sbuf_tensor(k.nm("xT"), [128, 2, 3200], F))
            layernorm(k, x, h[:, :])
            transpose_rows(k, h, xT)
            fence(k)
            w = e2.enter_context(nc.sbuf_tensor(k.nm("w"), [128, 2, 2048], F))
            wl = e2.enter_context(nc.sbuf_tensor(k.nm("wl"), [128, 2, D], F))
            for r in range(8):
                for c in range(2):
                    k.ld.start(w[:, c, D * r:D * (r + 1)], a['L1_gnn_weight'][r, 128 * c:128 * (c + 1), :])
            P.wait(load_w(k, wl, a['L1_gnn_loop_weight']))
            project(k, xT, w, 2048, dram_sink(k, e2, table, D))
            x3 = x.rearrange("p (b c) -> p b c", b=NB)

            def sink(b, m0, mw, ps):
                V.wait(P.now())
                return V.do(vec.scalar_tensor_tensor(out=x3[:, b, :], in0=ps, scalar=s, in1=x3[:, b, :],
                                                     op0=ALU.mult, op1=ALU.add))
            project(k, xT, wl, D, sink)
            fence(k)
        seg_sum(k, k.T, table, 8 * 3200, k.xtyp, k.dlR, k.off256, h)
        add_bias(k, x, a['L1_gnn_h_bias'])
        V.do(vec.scalar_tensor_tensor(out=x, in0=h[:, :], scalar=s, in1=x, op0=ALU.mult, op1=ALU.add))
        fence(k)


def top2_gates(k, sc, E, gates):
    nc, V, A = k.nc, k.V, k.A
    vec = nc.vector
    with ExitStack() as es:
        def sb(n, shape, dt=F):
            return es.enter_context(nc.sbuf_tensor(k.nm(n), shape, dt))
        mv = sb("mv", [128, NB, 8])
        mi = sb("mi", [128, NB, 8], U32)
        mf = sb("mf", [128, NB, 2])
        w = sb("w", [128, NB, 2])
        dn = sb("dn", [128, NB])
        t1 = sb("t1", [128, NB, E])

        def vs(op, *args, **kw):
            V.wait(V.now())
            V.do(op(*args, **kw))
        V.wait(V.now())
        for b in range(NB):
            V.do(vec.max(mv[:, b, :], sc[:, b, :]))
        V.wait(V.now())
        for b in range(NB):
            V.do(vec.max_index(mi[:, b, :], mv[:, b, :], sc[:, b, :]))
        vs(vec.tensor_copy, mf[:, :, :], mi[:, :, 0:2])
        vs(vec.tensor_tensor, dn[:, :], mv[:, :, 1], mv[:, :, 0], ALU.subtract)
        A.wait(V.now())
        A.do(nc.scalar.activation(w[:, :, 1], dn[:, :], ACT.Exp))
        V.wait(A.now())
        vs(vec.tensor_scalar, dn[:, :], w[:, :, 1], 1.0, None, ALU.add)
        vs(vec.reciprocal, w[:, :, 0], dn[:, :])
        vs(vec.tensor_tensor, w[:, :, 1], w[:, :, 1], w[:, :, 0], ALU.mult)
        io = bc(k.iof[:, 0:E].unsqueeze(1), [128, NB, E])
        vs(vec.tensor_tensor, gates, io, bc(mf[:, :, 0:1], [128, NB, E]), ALU.is_equal)
        vs(vec.tensor_tensor, gates, gates, bc(w[:, :, 0:1], [128, NB, E]), ALU.mult)
        vs(vec.tensor_tensor, t1[:, :, :], io, bc(mf[:, :, 1:2], [128, NB, E]), ALU.is_equal)
        vs(vec.tensor_tensor, t1[:, :, :], t1[:, :, :], bc(w[:, :, 1:2], [128, NB, E]), ALU.mult)
        vs(vec.tensor_tensor, gates, gates, t1[:, :, :], ALU.add)
        fence(k)


def moe(k, x, xT, gates, E, Hd, W1, b1, W2, b2):
    nc, V, A, P = k.nc, k.V, k.A, k.P
    vec = nc.vector
    HC = Hd // 128
    x3 = x.rearrange("p (b c) -> p b c", b=NB)
    with ExitStack() as es:
        def sb(n, shape, dt=F):
            return es.enter_context(nc.sbuf_tensor(k.nm(n), shape, dt))
        w1 = sb("w1", [128, 2, 2, Hd])
        w2 = sb("w2", [128, 2, HC, D])
        bb = sb("bb", [128, E, HC])
        b2s = sb("b2s", [E, D])
        gT = sb("gT", [E, 3200])
        hT = sb("hT", [128, 4, 512])
        k.ld.start(bb[:, :, :], b1.rearrange("e (c p) -> p e c", p=128), small=True)
        k.ld.start(b2s[:, :], b2)
        free = [None, None]

        def fetch(e):
            k.S.wait(free[e % 2])
            t = [k.ld.start(w1[:, e % 2, c, :], W1[e, 128 * c:128 * (c + 1), :]) for c in range(2)]
            t.append(k.ld.start(w2[:, e % 2, :, :], W2[e].rearrange("(c p) n -> p c n", p=128)))
            return t
        small = k.ld.all()
        tw = [fetch(0), fetch(1)]
        P.wait(small)
        A.wait(small)
        for b in range(NB):
            bk = b % 2
            P.wait(k.pst[bk])
            P.do(nc.tensor.transpose(k.ps[bk][0:E, 0:128], gates[:, b, :], k.ident[:, :]))
            A.wait(P.now())
            k.pst[bk] = A.do(nc.scalar.copy(gT[:, 128 * b:128 * (b + 1)], k.ps[bk][0:E, 0:128]))
            P.wait(A.now(), k.pst[2 + bk])
            mm(k, k.ps[2 + bk][:, 0:D], gT[:, 128 * b:128 * (b + 1)], b2s[:, :])
            V.wait(P.now())
            k.pst[2 + bk] = V.do(vec.tensor_tensor(x3[:, b, :], x3[:, b, :], k.ps[2 + bk][:, 0:D], ALU.add))
        hfree = [None] * 4
        hn = 0
        cn = 0
        for e in range(E):
            P.wait(tw[e])
            for ch in range(7):
                t0, tw_ = 512 * ch, min(512, 3200 - 512 * ch)
                oa = (4, 5) if cn % 2 == 0 else (6, 7)
                cn += 1
                pend = []

                def second(hc, slot, ta):
                    P.wait(ta)
                    if hc == 0:
                        P.wait(k.pst[oa[0]], k.pst[oa[1]])
                    for j in range(tw_ // 128):
                        hfree[slot] = mm(k, k.ps[oa[j // 2]][:, D * (j % 2):D * (j % 2 + 1)],
                                         hT[:, slot, 128 * j:128 * (j + 1)], w2[:, e % 2, hc, :],
                                         start=(hc == 0 and j % 2 == 0), stop=(hc == HC - 1))
                for hc in range(HC):
                    bk = hn % 4
                    slot = hn % 4
                    hn += 1
                    P.wait(k.pst[bk])
                    for c in range(2):
                        mm(k, k.ps[bk][:, 0:tw_], w1[:, e % 2, c, 128 * hc:128 * (hc + 1)], xT[:, c, t0:t0 + tw_],
                           start=(c == 0), stop=(c == 1))
                    A.wait(P.now(), hfree[slot])
                    ta = k.pst[bk] = A.do(nc.scalar.activation(hT[:, slot, 0:tw_], k.ps[bk][:, 0:tw_], ACT.Gelu,
                                                               bias=bb[:, e, hc:hc + 1]))
                    pend.append((hc, slot, ta))
                    if len(pend) > 1:
                        second(*pend.pop(0))
                for q in pend:
                    second(*q)
                tp = P.now()
                V.wait(tp)
                for j in range(tw_ // 128):
                    b = 4 * ch + j
                    V.wait(V.now())
                    k.pst[oa[j // 2]] = V.do(vec.scalar_tensor_tensor(
                        out=x3[:, b, :], in0=k.ps[oa[j // 2]][:, D * (j % 2):D * (j % 2 + 1)],
                        scalar=gates[:, b, e:e + 1], in1=x3[:, b, :], op0=ALU.mult, op1=ALU.add))
            free[e % 2] = P.now()
            if e + 2 < E:
                tw.append(fetch(e + 2))
        fence(k)


def second_edges(k, ei):
    nc, V, G = k.nc, k.V, k.G
    vec = nc.vector
    J, T = 537, 576
    k.T2 = T

    def load(sb, pay):
        d, t1 = load_int(k, sb, "d", J, ei[1, :], 4095)
        s, t2 = load_int(k, sb, "s", J, ei[0, :], 0)
        G.wait(t1, t2, V.now())
        lp = [G.do(nc.gpsimd.iota(z[:, 512:537], pattern=[[1, 25]], base=0, channel_multiplier=25)) for z in (d, s)]
        V.wait(lp, t1, t2)
        V.do(vec.tensor_copy(pay[:, :, 0], d[:, :]))
        V.do(vec.tensor_scalar(pay[:, :, 1], s[:, :], float(N - 1), None, ALU.min))
        return d
    tab, st, _ = sort_edges(k, "n", J, load, T, 2)
    blk, (k.n4, k.n16) = tile_blocks(k, "n", T, st, (4, 16))
    al = nc.alloc_sbuf_tensor
    k.dl2 = al("dl2", [128, T], F)
    k.xs2 = al("xs2", [128, T], U32)
    k.n_flags = edge_flags_dram(k, "n", T)
    with ExitStack() as es:
        p = es.enter_context(nc.sbuf_tensor("sorted_n", [128, T, 2], F))
        V.wait(k.ld.start(p[:, :, :].rearrange("p a b -> p (a b)"), tab.rearrange("(p r) w -> p (r w)", p=128)))
        V.do(vec.tensor_copy(k.xs2[:, :], p[:, :, 1]))
        V.do(vec.scalar_tensor_tensor(out=k.dl2[:, :], in0=blk[:, :], scalar=-128.0, in1=p[:, :, 0],
                                      op0=ALU.mult, op1=ALU.add))
        V.wait(V.now())
        to_rows(k, "nf", p[:, :, 0], T, k.n_flags[128:128 + T * 128])
        fence(k)


def stage_l1_ffn(k, x, a):
    nc, V, A, P, G = k.nc, k.V, k.A, k.P, k.G
    vec = nc.vector
    T = k.T2
    table = nc.dram_tensor("gat_rows", (3200, 20), F).ap()
    with ExitStack() as es:
        def sb(n, shape, dt=F):
            return es.enter_context(nc.sbuf_tensor(k.nm(n), shape, dt))

        def vs(op, *args, **kw):
            V.wait(V.now())
            return V.do(op(*args, **kw))
        xT = sb("xT", [128, 2, 3200])
        gates = sb("gates", [128, NB, 4])
        with ExitStack() as e2:
            def s2(n, shape, dt=F):
                return e2.enter_context(nc.sbuf_tensor(k.nm(n), shape, dt))
            with ExitStack() as e3:
                xn = e3.enter_context(nc.sbuf_tensor(k.nm("xn"), [128, NB * D], F))
                layernorm(k, x, xn[:, :])
                transpose_rows(k, xn, xT)
                fence(k)
            wg = s2("wg", [128, 2, 16])
            h = s2("h", [128, NB, 20])
            ad = s2("ad", [128, NB, 4])
            load_w(k, wg, a['L1_ffn_W_gat'])
            asr = bcast_row(k, e2, a['L1_ffn_att_src'].rearrange("h c -> (h c)"), 16)
            adr = bcast_row(k, e2, a['L1_ffn_att_dst'].rearrange("h c -> (h c)"), 16)
            bg = bcast_row(k, e2, a['L1_ffn_b_gat'], 16)
            lg = bcast_row(k, e2, a['L1_ffn_ln_gamma'], 16)
            lb = bcast_row(k, e2, a['L1_ffn_ln_beta'], 16)
            P.wait(k.ld.all())
            V.wait(k.ld.all())

            def sink(b, m0, mw, ps):
                V.wait(P.now())
                return V.do(vec.tensor_copy(h[:, b, 0:16], ps))
            project(k, xT, wg, 16, sink)
            tmp = s2("tmp", [128, NB, 16])
            for r, o in ((asr, h[:, :, 16:20]), (adr, ad[:, :, :])):
                vs(vec.tensor_tensor, tmp[:, :, :], h[:, :, 0:16], bc(r[:, :].unsqueeze(1), [128, NB, 16]), ALU.mult)
                vs(vec.tensor_reduce, o, tmp[:, :, :].rearrange("p b (h c) -> p b h c", h=4), AX, ALU.add)
            k.S.wait(V.now())
            k.ld.start(table.rearrange("(b p) c -> p b c", p=128), h[:, :, :])
            fence(k)
            gs = s2("gs", [128, T, 20])
            L = s2("L", [128, 4 * T])
            tg = [k.ind.gather(gs[:, t, :], table, k.xs2[:, t:t + 1], 3200) for t in range(T)]
            adf = ad[:, :, :].rearrange("p b c -> p (b c)")
            rows = DstRows(k, e2, k.dl2, k.n4, adf, 4)
            Lv = L[:, :].rearrange("p (h t) -> p h t", h=4)
            for t in range(T):
                bk, tp = rows(t)
                V.wait(tp, tg[t])
                k.pst[bk] = V.do(vec.tensor_tensor(Lv[:, :, t], k.ps[bk][:, 0:4], gs[:, t, 16:20], ALU.add))
            vs(vec.scalar_tensor_tensor, out=L[:, :], in0=L[:, :], scalar=0.2, in1=L[:, :], op0=ALU.mult, op1=ALU.max)
            fence(k)
            seg_softmax(k, "n1", L[:, :], 4, 32, T, k.n_flags, ALU.add, 1e-16)
            g4 = gs[:, :, 0:16].rearrange("p t (h c) -> p t h c", h=4)
            for c in range(4):
                vs(vec.tensor_tensor, gs[:, :, 0:16].rearrange("p t (h c) -> p h t c", h=4)[:, :, :, c],
                                     gs[:, :, 0:16].rearrange("p t (h c) -> p h t c", h=4)[:, :, :, c],
                                     Lv, ALU.mult)
            acc = s2("acc", [128, NB * 16])
            oh = s2("oh", [128, 6, 128])
            vs(vec.memset, acc[:, :], 0.0)
            free = [None] * 6
            pend = []

            def add(t, tp):
                V.wait(tp, V.now())
                off = vec.value_load(k.n16[0:1, t:t + 1], min_val=0, max_val=24 * 16)
                d = acc[:, bass.ds(off, 16)]
                k.pst[t % 4] = V.do(vec.tensor_tensor(d, d, k.ps[t % 4][:, 0:16], ALU.add))
            for t in range(T):
                V.wait(free[t % 6])
                to = onehot(k, oh[:, t % 6, :], k.dl2, t)
                P.wait(to, k.pst[t % 4])
                free[t % 6] = mm(k, k.ps[t % 4][:, 0:16], oh[:, t % 6, :], gs[:, t, 0:16])
                pend.append((t, free[t % 6]))
                if len(pend) > 2:
                    add(*pend.pop(0))
            for q in pend:
                add(*q)
            c3 = acc[:, :].rearrange("p (b c) -> p b c", b=NB)
            mu = s2("mu", [128, NB])

            def row16(r):
                return bc(r[:, :].unsqueeze(1), [128, NB, 16])
            vs(vec.tensor_tensor, c3, c3, row16(bg), ALU.add)
            vs(vec.tensor_reduce, mu[:, :], c3, AX, ALU.add)
            vs(vec.tensor_scalar, mu[:, :], mu[:, :], 1.0 / 16, None, ALU.mult)
            vs(vec.tensor_tensor, c3, c3, bc(mu[:, :].unsqueeze(2), [128, NB, 16]), ALU.subtract)
            vs(vec.tensor_tensor, tmp[:, :, :], c3, c3, ALU.mult)
            vs(vec.tensor_reduce, mu[:, :], tmp[:, :, :], AX, ALU.add)
            vs(vec.tensor_scalar, mu[:, :], mu[:, :], 1.0 / 16, 1e-5, ALU.mult, ALU.add)
            A.wait(V.now())
            A.do(nc.scalar.activation(mu[:, :], mu[:, :], ACT.Sqrt))
            V.wait(A.now())
            vs(vec.reciprocal, mu[:, :], mu[:, :])
            vs(vec.tensor_tensor, c3, c3, bc(mu[:, :].unsqueeze(2), [128, NB, 16]), ALU.mult)
            vs(vec.tensor_tensor, c3, c3, row16(lg), ALU.mult)
            vs(vec.tensor_tensor, c3, c3, row16(lb), ALU.add)
            sc = s2("sc", [128, NB, 8])
            vs(vec.memset, sc[:, :, :], NEG)
            vs(vec.tensor_reduce, sc[:, :, 0:4], c3.rearrange("p b (h e) -> p b e h", h=4), AX, ALU.add)
            vs(vec.tensor_scalar, sc[:, :, 0:4], sc[:, :, 0:4], 0.25, None, ALU.mult)
            fence(k)
            top2_gates(k, sc, 4, gates[:, :, :])
        moe(k, x, xT, gates, 4, 512, a['L1_ffn_W1'], a['L1_ffn_b1'], a['L1_ffn_W2'], a['L1_ffn_b2'])


def stage_l2_gnn(k, x, a):
    nc, V, A, P = k.nc, k.V, k.A, k.P
    vec = nc.vector
    with ExitStack() as es:
        def sb(n, shape, dt=F):
            return es.enter_context(nc.sbuf_tensor(k.nm(n), shape, dt))

        def vs(op, *args, **kw):
            V.wait(V.now())
            return V.do(op(*args, **kw))
        h = sb("h", [128, NB * D])
        h3 = h[:, :].rearrange("p (b c) -> p b c", b=NB)
        xT = sb("xT", [128, 2, 3200])
        dinv = sb("dinv", [128, NB])
        pos = sb("pos", [128, NB])
        xn = sb("xn", [128, NB * D])
        layernorm(k, x, xn[:, :])
        transpose_rows(k, xn, xT)
        fence(k)
        vs(vec.tensor_scalar, pos[:, :], k.deg[:, :], 0.5, None, ALU.is_gt)
        vs(vec.tensor_scalar, dinv[:, :], k.deg[:, :], 1e-12, None, ALU.max)
        A.wait(V.now())
        A.do(nc.scalar.activation(dinv[:, :], dinv[:, :], ACT.Sqrt))
        V.wait(A.now())
        vs(vec.reciprocal, dinv[:, :], dinv[:, :])
        vs(vec.tensor_tensor, dinv[:, :], dinv[:, :], pos[:, :], ALU.mult)
        w = sb("w", [128, 2, D])
        for i in range(2):
            table = nc.dram_tensor(f"gcn{i}", (3200, D), F).ap()
            with ExitStack() as e2:
                P.wait(load_w(k, w, a[f'L2_gnn_W{i + 1}']), V.now())
                buf = e2.enter_context(nc.sbuf_tensor(k.nm("tb"), [128, 6, D], F))
                free = [None] * 6

                def sink(b, m0, mw, ps):
                    V.wait(P.now(), free[b % 6])
                    t = V.do(vec.tensor_scalar(buf[:, b % 6, :], ps, dinv[:, b:b + 1], None, ALU.mult))
                    k.S.wait(t)
                    free[b % 6] = k.ld.start(table[128 * b:128 * (b + 1), :], buf[:, b % 6, :])
                    return t
                V.wait(V.now())
                project(k, xT, w, D, sink)
                fence(k)
            seg_sum(k, k.T, table, 3200, k.xsrc, k.dlA, k.off256, h)
            vs(vec.tensor_tensor, h3, h3, bc(dinv[:, :].unsqueeze(2), [128, NB, D]), ALU.mult)
            fence(k)
            add_bias(k, h[:, :], a[f'L2_gnn_b{i + 1}'])
            if i == 0:
                nr = sb("nr", [128, NB])
                junk = sb("junk", [128, D])
                for b in range(NB):
                    A.wait(A.now())
                    A.do(nc.scalar.activation(junk[:, :], h3[:, b, :], ACT.Square, accum_out=nr[:, b:b + 1]))
                A.wait(A.now())
                A.do(nc.scalar.activation(nr[:, :], nr[:, :], ACT.Sqrt))
                V.wait(A.now())
                vs(vec.tensor_scalar, nr[:, :], nr[:, :], 1e-12, None, ALU.max)
                vs(vec.reciprocal, nr[:, :], nr[:, :])
                vs(vec.tensor_tensor, h3, h3, bc(nr[:, :].unsqueeze(2), [128, NB, D]), ALU.mult)
                transpose_rows(k, h, xT)
                fence(k)
        vs(vec.tensor_tensor, h[:, :], h[:, :], xn[:, :], ALU.add)
        vs(vec.tensor_tensor, x, x, h[:, :], ALU.add)
        fence(k)


def stage_l2_ffn(k, x, a):
    nc, V, A, P, G = k.nc, k.V, k.A, k.P, k.G
    vec = nc.vector
    x3 = x.rearrange("p (b c) -> p b c", b=NB)
    with ExitStack() as es:
        def sb(n, shape, dt=F):
            return es.enter_context(nc.sbuf_tensor(k.nm(n), shape, dt))

        def vs(op, *args, **kw):
            V.wait(V.now())
            return V.do(op(*args, **kw))
        xT = sb("xT", [128, 2, 3200])
        with ExitStack() as e3:
            xn = e3.enter_context(nc.sbuf_tensor(k.nm("xn"), [128, NB * D], F))
            layernorm(k, x, xn[:, :])
            transpose_rows(k, xn, xT)
            fence(k)
        rw = sb("rw", [32, D])
        rwT = sb("rwT", [128, 2, 32])
        k.ld.start(rw[:, :], a['L2_ffn_router_w'])
        rb = bcast_row(k, es, a['L2_ffn_router_b'], 32)
        w1 = sb("w1", [128, 2, 32, 64])
        for c in range(2):
            k.ld.start(w1[:, c, :, :], a['L2_ffn_W1'][:, 128 * c:128 * (c + 1), :].rearrange("e p h -> p e h"))
        b1 = sb("b1", [128, 16])
        k.ld.start(b1[:, :], a['L2_ffn_b1'].rearrange("(i e) h -> (e h) i", e=2), small=True)
        w2 = sb("w2", [128, 16, D])
        k.ld.start(w2[:, :, :], a['L2_ffn_W2'].rearrange("(i e) h n -> (e h) i n", e=2))
        b2 = sb("b2", [32, D])
        k.ld.start(b2[:, :], a['L2_ffn_b2'])
        P.wait(k.ld.all())
        V.wait(k.ld.all())
        A.wait(k.ld.all())
        for c in range(2):
            P.do(nc.tensor.transpose(k.ps[0][:, 32 * c:32 * c + 32], rw[:, 128 * c:128 * (c + 1)], k.ident[0:32, 0:32]))
        V.wait(P.now())
        vs(vec.tensor_copy, rwT[:, :, :], k.ps[0][:, 0:64].rearrange("p (c e) -> p c e", c=2))
        k.pst[0] = V.now()
        lg = sb("lg", [128, NB, 32])

        def sink(b, m0, mw, ps):
            V.wait(P.now())
            return V.do(vec.tensor_tensor(lg[:, b, :], ps, rb[:, :], ALU.add))
        P.wait(V.now())
        project(k, xT, rwT, 32, sink)
        mv = sb("mv", [128, NB, 8])
        mi = sb("mi", [128, NB, 8], U32)
        mf = sb("mf", [128, NB, 1])
        oh = sb("oh", [128, NB, 32])
        V.wait(V.now())
        for b in range(NB):
            V.do(vec.max(mv[:, b, :], lg[:, b, :]))
        V.wait(V.now())
        for b in range(NB):
            V.do(vec.max_index(mi[:, b, :], mv[:, b, :], lg[:, b, :]))
        vs(vec.tensor_copy, mf[:, :, :], mi[:, :, 0:1])
        vs(vec.tensor_tensor, oh[:, :, :], bc(k.iof[:, 0:32].unsqueeze(1), [128, NB, 32]),
                             bc(mf[:, :, :], [128, NB, 32]), ALU.is_equal)
        P.wait(V.now())
        ohT = sb("ohT", [32, 3200])
        nohT = sb("nohT", [32, 3200], BF)
        sel = sb("sel", [32, 32, 64], BF)
        vs(vec.tensor_scalar, sel[:, :, :], bc(k.ident[0:32, 0:32].unsqueeze(2), [32, 32, 64]), NEG, None, ALU.mult)
        for b in range(NB):
            bk = b % 2
            P.wait(k.pst[bk])
            P.do(nc.tensor.transpose(k.ps[bk][0:32, 0:128], oh[:, b, :], k.ident[:, :]))
            A.wait(P.now())
            k.pst[bk] = A.do(nc.scalar.copy(ohT[:, 128 * b:128 * (b + 1)], k.ps[bk][0:32, 0:128]))
        V.wait(A.now())
        vs(vec.tensor_scalar, nohT[:, :], ohT[:, :], -1.0, 1.0, ALU.mult, ALU.add)
        P.wait(V.now(), A.now())
        hT = sb("hT", [128, 4, 512])
        hfree = [None] * 4
        hn = 0
        for ch in range(7):
            t0, tw = 512 * ch, min(512, 3200 - 512 * ch)
            oa = (4, 5) if ch % 2 == 0 else (6, 7)
            pend = []

            def second(i, slot, ta):
                P.wait(ta)
                for j in range(tw // 128):
                    hfree[slot] = mm(k, k.ps[oa[j // 2]][:, D * (j % 2):D * (j % 2 + 1)],
                                     hT[:, slot, 128 * j:128 * (j + 1)], w2[:, i, :], start=False, stop=(i == 15))
            P.wait(k.pst[oa[0]], k.pst[oa[1]])
            for j in range(tw // 128):
                mm(k, k.ps[oa[j // 2]][:, D * (j % 2):D * (j % 2 + 1)],
                   ohT[:, t0 + 128 * j:t0 + 128 * (j + 1)], b2[:, :], start=(j % 2 == 0), stop=False)
            for i in range(16):
                bk = slot = hn % 4
                hn += 1
                P.wait(k.pst[bk])
                for c in range(2):
                    mm(k, k.ps[bk][:, 0:tw], w1[:, c, 2 * i:2 * i + 2, :].rearrange("p e h -> p (e h)"),
                       xT[:, c, t0:t0 + tw], start=(c == 0), stop=False)
                mm(k, k.ps[bk][:, 0:tw], sel[:, 2 * i:2 * i + 2, :].rearrange("p e h -> p (e h)"),
                   nohT[:, t0:t0 + tw], start=False, stop=True)
                A.wait(P.now(), hfree[slot])
                ta = k.pst[bk] = A.do(nc.scalar.activation(hT[:, slot, 0:tw], k.ps[bk][:, 0:tw], ACT.Relu,
                                                           bias=b1[:, i:i + 1]))
                pend.append((i, slot, ta))
                if len(pend) > 1:
                    second(*pend.pop(0))
            for q in pend:
                second(*q)
            V.wait(P.now())
            for j in range(tw // 128):
                b = 4 * ch + j
                k.pst[oa[j // 2]] = V.do(vec.scalar_tensor_tensor(
                    out=x3[:, b, :], in0=k.ps[oa[j // 2]][:, D * (j % 2):D * (j % 2 + 1)],
                    scalar=0.0, in1=x3[:, b, :], op0=ALU.max, op1=ALU.add))
        fence(k)


def stage_l3_gnn(k, x, a):
    nc, V, A, P, G = k.nc, k.V, k.A, k.P, k.G
    vec = nc.vector
    T = k.T
    table = nc.dram_tensor("h3", (3200, D), F).ap()
    tabs = nc.dram_tensor("as3", (3200, 8), F).ap()
    with ExitStack() as es:
        def sb(n, shape, dt=F):
            return es.enter_context(nc.sbuf_tensor(k.nm(n), shape, dt))

        def vs(op, *args, **kw):
            V.wait(V.now())
            return V.do(op(*args, **kw))
        L = sb("L", [128, 8 * T])
        Lv = L[:, :].rearrange("p (h t) -> p h t", h=8)
        with ExitStack() as e2:
            def s2(n, shape, dt=F):
                return e2.enter_context(nc.sbuf_tensor(k.nm(n), shape, dt))
            ha = s2("ha", [128, NB, 264])
            with ExitStack() as e3:
                xn = e3.enter_context(nc.sbuf_tensor(k.nm("xn"), [128, NB * D], F))
                xT = e3.enter_context(nc.sbuf_tensor(k.nm("xT"), [128, 2, 3200], F))
                w = e3.enter_context(nc.sbuf_tensor(k.nm("w"), [128, 2, D], F))
                wT = e3.enter_context(nc.sbuf_tensor(k.nm("wT"), [128, 2, D], F))
                asb = e3.enter_context(nc.sbuf_tensor(k.nm("as"), [128, NB, 8], F))
                tmp = e3.enter_context(nc.sbuf_tensor(k.nm("tmp"), [128, NB, D], F))
                layernorm(k, x, xn[:, :])
                transpose_rows(k, xn, xT)
                load_w(k, w, a['L3_gnn_W'])
                asr = bcast_row(k, e3, a['L3_gnn_a_src'].rearrange("h c -> (h c)"), D)
                adr = bcast_row(k, e3, a['L3_gnn_a_dst'].rearrange("h c -> (h c)"), D)
                P.wait(k.ld.all(), k.pst[2], k.pst[3])
                V.wait(k.ld.all())
                for i in range(2):
                    for j in range(2):
                        P.do(nc.tensor.transpose(k.ps[2][:, 256 * i + 128 * j:256 * i + 128 * j + 128],
                                                 w[:, j, 128 * i:128 * (i + 1)], k.ident[:, :]))
                V.wait(P.now())
                k.pst[2] = vs(vec.tensor_copy, wT[:, :, :].rearrange("p a b -> p (a b)"), k.ps[2][:, :])
                P.wait(V.now())

                def sink(b, m0, mw, ps):
                    V.wait(P.now())
                    return V.do(vec.tensor_copy(ha[:, b, 0:D], ps))
                project(k, xT, wT, D, sink)
                k.S.wait(V.now())
                k.ld.start(table.rearrange("(b p) c -> p b c", p=128), ha[:, :, 0:D])
                for r, o in ((asr, asb[:, :, :]), (adr, ha[:, :, D:D + 8])):
                    vs(vec.tensor_tensor, tmp[:, :, :], ha[:, :, 0:D], bc(r[:, :].unsqueeze(1), [128, NB, D]), ALU.mult)
                    vs(vec.tensor_reduce, o, tmp[:, :, :].rearrange("p b (h c) -> p b h c", h=8), AX, ALU.add)
                k.S.wait(V.now())
                k.ld.start(tabs.rearrange("(b p) c -> p b c", p=128), asb[:, :, :])
                fence(k)
            ew = s2("ew", [4, D])
            k.ld.start(ew[0:3, :], a['L3_gnn_edge_W'].rearrange("n f -> f n"), small=True)
            k.ld.start(ew[3:4, :], rows_of(a['L3_gnn_edge_b']))
            P.wait(k.ld.all())
            AS = s2("AS", [128, T, 8])
            tg = [k.ind.gather(AS[:, t, :], tabs, k.xsrc[:, t:t + 1], 3200) for t in range(T)]
            rows = DstRows(k, e2, k.dlA, k.off264, ha[:, :, :].rearrange("p b c -> p (b c)"), 264)
            aT = s2("aT", [4, 4, 128])
            en = s2("en", [128, 4, D])
            af = [None] * 4
            ef = [None] * 4
            for t in range(T):
                i = t % 4
                P.wait(k.pst[7])
                P.do(nc.tensor.transpose(k.ps[7][0:4, 0:128], k.attr[:, t, :], k.ident[:, :]))
                A.wait(P.now(), af[i])
                k.pst[7] = A.do(nc.scalar.copy(aT[:, i, :], k.ps[7][0:4, 0:128]))
                bk, tp = rows(t)
                eb = 5 + t % 2
                P.wait(A.now(), k.pst[eb])
                P.wait(k.pst[7])
                af[i] = mm(k, k.ps[eb][:, 0:D], aT[:, i, :], ew[:, :])
                A.wait(af[i], ef[i])
                k.pst[eb] = te = A.do(nc.scalar.activation(en[:, i, :], k.ps[eb][:, 0:D], ACT.Relu))
                V.wait(te, tp)
                V.do(vec.tensor_tensor(en[:, i, :], en[:, i, :], k.ps[bk][:, 0:D], ALU.mult))
                V.wait(V.now())
                ef[i] = V.do(vec.tensor_reduce(Lv[:, :, t], en[:, i, :].rearrange("p (h c) -> p h c", h=8), AX, ALU.add))
                V.wait(V.now())
                k.pst[bk] = V.do(vec.tensor_tensor(Lv[:, :, t], Lv[:, :, t], k.ps[bk][:, D:D + 8], ALU.add))
            V.wait(tg)
            vs(vec.tensor_tensor, Lv, Lv, AS[:, :, :].rearrange("p t h -> p h t"), ALU.add)
            vs(vec.scalar_tensor_tensor, out=L[:, :], in0=L[:, :], scalar=0.2, in1=L[:, :], op0=ALU.mult, op1=ALU.max)
            vs(vec.tensor_tensor, Lv, Lv, bc(k.loopneg[:, :].unsqueeze(1), [128, 8, T]), ALU.add)
            fence(k)
        seg_softmax(k, "g3", L[:, :], 8, 16, T, k.m_flags, ALU.max, 1e-10)
        h = sb("h", [128, NB * D])
        seg_sum(k, T, table, 3200, k.xsrc, k.dlR, k.off256, h, alpha=L[:, :], H=8)
        add_bias(k, h[:, :], a['L3_gnn_bias'])
        vs(vec.tensor_tensor, x, x, h[:, :], ALU.add)
        fence(k)


def stage_l3_ffn(k, x, a):
    nc, V, A, P, G = k.nc, k.V, k.A, k.P, k.G
    vec = nc.vector
    with ExitStack() as es:
        def sb(n, shape, dt=F):
            return es.enter_context(nc.sbuf_tensor(k.nm(n), shape, dt))
        xT = sb("xT", [128, 2, 3200])
        gates = sb("gates", [128, NB, 8])
        with ExitStack() as e3:
            xn = e3.enter_context(nc.sbuf_tensor(k.nm("xn"), [128, NB * D], F))
            layernorm(k, x, xn[:, :])
            transpose_rows(k, xn, xT)
            fence(k)
        with ExitStack() as e3:
            wg = e3.enter_context(nc.sbuf_tensor(k.nm("wg"), [128, 2, 8], F))
            sc = e3.enter_context(nc.sbuf_tensor(k.nm("sc"), [128, NB, 8], F))
            load_w(k, wg, a['L3_ffn_Wg'])
            bg = bcast_row(k, e3, a['L3_ffn_bg'], 8)
            P.wait(k.ld.all())
            V.wait(k.ld.all())

            def sink(b, m0, mw, ps):
                V.wait(P.now())
                return V.do(vec.tensor_tensor(sc[:, b, :], ps, bg[:, :], ALU.add))
            project(k, xT, wg, 8, sink)
            fence(k)
            top2_gates(k, sc, 8, gates[:, :, :])
        moe(k, x, xT, gates, 8, 1024, a['L3_ffn_W1'], a['L3_ffn_b1'], a['L3_ffn_W2'], a['L3_ffn_b2'])


STAGES = [stage_l0_gnn, stage_l0_ffn, stage_l1_gnn, stage_l1_ffn, stage_l2_gnn, stage_l2_ffn, stage_l3_gnn,
          stage_l3_ffn]


def build(nc, a, out, stages=tuple(range(8))):
    k = make_ctx(nc)
    n = [0]

    def nm(s):
        n[0] += 1
        return f"{s}_{n[0]}"
    k.nm = nm
    constants(k)
    main_edges(k, a['src'], a['dst'], a['edge_attr_3'], a['edge_type_8'])
    if 3 in stages:
        second_edges(k, a['L1_ffn_edge_index'])
    x = nc.alloc_sbuf_tensor("x", [128, NB * D], F)
    x3 = x[:, :].rearrange("p (b c) -> p b c", b=NB)
    k.V.do(nc.vector.memset(x[:, 24 * D:], 0.0))
    k.S.wait(k.V.now())
    k.ld.start(x3[:, 0:24, :], a['x'][0:3072, :].rearrange("(b p) c -> p b c", p=128))
    k.ld.start(x[0:LASTP, 24 * D:], a['x'][3072:N, :])
    fence(k)
    for i in stages:
        STAGES[i](k, x[:, :], a)
    k.ld.start(out[0:3072, :].rearrange("(b p) c -> p b c", p=128), x3[:, 0:24, :])
    k.ld.start(out[3072:N, :], x[0:LASTP, 24 * D:])
    fence(k)


_INS = ['x', 'src', 'dst', 'edge_attr_3', 'edge_type_8', 'L0_gnn_Wl1', 'L0_gnn_Wr1', 'L0_gnn_att1', 'L0_gnn_b1', 'L0_gnn_Wl2', 'L0_gnn_Wr2', 'L0_gnn_att2', 'L0_gnn_b2', 'L0_ffn_W_fx', 'L0_ffn_b_fx', 'L0_ffn_W_x', 'L0_ffn_b_x', 'L0_ffn_W_slice', 'L0_ffn_b_slice', 'L0_ffn_W_q', 'L0_ffn_W_k', 'L0_ffn_W_v', 'L0_ffn_W_out', 'L0_ffn_b_out', 'L0_ffn_temperature', 'L1_gnn_weight', 'L1_gnn_h_bias', 'L1_gnn_loop_weight', 'L1_ffn_W_gat', 'L1_ffn_att_src', 'L1_ffn_att_dst', 'L1_ffn_b_gat', 'L1_ffn_ln_gamma', 'L1_ffn_ln_beta', 'L1_ffn_W1', 'L1_ffn_b1', 'L1_ffn_W2', 'L1_ffn_b2', 'L1_ffn_edge_index', 'L2_gnn_W1', 'L2_gnn_b1', 'L2_gnn_W2', 'L2_gnn_b2', 'L2_ffn_router_w', 'L2_ffn_router_b', 'L2_ffn_W1', 'L2_ffn_b1', 'L2_ffn_W2', 'L2_ffn_b2', 'L3_gnn_W', 'L3_gnn_a_src', 'L3_gnn_a_dst', 'L3_gnn_edge_W', 'L3_gnn_edge_b', 'L3_gnn_bias', 'L3_ffn_Wg', 'L3_ffn_bg', 'L3_ffn_W1', 'L3_ffn_b1', 'L3_ffn_W2', 'L3_ffn_b2']


def kernel(**inputs):
    import numpy as _np
    import concourse.bacc as _bacc
    from concourse import mybir as _mybir
    from concourse.bass_utils import run_bass_kernel_spmd as _run

    nc = _bacc.Bacc("TRN2", target_bir_lowering=False, num_devices=1)
    arrays, args = {}, {}
    for name in _INS:
        v = _np.ascontiguousarray(inputs[name])
        arrays[f"in_{name}_dram"] = v
        args[name] = nc.dram_tensor(f"in_{name}_dram", v.shape, _mybir.dt.from_np(v.dtype), kind="ExternalInput").ap()
    out = nc.dram_tensor("out_0_dram", (3125, 256), _mybir.dt.float32, kind="ExternalOutput").ap()
    build(nc, args, out)
    r = _run(nc, [arrays], core_ids=[0])
    return r.results[0]["out_0_dram"]
```

```python
from contextlib import ExitStack

import numpy as np

import concourse.bass as bass
from concourse import mybir

F = mybir.dt.float32
BF = mybir.dt.bfloat16
I32 = mybir.dt.int32
U32 = mybir.dt.uint32
ALU = mybir.AluOpType
ACT = mybir.ActivationFunctionType
AX = mybir.AxisListType.X

N = 3125
NB = 25
D = 256
LASTP = N - 24 * 128
NEG = -1.0e30
FILL = -1000.0


class Queue:

    def __init__(self, nc, eng, name):
        self.nc, self.eng, self.sem, self.n = nc, eng, nc.alloc_semaphore(name), 0
        self.name = self.base = name
        self.gen = 0
        self.seen = {}

    def wait(self, *tokens):
        for tok in tokens:
            if tok is None:
                continue
            if isinstance(tok, list):
                self.wait(*tok)
                continue
            name, sem, value = tok
            if self.seen.get(name, 0) < value:
                self.eng.wait_ge(sem, value)
                self.seen[name] = value

    def do(self, ins):
        ins.then_inc(self.sem, 1)
        self.n += 1
        return (self.name, self.sem, self.n)

    def renew(self):
        if self.n > 4000:
            self.gen += 1
            self.name = f"{self.base}_{self.gen}"
            self.sem, self.n = self.nc.alloc_semaphore(self.name), 0

    def now(self):
        return (self.name, self.sem, self.n) if self.n else None


class Dmas:

    def __init__(self, nc, queue, name, ring):
        self.q, self.name = queue, name
        self.sems = [nc.alloc_semaphore(f"{name}{i}") for i in range(ring)]
        self.count = [0] * ring
        self.k = 0

    def slot(self):
        i = self.k % len(self.sems)
        self.k += 1
        self.q.wait(self.token(i))
        return i

    def token(self, i):
        return (f"{self.name}{i}", self.sems[i], 16 * self.count[i]) if self.count[i] else None

    def start(self, out, in_, small=False):
        i = self.slot()
        self.q.eng.dma_start(out, in_, allow_slow_non_contiguous=small).then_inc(self.sems[i], 16)
        self.count[i] += 1
        return self.token(i)

    def gather(self, out, table, index, rows):
        i = self.slot()
        self.q.eng.indirect_dma_start(
            out=out, out_offset=None, in_=table,
            in_offset=bass.IndirectOffsetOnAxis(ap=index, axis=0),
            bounds_check=rows - 1, oob_is_err=False).then_inc(self.sems[i], 16)
        self.count[i] += 1
        return self.token(i)

    def scatter(self, table, index, in_, rows):
        i = self.slot()
        self.q.eng.indirect_dma_start(
            out=table, out_offset=bass.IndirectOffsetOnAxis(ap=index, axis=0),
            in_=in_, in_offset=None,
            bounds_check=rows - 1, oob_is_err=False).then_inc(self.sems[i], 16)
        self.count[i] += 1
        return self.token(i)

    def all(self):
        return [self.token(i) for i in range(len(self.sems))]


class Ctx:
    pass


def bc(ap, shape):
    return ap.to_broadcast(shape)


def make_ctx(nc):
    k = Ctx()
    k.nc = nc
    k.edges = ExitStack()
    k.V = Queue(nc, nc.vector, "qv")
    k.A = Queue(nc, nc.scalar, "qa")
    k.P = Queue(nc, nc.tensor, "qp")
    k.G = Queue(nc, nc.gpsimd, "qg")
    k.S = Queue(nc, nc.sync, "qs")
    k.ld = Dmas(nc, k.S, "dl", 12)
    k.st = Dmas(nc, k.A, "da", 8)
    k.ind = Dmas(nc, k.G, "dg", 24)
    k.late = Dmas(nc, k.G, "dt", 16)
    k.ps = [nc.alloc_psum_tensor(f"ps{i}", [128, 512], F) for i in range(8)]
    k.pst = [None] * 8
    return k


def fence_but_pool(k):
    toks = [q.now() for q in (k.V, k.A, k.P)] + k.ld.all() + k.st.all()
    for q in (k.V, k.A, k.P, k.S):
        q.wait(toks)
    k.pst = [None] * 8


def fence(k):
    toks = [q.now() for q in (k.V, k.A, k.P, k.G)] + k.ld.all() + k.st.all() + k.ind.all()
    for q in (k.V, k.A, k.P, k.G, k.S):
        q.wait(toks)
    k.pst = [None] * 8
    for q in (k.V, k.A, k.P, k.G):
        q.renew()


def pipeline(n, *steps):
    top = max(lag for lag, _ in steps)
    for i in range(n + top):
        for lag, fn in sorted(steps, key=lambda s: -s[0]):
            if 0 <= i - lag < n:
                fn(i - lag)


class Offsets:

    def __init__(self, k, engine, offs, top):
        self.k, self.engine, self.offs, self.top = k, engine, offs, top
        self.at = None

    def __call__(self, t):
        if self.at != t // 8:
            self.at = t // 8
            n = min(8, self.offs.shape[1] - 8 * self.at)
            _, self.regs = self.k.nc.values_load_multi_w_load_instructions(
                self.offs[0:1, 8 * self.at:8 * self.at + n], engines=[self.engine], min_val=0, max_val=self.top,
                skip_runtime_bounds_check_because="a tile's block is at most 24 by construction")
        return self.regs[t % 8]


def mm(k, out, lhsT, rhs, start=True, stop=True):
    return k.P.do(k.nc.tensor.matmul(out, lhsT, rhs, start=start, stop=stop, skip_group_check=True))


def constants(k):
    nc, V, G = k.nc, k.V, k.G
    al = nc.alloc_sbuf_tensor
    k.ident = al("ident", [128, 128], F)
    k.identb = al("identb", [128, 128], BF)
    k.ltri = al("ltri", [128, 128], F)
    k.lmask = al("lmask", [128, 128], F)
    k.ones = al("ones", [128, 128], F)
    k.iof = al("iof", [128, 128], F)
    k.iob = al("iob", [128, 128], BF)
    k.ltrib = al("ltrib", [128, 128], BF)
    k.onesb = al("onesb", [128, 128], BF)
    a = V.do(nc.vector.memset(k.ones[:, :], 1.0))
    V.do(nc.vector.memset(k.ident[:, :], 0.0))
    b = V.do(nc.vector.memset(k.identb[:, :], 0.0))
    G.wait(a, b)
    t0 = G.do(nc.gpsimd.affine_select(out=k.ident[:, :], in_=k.ident[:, :], compare_op=ALU.not_equal, fill=1.0,
                                      base=0, pattern=[[-1, 128]], channel_multiplier=1))
    t2 = G.do(nc.gpsimd.affine_select(out=k.ltri[:, :], in_=k.ones[:, :], compare_op=ALU.is_gt, fill=0.0,
                                 base=0, pattern=[[1, 128]], channel_multiplier=-1))
    G.do(nc.gpsimd.affine_select(out=k.lmask[:, :], in_=k.ones[:, :], compare_op=ALU.is_gt, fill=0.0,
                                 base=0, pattern=[[-1, 128]], channel_multiplier=1))
    t1 = G.do(nc.gpsimd.iota(k.iof[:, :], pattern=[[1, 128]], base=0, channel_multiplier=0,
                             allow_small_or_imprecise_dtypes=True))
    k.tiles = al("tiles", [128, 576], F)
    G.do(nc.gpsimd.iota(k.tiles[:, :], pattern=[[1, 576]], base=0, channel_multiplier=0,
                        allow_small_or_imprecise_dtypes=True))
    V.wait(t0, t1, t2)
    V.do(nc.vector.tensor_copy(k.ltrib[:, :], k.ltri[:, :]))
    V.do(nc.vector.tensor_copy(k.onesb[:, :], k.ones[:, :]))
    V.do(nc.vector.tensor_copy(k.identb[:, :], k.ident[:, :]))
    V.do(nc.vector.tensor_copy(k.iob[:, :], k.iof[:, :]))
    fence(k)


class EdgeList:

    def __init__(self, k, es, name, J, T, Wd):
        nc = k.nc
        self.name, self.J, self.T, self.Wd = name, J, T, Wd
        self.tab = nc.dram_tensor(f"tab_{name}", (128 * T, Wd), F).ap()

        def al(n, shape, dt):
            return k.edges.enter_context(nc.sbuf_tensor(n, shape, dt))

        def sb(n, shape, dt):
            return es.enter_context(nc.sbuf_tensor(f"{name}_{n}", shape, dt))
        self.st = al(f"st_{name}", [128, 26], F)
        self.cnt = al(f"cnt_{name}", [128, NB], F)
        keep = al if name == "n" else None
        self.pay = keep("n_pay", [128, J, Wd], F) if keep else None
        self.addr = keep("n_addr", [128, J], U32) if keep else None
        self.sb = sb

    def place(self, x, at):
        sb, J = self.sb, self.J
        if self.pay is None:
            self.pay = x[:, at:at + J * self.Wd].rearrange("p (j w) -> p j w", w=self.Wd)
            self.addr = sb("addr", [128, J], U32)
            at += J * self.Wd
        self.lo, self.hi = x[:, at:at + J], x[:, at + J:at + 2 * J]
        at += 2 * J
        if at + J <= x.shape[1]:
            self.inv = x[:, at:at + J]
            return at + J
        self.inv = sb("inv", [128, J], F)
        return at


def split_digits(k, e, load):
    nc, V = k.nc, k.V
    vec = nc.vector
    with ExitStack() as es:
        def sb(n, shape, dt):
            return es.enter_context(nc.sbuf_tensor(f"{e.name}_{n}", shape, dt))
        filla = sb("fill", [128, e.T, e.Wd], F)
        V.do(vec.memset(filla[:, :, :], 0.0))
        V.wait(V.now())
        V.do(vec.memset(filla[:, :, 0], FILL))
        k.S.wait(V.now())
        k.ld.start(e.tab.rearrange("(p r) w -> p (r w)", p=128), filla[:, :, :].rearrange("p a b -> p (a b)"))
        dst = load(sb, e.pay)
        ti = sb("ti", [128, e.J], I32)
        V.wait(V.now())
        V.do(vec.tensor_scalar(ti[:, :], dst[:, :], 127, None, ALU.bitwise_and))
        V.wait(V.now())
        V.do(vec.tensor_copy(e.lo[:, :], ti[:, :]))
        V.wait(V.now())
        V.do(vec.tensor_scalar(ti[:, :], dst[:, :], 7, None, ALU.arith_shift_right))
        V.wait(V.now())
        V.do(vec.tensor_copy(e.hi[:, :], ti[:, :]))
        V.do(vec.tensor_scalar(e.inv[:, :], e.pay[:, :, 0], float(N) - 0.5, 1.0e6, ALU.is_gt, ALU.mult))
        V.wait(V.now())
        V.do(vec.tensor_tensor(e.hi[:, :], e.hi[:, :], e.inv[:, :], ALU.add))
        V.wait(V.now())
        fence(k)


def sort_edges(k, e, now):
    nc, V, A, P, G = k.nc, k.V, k.A, k.P, k.G
    vec = nc.vector
    name, J, T, st, cnt = e.name, e.J, e.T, e.st, e.cnt
    pay, lo, hi, inv, addr = e.pay, e.lo, e.hi, e.inv, e.addr
    with ExitStack() as es:
        def sb(n, shape, dt):
            return es.enter_context(nc.sbuf_tensor(f"{name}_{n}", shape, dt))
        NG = (J + 15) // 16
        ohi = sb("ohi", [128, NG, 16, NB], BF)
        hist = sb("hist", [128, J, NB], BF)
        cum = sb("cum", [128, NB, J + 1], F)
        olo = sb("olo", [128, 12, 128], BF)
        use = [None] * 8
        tko = []
        for g in range(NG):
            w = min(16, J - 16 * g)
            h = ohi[:, g, 0:w, :]
            tko.append(V.do(vec.tensor_tensor(h, bc(k.iof[:, 0:NB].unsqueeze(1), [128, w, NB]),
                                              bc(hi[:, 16 * g:16 * g + w].unsqueeze(2), [128, w, NB]), ALU.is_equal)))
        for g in range(NG):
            w = min(16, J - 16 * g)
            bank = g % 2
            for c in range(w):
                t = 16 * g + c
                b = t % 8
                V.wait(use[b])
                tv = V.do(vec.tensor_scalar(olo[:, b, :], k.iob[:, :], lo[:, t:t + 1], None, ALU.is_equal))
                P.wait(tv, tko[g])
                if c == 0:
                    P.wait(k.pst[bank])
                use[b] = mm(k, k.ps[bank][:, c * NB:(c + 1) * NB], olo[:, b, :], ohi[:, g, c, :])
            A.wait(P.now())
            k.pst[bank] = A.do(nc.scalar.copy(hist[:, 16 * g:16 * g + w, :],
                                              k.ps[bank][:, 0:w * NB].rearrange("p (a b) -> p a b", b=NB)))
        V.wait(A.now())
        hv = hist[:, :, :].rearrange("p t b -> p b t")
        V.do(vec.tensor_reduce(cnt[:, :], hv, AX, ALU.add))
        P.wait(V.now(), k.pst[2])
        mm(k, k.ps[2][:, 0:NB], k.ltri[:, :], cnt[:, :])
        mm(k, k.ps[2][:, 32:32 + NB], k.ones[:, :], cnt[:, :])
        V.wait(P.now())
        tot = sb("tot", [128, NB], F)
        toti = sb("toti", [128, NB], I32)
        V.do(vec.tensor_scalar(tot[:, :], k.ps[2][:, 32:32 + NB], 1.0, 127.0, ALU.max, ALU.add))
        V.wait(V.now())
        V.do(vec.tensor_copy(toti[:, :], tot[:, :]))
        V.wait(V.now())
        V.do(vec.tensor_scalar(toti[:, :], toti[:, :], 7, None, ALU.arith_shift_right))
        V.wait(V.now())
        V.do(vec.tensor_copy(tot[:, :], toti[:, :]))
        V.do(vec.memset(st[:, 0:1], 0.0))
        V.wait(V.now())
        V.do(vec.tensor_tensor_scan(st[:, 1:26], k.ones[:, 0:25], tot[:, :], 0.0, ALU.mult, ALU.add))
        V.wait(V.now())
        V.do(vec.scalar_tensor_tensor(out=cum[:, :, 0], in0=st[:, 0:25], scalar=128.0, in1=k.ps[2][:, 0:NB],
                                      op0=ALU.mult, op1=ALU.add))
        V.wait(V.now())
        k.pst[2] = V.now()
        one = sb("one", [128, J], F)
        V.do(vec.memset(one[:, :], 1.0))
        V.wait(V.now())
        for b in range(NB):
            V.do(vec.tensor_tensor_scan(cum[:, b, 1:J + 1], one[:, :], hist[:, :, b], cum[:, b, 0:1],
                                        ALU.mult, ALU.add))
        tcum = V.now()
        NT = (J + 127) // 128
        dT = sb("dT", [128, NT, 128], F)
        P.wait(k.pst[2])
        P.wait(V.now())
        for a in range(NT):
            w = min(128, J - 128 * a)
            P.wait(k.pst[2 + a % 2])
            P.do(nc.tensor.transpose(k.ps[2 + a % 2][0:w, 0:128], pay[:, 128 * a:128 * a + w, 0], k.ident[:, :]))
            A.wait(P.now())
            k.pst[2 + a % 2] = A.do(nc.scalar.copy(dT[0:w, a, :], k.ps[2 + a % 2][0:w, 0:128]))
        tdT = A.now()
        olt = sb("olt", [128, 3, 512], F)
        rank = sb("rank", [128, J], F)
        junk = sb("junk", [128, 4, 128], F)
        prod = sb("prod", [128, 2, 16, NB], F)
        fa = sb("fa", [128, J], F)
        fi = sb("fi", [128, J], I32)
        fj = sb("fj", [128, J], I32)
        fb = sb("fb", [128, J], F)
        use = [None] * 3
        uselt = [None] * 3
        junkt = [None] * 4
        tolt = {}
        ready = {}
        tv = {}
        dest = (2, 3, 6, 7)

        def group(g):
            return range(4 * g, min(4 * g + 4, J))

        def first(g):
            for t in group(g):
                V.wait(use[g % 3])
                tv[g] = V.do(vec.tensor_scalar(olo[:, 4 * (g % 3) + t % 4, :], k.iob[:, :], lo[:, t:t + 1], None,
                                               ALU.is_equal))

        def spread(g):
            rb = dest[g % 4]
            P.wait(tdT, k.pst[rb])
            for t in group(g):
                kk = min(128, J - 128 * (t // 128))
                ready[g] = mm(k, k.ps[rb][:, 128 * (t % 4):128 * (t % 4) + 128],
                              bc(k.ident[0:kk, t % 128:t % 128 + 1], [kk, 128]), dT[0:kk, t // 128, :])
            P.wait(tv.pop(g), k.pst[g % 2])
            for t in group(g):
                use[g % 3] = P.do(nc.tensor.transpose(k.ps[g % 2][:, 64 * (t % 4):64 * (t % 4) + 64].bitcast(BF),
                                                      olo[:, 4 * (g % 3) + t % 4, :], k.identb[:, :]))

        def second(g):
            w = len(group(g))
            A.wait(use[g % 3], uselt[g % 3])
            k.pst[g % 2] = tolt[g] = A.do(nc.scalar.copy(
                olt[:, g % 3, 0:128 * w], k.ps[g % 2][:, 0:64 * w].bitcast(BF)))

        def compare(g):
            V.wait(ready.pop(g))
            for t in group(g):
                V.wait(junkt[t % 4])
                k.pst[dest[g % 4]] = junkt[t % 4] = V.do(vec.scalar_tensor_tensor(
                    out=junk[:, t % 4, :], in0=k.ps[dest[g % 4]][:, 128 * (t % 4):128 * (t % 4) + 128],
                    scalar=pay[:, t, 0:1], in1=k.lmask[:, :],
                    op0=ALU.is_equal, op1=ALU.mult, accum_out=rank[:, t:t + 1]))

        def third(g):
            P.wait(tolt.pop(g), tcum)
            for t in group(g):
                lb = 4 + (t // 16) % 2
                c = t % 16
                if c == 0:
                    P.wait(k.pst[lb])
                uselt[g % 3] = mm(k, k.ps[lb][:, c * NB:(c + 1) * NB], olt[:, g % 3, 128 * (t % 4):128 * (t % 4) + 128],
                                  cum[:, :, t])

        def fourth(g4):
            t = group(g4)[-1]
            if t % 16 != 15 and t != J - 1:
                return
            g = t // 16
            w = t % 16 + 1
            lb = 4 + g % 2
            s = slice(16 * g, 16 * g + w)
            V.wait(uselt[g4 % 3], V.now())
            k.pst[lb] = V.do(vec.tensor_tensor(prod[:, g % 2, 0:w, :],
                                               k.ps[lb][:, 0:w * NB].rearrange("p (a b) -> p a b", b=NB),
                                               ohi[:, g, 0:w, :], ALU.mult))
            V.wait(V.now())
            V.do(vec.tensor_reduce(fa[:, s], prod[:, g % 2, 0:w, :], AX, ALU.add))
            V.wait(V.now())
            V.do(vec.tensor_tensor(fi[:, s], fa[:, s], rank[:, s], ALU.add))
            V.wait(V.now())
            V.do(vec.tensor_scalar(fj[:, s], fi[:, s], 7, None, ALU.arith_shift_right))
            V.do(vec.tensor_scalar(fi[:, s], fi[:, s], 127, None, ALU.bitwise_and))
            V.wait(V.now())
            V.do(vec.scalar_tensor_tensor(out=fb[:, s], in0=fi[:, s], scalar=float(T), in1=fj[:, s],
                                          op0=ALU.mult, op1=ALU.add))
            V.wait(V.now())
            tad = V.do(vec.tensor_tensor(addr[:, s], fb[:, s], inv[:, s], ALU.add))
            if now:
                G.wait(tad)
                send(k, k.ind, e, range(16 * g, 16 * g + w))
        pipeline((J + 3) // 4, (0, first), (1, spread), (2, second), (3, compare), (3, third), (4, fourth))
        fence_but_pool(k)


def send(k, dmas, e, tiles):
    for u in tiles:
        dmas.scatter(e.tab, e.addr[:, u:u + 1], e.pay[:, u, :], 128 * e.T)


def tile_blocks(k, name, T, st, blk, offsets):
    nc, V = k.nc, k.V
    vec = nc.vector
    with ExitStack() as es:
        io = k.tiles
        tmp = es.enter_context(nc.sbuf_tensor(f"tmp_{name}", [128, T], F))
        V.do(vec.memset(blk[:, :], 0.0))
        for b in range(1, 25):
            V.wait(V.now())
            V.do(vec.scalar_tensor_tensor(out=blk[:, :], in0=io[:, 0:T], scalar=st[:, b:b + 1], in1=blk[:, :],
                                          op0=ALU.is_ge, op1=ALU.add))
        for w, o in offsets:
            V.wait(V.now())
            V.do(vec.tensor_scalar(tmp[:, :], blk[:, :], float(w), None, ALU.mult))
            V.wait(V.now())
            V.do(vec.tensor_copy(o[:, :], tmp[0:1, :]))
        fence(k)


def load_int(k, sb, name, J, src, fill):
    nc, V = k.nc, k.V
    t = sb(name, [128, J], I32)
    V.do(nc.vector.memset(t[:, :], fill))
    k.S.wait(V.now())
    E = src.shape[0]
    c = (E + 127) // 128
    full = E // c
    toks = [k.ld.start(t[0:full, 0:c], src[0:full * c].rearrange("(p c) -> p c", c=c))]
    if E > full * c:
        toks.append(k.ld.start(t[full:full + 1, 0:E - full * c],
                               src[full * c:E].rearrange("(a c) -> a c", a=1)))
    return t, toks


def main_loader(k, src, dst, attr, typ):
    nc, V, G = k.nc, k.V, k.G
    vec = nc.vector
    J = 441

    def load(sb, pay):
        d, t1 = load_int(k, sb, "d", J, dst, 4095)
        s, t2 = load_int(k, sb, "s", J, src, 0)
        y, t3 = load_int(k, sb, "y", J, typ, 0)
        at = sb("at", [128, 416, 3], F)
        V.do(vec.memset(at[:, :, :], 0.0))
        k.S.wait(V.now())
        t4 = [k.ld.start(at[0:127, :, :].rearrange("p a b -> p (a b)"),
                         attr[0:127 * 416, :].rearrange("(p c) w -> p (c w)", c=416)),
              k.ld.start(at[127:128, 0:293, :].rearrange("p a b -> p (a b)"),
                         attr[127 * 416:53125, :].rearrange("(p c) w -> p (c w)", p=1))]
        G.wait(t1, t2, V.now())
        lp = [G.do(nc.gpsimd.iota(x[:, 416:441], pattern=[[1, 25]], base=0, channel_multiplier=25)) for x in (d, s)]
        V.wait(lp, t1, t2, t3, t4)
        V.do(vec.tensor_copy(pay[:, :, 0], d[:, :]))
        V.do(vec.tensor_scalar(pay[:, :, 1], s[:, :], float(N - 1), None, ALU.min))
        V.wait(V.now())
        V.do(vec.scalar_tensor_tensor(out=pay[:, :, 2], in0=y[:, :], scalar=3200.0, in1=pay[:, :, 1],
                                      op0=ALU.mult, op1=ALU.add))
        V.do(vec.memset(pay[:, 0:416, 3], 1.0))
        V.do(vec.memset(pay[:, 416:441, 3:8], 0.0))
        V.do(vec.memset(pay[:, 0:416, 7], 0.0))
        V.do(vec.tensor_copy(pay[:, 0:416, 4:7], at[:, :, :]))
        return d

    return load


def second_loader(k, ei):
    nc, V, G = k.nc, k.V, k.G
    vec = nc.vector
    J = 537

    def load(sb, pay):
        d, t1 = load_int(k, sb, "d", J, ei[1, :], 4095)
        s, t2 = load_int(k, sb, "s", J, ei[0, :], 0)
        G.wait(t1, t2, V.now())
        lp = [G.do(nc.gpsimd.iota(z[:, 512:537], pattern=[[1, 25]], base=0, channel_multiplier=25)) for z in (d, s)]
        V.wait(lp, t1, t2)
        V.do(vec.tensor_copy(pay[:, :, 0], d[:, :]))
        V.do(vec.tensor_scalar(pay[:, :, 1], s[:, :], float(N - 1), None, ALU.min))
        return d
    return load


def both_graphs(k, a, x):

    def al(n, shape, dt):
        return k.edges.enter_context(k.nc.sbuf_tensor(n, shape, dt))
    with ExitStack() as es:
        m = EdgeList(k, es, "m", 441, 464, 8)
        n = EdgeList(k, es, "n", 537, 576, 2)
        k.T, k.T2 = m.T, n.T
        k.second = n
        k.deg = m.cnt
        k.blk = al("blk_m", [128, m.T], F)
        k.off256 = al("off_m256", [1, m.T], I32)
        k.off264 = al("off_m264", [1, m.T], I32)
        k.dlA = al("dlA", [128, m.T], F)
        k.dlR = al("dlR", [128, m.T], F)
        k.xsrc = al("xsrc", [128, m.T], U32)
        k.xtyp = al("xtyp", [128, m.T], U32)
        k.attr = al("attr", [128, m.T, 4], F)
        k.loopneg = al("loopneg", [128, m.T], F)
        n.place(x, m.place(x, 0))
        split_digits(k, m, main_loader(k, a['src'], a['dst'], a['edge_attr_3'], a['edge_type_8']))
        split_digits(k, n, second_loader(k, a['L1_ffn_edge_index']))
        sort_edges(k, m, True)
        sort_edges(k, n, False)
        fence(k)
        finish_main(k, m)


def finish_main(k, e):
    nc, V = k.nc, k.V
    vec = nc.vector
    T, tab = e.T, e.tab
    tile_blocks(k, "m", T, e.st, k.blk, ((256, k.off256), (264, k.off264)))
    k.m_flags = edge_flags_dram(k, "m", T)
    with ExitStack() as es:
        p = es.enter_context(nc.sbuf_tensor("sorted_m", [128, T, 8], F))
        V.wait(k.ld.start(p[:, :, :].rearrange("p a b -> p (a b)"), tab.rearrange("(p r) w -> p (r w)", p=128)))
        V.do(vec.tensor_copy(k.xsrc[:, :], p[:, :, 1]))
        V.do(vec.tensor_copy(k.xtyp[:, :], p[:, :, 2]))
        V.do(vec.tensor_copy(k.attr[:, :, 0:3], p[:, :, 4:7]))
        V.do(vec.memset(k.attr[:, :, 3:4], 1.0))
        V.do(vec.scalar_tensor_tensor(out=k.dlA[:, :], in0=k.blk[:, :], scalar=-128.0, in1=p[:, :, 0],
                                      op0=ALU.mult, op1=ALU.add))
        V.do(vec.tensor_scalar(k.loopneg[:, :], p[:, :, 3], 1.0, -NEG, ALU.subtract, ALU.mult))
        V.wait(V.now())
        V.do(vec.tensor_tensor(k.dlR[:, :], k.dlA[:, :], k.loopneg[:, :], ALU.add))
        V.wait(V.now())
        to_rows(k, "mf", p[:, :, 0], T, k.m_flags[128:128 + T * 128])
        fence(k)


def edge_flags_dram(k, name, T):
    nc, V = k.nc, k.V
    d = nc.dram_tensor(f"dsts_{name}", (128 * (T + 2),), F).ap()
    with ExitStack() as es:
        s = es.enter_context(nc.sbuf_tensor(f"sent_{name}", [2, 128], F))
        V.do(nc.vector.memset(s[:, :], -7.0))
        k.S.wait(V.now())
        k.ld.start(d[0:128].rearrange("(a b) -> a b", a=1), s[0:1, :])
        k.ld.start(d[128 * (T + 1):128 * (T + 2)].rearrange("(a b) -> a b", a=1), s[1:2, :])
        fence(k)
    return d


def to_rows(k, name, src, C, dram):
    nc, P, A = k.nc, k.P, k.A
    with ExitStack() as es:
        buf = es.enter_context(nc.sbuf_tensor(f"rows_{name}", [128, 4, 128], F))
        free = [None] * 4
        P.wait(k.V.now())
        for a in range((C + 127) // 128):
            w = min(128, C - 128 * a)
            b = a % 2
            P.wait(k.pst[b])
            P.do(nc.tensor.transpose(k.ps[b][0:w, 0:128], src[:, 128 * a:128 * a + w], k.ident[:, :]))
            A.wait(P.now(), free[a % 4])
            k.pst[b] = A.do(nc.scalar.copy(buf[0:w, a % 4, :], k.ps[b][0:w, 0:128]))
            k.S.wait(A.now())
            free[a % 4] = k.ld.start(dram[128 * 128 * a:128 * (128 * a + w)].rearrange("(q e) -> q e", e=128),
                                     buf[0:w, a % 4, :])
        fence(k)


def from_rows(k, name, dram, C, dst):
    nc, P, A = k.nc, k.P, k.A
    with ExitStack() as es:
        buf = es.enter_context(nc.sbuf_tensor(f"fr_{name}", [128, 4, 128], F))
        free = [None] * 4
        for a in range((C + 127) // 128):
            w = min(128, C - 128 * a)
            b = a % 2
            k.S.wait(free[a % 4])
            t = k.ld.start(buf[0:w, a % 4, :],
                           dram[128 * 128 * a:128 * (128 * a + w)].rearrange("(q e) -> q e", e=128))
            P.wait(t, k.pst[b])
            free[a % 4] = P.do(nc.tensor.transpose(k.ps[b][:, 0:w], buf[0:w, a % 4, :], k.ident[0:w, 0:w]))
            A.wait(P.now())
            k.pst[b] = A.do(nc.scalar.copy(dst[:, 128 * a:128 * a + w], k.ps[b][:, 0:w]))
        fence(k)


def rev(ap):
    return ap[:, ::-1]


def seg_softmax(k, name, L, H, C, T, flags, eps_op, eps):
    nc, V, P, A = k.nc, k.V, k.P, k.A
    vec = nc.vector
    Q = H * C
    r = T // C
    n = r * 128
    dram = nc.dram_tensor(f"soft_{name}", (H * T * 128,), F).ap()
    dram2 = nc.dram_tensor(f"softo_{name}", (H * T * 128,), F).ap()
    to_rows(k, name + "i", L, H * T, dram)
    with ExitStack() as es:
        def sb(nm, shape, dt=F):
            return es.enter_context(nc.sbuf_tensor(f"{name}_{nm}", shape, dt))
        x = sb("x", [128, n])
        d = sb("d", [128, n + 2])
        ks = sb("ks", [128, n], BF)
        ke = sb("ke", [128, n], BF)
        a = sb("a", [128, n])
        b = sb("b", [128, n])
        row = sb("row", [1, 4, 128])
        col = sb("col", [128, 2])
        toks = [k.ld.start(x[0:Q, :], dram.rearrange("(q e) -> q e", q=Q))]
        for h in range(H):
            win = flags[127:127 + C * n].rearrange("(c e) -> c e", c=C)
            toks.append(k.ld.start(d[h * C:(h + 1) * C, 0:n], win))
            win = flags[129:129 + C * n].rearrange("(c e) -> c e", c=C)
            toks.append(k.ld.start(d[h * C:(h + 1) * C, n:n + 2], win[:, n - 2:n]))
        V.wait(toks)
        V.do(vec.tensor_tensor(ks[0:Q, :], d[0:Q, 1:n + 1], d[0:Q, 0:n], ALU.not_equal))
        V.do(vec.tensor_tensor(ke[0:Q, :], d[0:Q, 1:n + 1], d[0:Q, 2:n + 2], ALU.not_equal))
        V.wait(V.now())
        V.do(vec.tensor_reduce(col[0:Q, 0:1], ks[0:Q, :], AX, ALU.max))
        V.do(vec.tensor_reduce(col[0:Q, 1:2], ke[0:Q, :], AX, ALU.max))
        V.wait(V.now())
        anys = sb("anys", [1, 2, 128])
        cc = sb("cc", [128, 4])
        for i in range(2):
            P.wait(V.now(), k.pst[0])
            P.do(nc.tensor.transpose(k.ps[0][0:1, 128 * i:128 * i + Q], col[0:Q, i:i + 1], k.ident[0:Q, 0:Q]))
        V.wait(P.now())
        V.do(vec.tensor_copy(anys[0:1, :, 0:Q], k.ps[0][0:1, 0:256].rearrange("p (a b) -> p a b", a=2)[:, :, 0:Q]))
        V.wait(V.now())
        k.pst[0] = V.now()

        def scans(out, gate, inp, back, op_gate, op_in, init, any_row):
            o, g, i_ = out[0:Q, 0:n], gate[0:Q, 0:n], inp[0:Q, 0:n]
            if back:
                o, g, i_ = rev(o), rev(g), rev(i_)
            V.wait(V.now())
            V.do(vec.tensor_tensor_scan(o, g, i_, init, op_gate, op_in))
            V.wait(V.now())
            last = out[0:Q, 0:1] if back else out[0:Q, n - 1:n]
            P.wait(V.now(), k.pst[0])
            P.do(nc.tensor.transpose(k.ps[0][0:1, 0:Q], last, k.ident[0:Q, 0:Q]))
            V.wait(P.now())
            v = row[0:1, 0, 0:Q]
            V.do(vec.tensor_copy(v, k.ps[0][0:1, 0:Q]))
            gt = row[0:1, 1, 0:Q]
            if op_gate == ALU.add:
                V.do(vec.tensor_scalar(gt, any_row, NEG, None, ALU.mult))
            else:
                V.do(vec.tensor_scalar(gt, any_row, -1.0, 1.0, ALU.mult, ALU.add))
            V.wait(V.now())
            res = row[0:1, 2, 0:Q]
            V.do(vec.memset(res, init))
            V.wait(V.now())
            for h in range(H):
                s = slice(h * C, (h + 1) * C)
                vo, vg, vi = row[0:1, 3, s], row[0:1, 1, s], row[0:1, 0, s]
                if back:
                    vo, vg, vi = rev(vo), rev(vg), rev(vi)
                V.do(vec.tensor_tensor_scan(vo, vg, vi, init, op_gate, op_in))
            V.wait(V.now())
            for h in range(H):
                if back:
                    V.do(vec.tensor_copy(row[0:1, 2, h * C:(h + 1) * C - 1], row[0:1, 3, h * C + 1:(h + 1) * C]))
                else:
                    V.do(vec.tensor_copy(row[0:1, 2, h * C + 1:(h + 1) * C], row[0:1, 3, h * C:(h + 1) * C - 1]))
            P.wait(V.now())
            P.do(nc.tensor.transpose(k.ps[0][0:Q, 0:1], res, k.ident[0:1, 0:1]))
            V.wait(P.now(), V.now())
            V.do(vec.tensor_copy(cc[0:Q, 0:1], k.ps[0][0:Q, 0:1]))
            k.pst[0] = V.now()
            V.wait(V.now())
            V.do(vec.tensor_tensor_scan(o, g, i_, cc[0:Q, 0:1], op_gate, op_in))
            V.wait(V.now())

        aS, aE = anys[0:1, 0, 0:Q], anys[0:1, 1, 0:Q]
        V.do(vec.tensor_scalar(b[0:Q, :], ks[0:Q, :], NEG, None, ALU.mult))
        scans(a, b, x, False, ALU.add, ALU.max, NEG, aS)
        V.do(vec.tensor_scalar(b[0:Q, :], ke[0:Q, :], NEG, None, ALU.mult))
        V.wait(V.now())
        g2 = d
        scans(g2, b, a, True, ALU.add, ALU.max, NEG, aE)
        V.do(vec.tensor_tensor(x[0:Q, :], x[0:Q, :], g2[0:Q, 0:n], ALU.subtract))
        A.wait(V.now())
        V.wait(A.do(nc.scalar.activation(x[0:Q, :], x[0:Q, :], ACT.Exp)))
        V.do(vec.tensor_scalar(b[0:Q, :], ks[0:Q, :], -1.0, 1.0, ALU.mult, ALU.add))
        scans(a, b, x, False, ALU.mult, ALU.add, 0.0, aS)
        V.do(vec.tensor_tensor(a[0:Q, :], a[0:Q, :], ke[0:Q, :], ALU.mult))
        V.do(vec.tensor_scalar(b[0:Q, :], ke[0:Q, :], -1.0, 1.0, ALU.mult, ALU.add))
        scans(g2, b, a, True, ALU.mult, ALU.add, 0.0, aE)
        if eps_op is not None:
            V.do(vec.tensor_scalar(g2[0:Q, 0:n], g2[0:Q, 0:n], eps, None, eps_op))
            V.wait(V.now())
        V.do(vec.reciprocal(g2[0:Q, 0:n], g2[0:Q, 0:n]))
        V.wait(V.now())
        V.do(vec.tensor_tensor(x[0:Q, :], x[0:Q, :], g2[0:Q, 0:n], ALU.mult))
        k.S.wait(V.now())
        k.ld.start(dram2.rearrange("(q e) -> q e", q=Q), x[0:Q, :])
        fence(k)
    from_rows(k, name + "o", dram2, H * T, L)


def rows_of(ap):
    return ap[:].rearrange("(a c) -> a c", a=1)


def layernorm(k, x, out):
    nc, V, A = k.nc, k.V, k.A
    vec = nc.vector
    x3 = x.rearrange("p (b c) -> p b c", b=NB)
    o3 = out.rearrange("p (b c) -> p b c", b=NB)
    with ExitStack() as es:
        mu = es.enter_context(nc.sbuf_tensor(k.nm("mu"), [128, NB], F))
        va = es.enter_context(nc.sbuf_tensor(k.nm("va"), [128, NB], F))
        junk = es.enter_context(nc.sbuf_tensor(k.nm("junk"), [128, 2, D], F))
        V.do(vec.tensor_reduce(mu[:, :], x3, AX, ALU.add))
        V.wait(V.now())
        V.do(vec.tensor_scalar(mu[:, :], mu[:, :], 1.0 / D, None, ALU.mult))
        V.wait(V.now())
        for b in range(NB):
            t = V.do(vec.tensor_scalar(o3[:, b, :], x3[:, b, :], mu[:, b:b + 1], None, ALU.subtract))
            A.wait(t)
            A.wait(A.now())
            A.do(nc.scalar.activation(junk[:, b % 2, :], o3[:, b, :], ACT.Square, accum_out=va[:, b:b + 1]))
        V.wait(A.now())
        V.do(vec.tensor_scalar(va[:, :], va[:, :], 1.0 / D, 1e-5, ALU.mult, ALU.add))
        A.wait(V.now())
        A.do(nc.scalar.activation(va[:, :], va[:, :], ACT.Sqrt))
        V.wait(A.now())
        V.do(vec.reciprocal(va[:, :], va[:, :]))
        V.wait(V.now())
        for b in range(NB):
            V.do(vec.tensor_scalar(o3[:, b, :], o3[:, b, :], va[:, b:b + 1], None, ALU.mult))
        fence(k)


def transpose_rows(k, x, xT, banks=(0, 1)):
    nc, P, A, V = k.nc, k.P, k.A, k.V
    P.wait(V.now(), A.now())
    i = 0
    for c in range(2):
        for b0 in range(0, NB, 4):
            w = min(4, NB - b0)
            bk = banks[i % len(banks)]
            P.wait(k.pst[bk])
            for j in range(w):
                b = b0 + j
                P.do(nc.tensor.transpose(k.ps[bk][:, 128 * j:128 * (j + 1)],
                                         x[:, b * D + c * 128:b * D + c * 128 + 128], k.ident[:, :]))
            E, f = (A, nc.scalar.copy) if i % 2 else (V, nc.vector.tensor_copy)
            E.wait(P.now())
            k.pst[bk] = E.do(f(xT[:, c, 128 * b0:128 * (b0 + w)], k.ps[bk][:, 0:128 * w]))
            i += 1
    P.wait(A.now(), V.now())


def load_w(k, dst, src):
    for c in range(2):
        k.ld.start(dst[:, c, :], src[128 * c:128 * (c + 1), :])
    return k.ld.all()


def project(k, xT, w, M, sink, banks=(2, 3, 4, 5)):
    i = 0
    for b in range(NB):
        for m0 in range(0, M, 512):
            mw = min(512, M - m0)
            bk = banks[i % len(banks)]
            i += 1
            k.P.wait(k.pst[bk])
            for c in range(2):
                mm(k, k.ps[bk][:, 0:mw], xT[:, c, 128 * b:128 * (b + 1)], w[:, c, m0:m0 + mw],
                   start=(c == 0), stop=(c == 1))
            k.pst[bk] = sink(b, m0, mw, k.ps[bk][:, 0:mw])


def copy_sink(k, dst, M):
    n = [0]

    def sink(b, m0, mw, ps):
        E, f = (k.A, k.nc.scalar.copy) if n[0] % 2 else (k.V, k.nc.vector.tensor_copy)
        n[0] += 1
        E.wait(k.P.now())
        return E.do(f(dst[:, b * M + m0:b * M + m0 + mw], ps))
    return sink


def dram_sink(k, es, dram, M):
    buf = es.enter_context(k.nc.sbuf_tensor(k.nm("tb"), [128, 6, 512], F))
    free = [None] * 6
    n = [0]

    def sink(b, m0, mw, ps):
        i = n[0] % 6
        E, f = (k.A, k.nc.scalar.copy) if n[0] % 2 else (k.V, k.nc.vector.tensor_copy)
        n[0] += 1
        E.wait(k.P.now(), free[i])
        t = E.do(f(buf[:, i, 0:mw], ps))
        k.S.wait(t)
        free[i] = []
        for j in range(0, mw, D):
            r = 3200 * ((m0 + j) // D) + 128 * b
            free[i].append(k.ld.start(dram[r:r + 128, :], buf[:, i, j:j + min(D, mw)]))
        return t
    return sink


def bcast_row(k, es, vecap, M):
    t = es.enter_context(k.nc.sbuf_tensor(k.nm("bc"), [128, M], F))
    k.ld.start(t[:, :], vecap.partition_broadcast(128))
    return t


def onehot(k, buf, dl, t, weight=None):
    if weight is None:
        return k.V.do(k.nc.vector.tensor_scalar(buf, k.iof[:, :], dl[:, t:t + 1], None, ALU.is_equal))
    return k.V.do(k.nc.vector.tensor_scalar(buf, k.iof[:, :], dl[:, t:t + 1], weight, ALU.is_equal, ALU.mult))


def seg_sum(k, T, table, rows, idx, dl, offs, acc, Rw=D, alpha=None, H=1):
    nc, V, P, G = k.nc, k.V, k.P, k.G
    vec = nc.vector
    R = 16
    with ExitStack() as es:
        g = es.enter_context(nc.sbuf_tensor(k.nm("g"), [128, R, Rw], F))
        oh = es.enter_context(nc.sbuf_tensor(k.nm("oh"), [128, 6, 128], F))
        V.do(vec.memset(acc[:, :], 0.0))
        freeg = [None] * R
        freeo = [None] * 6
        tg, to, tp = {}, {}, {}
        off = Offsets(k, mybir.EngineType.DVE, offs, 24 * D)
        if alpha is not None:
            av = alpha.rearrange("p (h t) -> p h t", h=H)

        def fetch(t):
            G.wait(freeg[t % R])
            tg[t] = k.ind.gather(g[:, t % R, :], table, idx[:, t:t + 1], rows)

        def mark(t):
            V.wait(freeo[t % 6])
            w = alpha[:, t:t + 1] if alpha is not None and H == 1 else None
            to[t] = onehot(k, oh[:, t % 6, :], dl, t, w)

        def weigh(t):
            V.wait(tg[t])
            gv = g[:, t % R, 0:D].rearrange("p (h c) -> p h c", h=H)
            tg[t] = V.do(vec.tensor_tensor(gv, gv, bc(av[:, :, t:t + 1], [128, H, D // H]), ALU.mult))

        def product(t):
            P.wait(to.pop(t), tg.pop(t), k.pst[t % 6])
            tp[t] = freeg[t % R] = freeo[t % 6] = mm(k, k.ps[t % 6][:, 0:D], oh[:, t % 6, :], g[:, t % R, 0:D])

        def add(t):
            d = acc[:, bass.ds(off(t), D)]
            V.wait(tp.pop(t), V.now())
            k.pst[t % 6] = V.do(vec.tensor_tensor(d, d, k.ps[t % 6][:, 0:D], ALU.add))
        steps = [(0, fetch), (0, mark), (1, product), (4, add)]
        if H > 1:
            steps.insert(2, (0, weigh))
        pipeline(T, *steps)
        fence(k)


class DstRows:

    def __init__(self, k, es, dl, offs, src, width, used):
        nc = k.nc
        self.k, self.dl, self.src, self.width, self.used = k, dl, src, width, used
        self.off = Offsets(k, mybir.EngineType.PE, offs, 24 * width)
        self.oh = es.enter_context(nc.sbuf_tensor(k.nm("oh"), [128, 8, 128], F))
        self.ot = es.enter_context(nc.sbuf_tensor(k.nm("ot"), [128, 3, 512], F))
        self.fo = [None] * 2
        self.ft = [None] * 3
        self.tt = [None] * 3

    def mark(self, t):
        if t % 4:
            return
        k, nc, g = self.k, self.k.nc, t // 4
        b = g % 2
        for u in range(4):
            k.V.wait(self.fo[b])
            to = onehot(k, self.oh[:, 4 * b + u, :], self.dl, t + u)
        k.P.wait(to, k.pst[b])
        for u in range(4):
            self.fo[b] = k.P.do(nc.tensor.transpose(k.ps[b][:, 128 * u:128 * u + 128], self.oh[:, 4 * b + u, :],
                                                    k.ident[:, :]))

    def turn(self, t):
        if t % 4:
            return
        k, nc, g = self.k, self.k.nc, t // 4
        k.A.wait(self.fo[g % 2], self.ft[g % 3])
        k.pst[g % 2] = self.tt[g % 3] = k.A.do(nc.scalar.copy(self.ot[:, g % 3, :], k.ps[g % 2][:, :]))

    def spread(self, t, out, stop=True):
        k, i = self.k, (t // 4) % 3
        r = self.src[:, bass.ds(self.off(t), self.used)]
        k.P.wait(self.tt[i])
        self.ft[i] = mm(k, out, self.ot[:, i, 128 * (t % 4):128 * (t % 4) + 128], r, stop=stop)
        return self.ft[i]


def gatv2_logits(k, T, table, xr, att8, H, L):
    nc, V, P, G, A = k.nc, k.V, k.P, k.G, k.A
    vec = nc.vector
    R = 12
    W = D + H
    with ExitStack() as es:
        def sb(n, shape, dt=F):
            return es.enter_context(nc.sbuf_tensor(k.nm(n), shape, dt))
        g = sb("g", [128, R, W])
        r = sb("r", [128, 6, D])
        lin = sb("lin", [128, T, H])
        rows = DstRows(k, es, k.dlA, k.off264, xr, 264, W)
        free = [None] * R
        rfree = [None] * 6
        tg, tm, tr, tx = {}, {}, {}, {}
        Lv = L.rearrange("p (h t) -> p h t", h=H)

        def fetch(t):
            G.wait(free[t % R])
            tg[t] = k.ind.gather(g[:, t % R, :], table, k.xsrc[:, t:t + 1], 3200)

        def join(t):
            bk = 2 + t % 6
            P.wait(k.pst[bk])
            rows.spread(t, k.ps[bk][:, 0:W], stop=False)
            P.wait(tg.pop(t))
            tm[t] = free[t % R] = mm(k, k.ps[bk][:, 0:W], k.ident[:, :], g[:, t % R, :], start=False)

        def relu(t):
            bk = 2 + t % 6
            A.wait(tm.pop(t), rfree[t % 6])
            tr[t] = A.do(nc.scalar.activation(r[:, t % 6, :], k.ps[bk][:, 0:D], ACT.Relu))
            k.pst[bk] = A.do(nc.scalar.copy(lin[:, t, :], k.ps[bk][:, D:W]))

        def weigh(t):
            V.wait(tr.pop(t))
            x = r[:, t % 6, :]
            if H == 1:
                rfree[t % 6] = V.do(vec.tensor_tensor_reduce(x, x, att8[:, :], 1.0, 0.0, ALU.mult, ALU.add,
                                                             L[:, t:t + 1]))
            else:
                tx[t] = V.do(vec.tensor_tensor(x, x, att8[:, :], ALU.mult))

        def total(t):
            V.wait(tx.pop(t))
            rfree[t % 6] = V.do(vec.tensor_reduce(Lv[:, :, t], r[:, t % 6, :].rearrange("p (h c) -> p h c", h=H),
                                                  AX, ALU.add))
        steps = [(0, fetch), (0, rows.mark), (2, rows.turn), (5, join), (6, relu), (8, weigh)]
        if H > 1:
            steps.append((9, total))
        pipeline(T, *steps)
        V.wait(A.now(), V.now())
        V.do(vec.tensor_tensor(Lv, Lv, lin[:, :, :].rearrange("p t h -> p h t"), ALU.add))
        fence(k)


def gat_layer(k, name, xT, Wl, Wr, att, H, acc):
    nc = k.nc
    T = k.T
    V, A, P = k.V, k.A, k.P
    vec = nc.vector
    W = D + H
    table = nc.dram_tensor("xl_" + name, (3200, W), F).ap()
    with ExitStack() as es:
        def sb(n, shape, dt=F):
            return es.enter_context(nc.sbuf_tensor(k.nm(n), shape, dt))
        L = sb("L", [128, H * T])
        with ExitStack() as e2:
            def s2(n, shape, dt=F):
                return e2.enter_context(nc.sbuf_tensor(k.nm(n), shape, dt))
            xr = s2("xr", [128, NB * 264])
            att8 = bcast_row(k, e2, att, D)
            with ExitStack() as e3:
                wl = e3.enter_context(nc.sbuf_tensor(k.nm("wl"), [128, 2, D], F))
                wr = e3.enter_context(nc.sbuf_tensor(k.nm("wr"), [128, 2, D], F))
                att2 = e3.enter_context(nc.sbuf_tensor(k.nm("att2"), [128, D], F))
                buf = e3.enter_context(nc.sbuf_tensor(k.nm("buf"), [128, 6, W], F))
                tmp = e3.enter_context(nc.sbuf_tensor(k.nm("tmp"), [128, 4, D], F))
                load_w(k, wl, Wl)
                P.wait(load_w(k, wr, Wr))
                V.wait(k.ld.all())
                V.do(vec.tensor_scalar(att2[:, :], att8[:, :], 0.2, None, ALU.mult))
                V.wait(V.now())
                V.do(vec.tensor_scalar(att8[:, :], att8[:, :], 0.8, None, ALU.mult))
                n = [0]
                tfree = [None] * 4

                def widen(dst, ps):
                    i = n[0] % 4
                    n[0] += 1
                    A.wait(P.now())
                    t = A.do(nc.scalar.copy(dst[:, 0:D], ps))
                    V.wait(t)
                    V.do(vec.tensor_tensor(tmp[:, i, :], dst[:, 0:D], att2[:, :], ALU.mult))
                    V.wait(V.now())
                    V.do(vec.tensor_reduce(dst[:, D:W], tmp[:, i, :].rearrange("p (h c) -> p h c", h=H), AX, ALU.add))
                    return t
                free = [None] * 6

                def table_sink(b, m0, mw, ps):
                    A.wait(free[b % 6])
                    t = widen(buf[:, b % 6, :], ps)
                    k.S.wait(t, V.now())
                    free[b % 6] = k.ld.start(table[128 * b:128 * (b + 1), :], buf[:, b % 6, :])
                    return t

                def xr_sink(b, m0, mw, ps):
                    return widen(xr[:, 264 * b:264 * b + W], ps)
                project(k, xT, wl, D, table_sink)
                project(k, xT, wr, D, xr_sink)
                fence(k)
            gatv2_logits(k, T, table, xr, att8, H, L[:, :])
        seg_softmax(k, name, L[:, :], H, 29 if H == 4 else 116, T, k.m_flags, None, 0)
        seg_sum(k, T, table, 3200, k.xsrc, k.dlA, k.off256, acc, Rw=W, alpha=L[:, :], H=H)


def add_bias(k, acc, bias_ap):
    with ExitStack() as es:
        b = bcast_row(k, es, bias_ap, D)
        k.V.wait(k.ld.all(), k.V.now())
        a3 = acc.rearrange("p (b c) -> p b c", b=NB)
        k.V.do(k.nc.vector.tensor_tensor(a3, a3, bc(b[:, :].unsqueeze(1), [128, NB, D]), ALU.add))
        fence(k)


def stage_l0_gnn(k, x, a):
    nc, V, A = k.nc, k.V, k.A
    vec = nc.vector
    with ExitStack() as es:
        def sb(n, shape, dt=F):
            return es.enter_context(nc.sbuf_tensor(k.nm(n), shape, dt))
        h = sb("h", [128, NB * D])
        xT = sb("xT", [128, 2, 3200])
        layernorm(k, x, h[:, :])
        transpose_rows(k, h, xT)
        fence(k)
        gat_layer(k, "g1", xT, a['L0_gnn_Wl1'], a['L0_gnn_Wr1'],
                  a['L0_gnn_att1'].rearrange("h c -> (h c)"), 4, h)
        add_bias(k, h[:, :], a['L0_gnn_b1'])
        with ExitStack() as e2:
            t = e2.enter_context(nc.sbuf_tensor(k.nm("t"), [128, NB * D], F))
            V.do(vec.tensor_scalar(t[:, :], h[:, :], 0.0, None, ALU.min))
            A.wait(V.now())
            A.do(nc.scalar.activation(t[:, :], t[:, :], ACT.Exp))
            V.wait(A.now())
            V.do(vec.tensor_scalar(t[:, :], t[:, :], -1.0, None, ALU.add))
            V.wait(V.now())
            V.do(vec.scalar_tensor_tensor(out=h[:, :], in0=h[:, :], scalar=0.0, in1=t[:, :],
                                          op0=ALU.max, op1=ALU.add))
            fence(k)
        transpose_rows(k, h, xT)
        fence(k)
        gat_layer(k, "g2", xT, a['L0_gnn_Wl2'], a['L0_gnn_Wr2'],
                  a['L0_gnn_att2'].rearrange("h c -> (h c)"), 1, h)
        add_bias(k, h[:, :], a['L0_gnn_b2'])
        V.do(vec.tensor_tensor(x, x, h[:, :], ALU.add))
        fence(k)


def stage_l0_ffn(k, x, a):
    nc, V, A, P = k.nc, k.V, k.A, k.P
    vec = nc.vector
    send(k, k.late, k.second, range(k.second.J))
    with ExitStack() as es:
        def sb(n, shape, dt=F):
            return es.enter_context(nc.sbuf_tensor(k.nm(n), shape, dt))
        sw = sb("sw", [128, NB, 512])
        Pm = sb("Pm", [128, 4, D])
        with ExitStack() as e2:
            def s2(n, shape, dt=F):
                return e2.enter_context(nc.sbuf_tensor(k.nm(n), shape, dt))
            xT = s2("xT", [128, 2, 3200])
            with ExitStack() as e3:
                xn = e3.enter_context(nc.sbuf_tensor(k.nm("xn"), [128, NB * D], F))
                layernorm(k, x, xn[:, :])
                transpose_rows(k, xn, xT)
                fence(k)
            wfx = s2("wfx", [128, 2, 512])
            wx = s2("wx", [128, 2, 512])
            load_w(k, wfx, a['L0_ffn_W_fx'])
            load_w(k, wx, a['L0_ffn_W_x'])
            bfx = bcast_row(k, e2, a['L0_ffn_b_fx'], 512)
            bxc = s2("bxc", [128, 4])
            k.ld.start(bxc[:, :], a['L0_ffn_b_x'].rearrange("(c p) -> p c", p=128), small=True)
            ws = s2("ws", [128, 128])
            V.do(vec.memset(ws[:, :], 0.0))
            k.S.wait(V.now())
            k.ld.start(ws[0:64, 0:64], a['L0_ffn_W_slice'])
            k.ld.start(ws[64:128, 64:128], a['L0_ffn_W_slice'])
            bs = bcast_row(k, e2, a['L0_ffn_b_slice'], 64)
            tp = bcast_row(k, e2, a['L0_ffn_temperature'].rearrange("a h b c -> (a h b c)"), 8)
            V.wait(k.ld.all())
            P.wait(k.ld.all())
            A.wait(k.ld.all())
            V.do(vec.tensor_scalar(tp[:, :], tp[:, :], 0.1, 5.0, ALU.max, ALU.min))
            V.wait(V.now())
            V.do(vec.reciprocal(tp[:, :], tp[:, :]))
            xm = s2("xm", [128, 2, 4, 512])
            fx = s2("fx", [128, 2, 8, 65])
            V.do(vec.memset(fx[:, :, :, :], 1.0))
            mx = s2("mx", [128, 2, 8])
            V.wait(V.now())
            pst = k.pst
            tok8 = [k.ps[6][0:64, :], k.ps[7][0:64, :]]
            fxfree = [None, None]
            for ch in range(7):
                t0, tw = 512 * ch, min(512, 3200 - 512 * ch)
                xb = ch % 2
                for i in range(4):
                    bk = i % 2
                    P.wait(pst[bk])
                    for c in range(2):
                        mm(k, k.ps[bk][:, 0:tw], wx[:, c, 128 * i:128 * (i + 1)], xT[:, c, t0:t0 + tw],
                           start=(c == 0), stop=(c == 1))
                    A.wait(P.now())
                    pst[bk] = A.do(nc.scalar.activation(xm[:, xb, i, 0:tw], k.ps[bk][:, 0:tw], ACT.Identity,
                                                        bias=bxc[:, i:i + 1]))
                txm = A.now()
                for j in range(tw // 128):
                    b = 4 * ch + j
                    bk = 2 + b % 2
                    P.wait(txm, pst[bk])
                    for i in range(4):
                        mm(k, k.ps[bk][:, 128 * i:128 * (i + 1)], xm[:, xb, i, 128 * j:128 * (j + 1)], ws[:, :])
                    w3 = sw[:, b, :].rearrange("p (h g) -> p h g", h=8)
                    V.wait(P.now())
                    pst[bk] = V.do(vec.tensor_tensor(w3, k.ps[bk][:, :].rearrange("p (h g) -> p h g", h=8),
                                                     bc(bs[:, :].unsqueeze(1), [128, 8, 64]), ALU.add))
                    m = mx[:, b % 2, :]

                    def step(ins):
                        V.do(ins)
                        V.wait(V.now())
                    V.wait(V.now())
                    step(vec.tensor_tensor(w3, w3, bc(tp[:, :].unsqueeze(2), [128, 8, 64]), ALU.mult))
                    step(vec.tensor_reduce(m, w3, AX, ALU.max))
                    step(vec.tensor_tensor(w3, w3, bc(m.unsqueeze(2), [128, 8, 64]), ALU.subtract))
                    A.wait(V.now())
                    A.do(nc.scalar.activation(sw[:, b, :], sw[:, b, :], ACT.Exp))
                    fk = 4 + b % 2
                    P.wait(pst[fk])
                    for c in range(2):
                        mm(k, k.ps[fk][:, :], xT[:, c, 128 * b:128 * (b + 1)], wfx[:, c, :],
                           start=(c == 0), stop=(c == 1))
                    V.wait(P.now(), fxfree[b % 2])
                    pst[fk] = V.do(vec.tensor_tensor(fx[:, b % 2, :, 0:64],
                                                     k.ps[fk][:, :].rearrange("p (h g) -> p h g", h=8),
                                                     bfx[:, :].rearrange("p (h g) -> p h g", h=8), ALU.add))
                    V.wait(A.now())
                    step(vec.tensor_reduce(m, w3, AX, ALU.add))
                    step(vec.reciprocal(m, m))
                    step(vec.tensor_tensor(w3, w3, bc(m.unsqueeze(2), [128, 8, 64]), ALU.mult))
                    P.wait(V.now())
                    kp = 128 if b < 24 else LASTP
                    for h in range(8):
                        fxfree[b % 2] = mm(k, tok8[h // 4][:, 65 * (h % 4):65 * (h % 4) + 65],
                                           sw[0:kp, b, 64 * h:64 * h + 64], fx[0:kp, b % 2, h, :],
                                           start=(b == 0 and h % 4 == 0), stop=(b == 24))
            fence(k)
            wq = s2("wq", [64, 64])
            wk = s2("wk", [64, 64])
            wv = s2("wv", [64, 64])
            wo = s2("wo", [64, 8, D])
            for t, n in ((wq, 'q'), (wk, 'k'), (wv, 'v')):
                k.ld.start(t[:, :], a['L0_ffn_W_' + n])
            k.ld.start(wo[:, :, :], a['L0_ffn_W_out'].rearrange("(h c) n -> c h n", c=64))
            P.wait(k.ld.all())
            st = s2("st", [64, 8, 65])
            nr = s2("nr", [64, 8])
            stT = s2("stT", [64, 8, 64])
            qT = s2("qT", [64, 8, 64])
            kT = s2("kT", [64, 8, 64])
            vv = s2("vv", [64, 8, 64])
            at = s2("at", [64, 8, 64])
            atT = s2("atT", [64, 8, 64])
            oT = s2("oT", [64, 8, 64])
            am = s2("am", [64, 8])

            def vs(op, *args, **kw):
                V.wait(V.now())
                V.do(op(*args, **kw))
                V.wait(V.now())
            for i in range(2):
                vs(vec.tensor_copy, st[:, 4 * i:4 * i + 4, :],
                                   tok8[i][:, 0:260].rearrange("p (h c) -> p h c", h=4))
            vs(vec.tensor_scalar, nr[:, :], st[:, :, 64], 1e-5, None, ALU.add)
            vs(vec.reciprocal, nr[:, :], nr[:, :])
            vs(vec.tensor_tensor, st[:, :, 0:64], st[:, :, 0:64], bc(nr[:, :].unsqueeze(2), [64, 8, 64]), ALU.mult)

            def heads(fn, dst, bank):
                P.wait(V.now(), A.now())
                for h in range(8):
                    fn(h, k.ps[bank][0:64, 64 * h:64 * h + 64])
                vs_wait = P.now()
                V.wait(vs_wait)
                vs(vec.tensor_copy, dst[:, :, :], k.ps[bank][0:64, :].rearrange("p (h c) -> p h c", h=8))
            i64 = k.ident[0:64, 0:64]
            heads(lambda h, o: P.do(nc.tensor.transpose(o, st[:, h, 0:64], i64)), stT, 0)
            heads(lambda h, o: mm(k, o, wq[:, :], stT[:, h, :]), qT, 1)
            heads(lambda h, o: mm(k, o, wk[:, :], stT[:, h, :]), kT, 2)
            heads(lambda h, o: mm(k, o, stT[:, h, :], wv[:, :]), vv, 3)
            heads(lambda h, o: mm(k, o, qT[:, h, :], kT[:, h, :]), at, 4)
            vs(vec.tensor_scalar, at[:, :, :], at[:, :, :], 0.125, None, ALU.mult)
            vs(vec.tensor_reduce, am[:, :], at[:, :, :], AX, ALU.max)
            vs(vec.tensor_tensor, at[:, :, :], at[:, :, :], bc(am[:, :].unsqueeze(2), [64, 8, 64]), ALU.subtract)
            A.wait(V.now())
            A.do(nc.scalar.activation(at[:, :, :], at[:, :, :], ACT.Exp))
            V.wait(A.now())
            vs(vec.tensor_reduce, am[:, :], at[:, :, :], AX, ALU.add)
            vs(vec.reciprocal, am[:, :], am[:, :])
            vs(vec.tensor_tensor, at[:, :, :], at[:, :, :], bc(am[:, :].unsqueeze(2), [64, 8, 64]), ALU.mult)
            heads(lambda h, o: P.do(nc.tensor.transpose(o, at[:, h, :], i64)), atT, 0)
            heads(lambda h, o: mm(k, o, vv[:, h, :], atT[:, h, :]), oT, 1)
            P.wait(V.now())
            pp = s2("pp", [64, 8, D])
            for h in range(8):
                bk = h % 2
                P.wait(k.pst[bk])
                mm(k, k.ps[bk][0:64, 0:D], oT[:, h, :], wo[:, h, :])
                V.wait(P.now())
                k.pst[bk] = V.do(vec.tensor_copy(pp[:, h, :], k.ps[bk][0:64, 0:D]))
            k.S.wait(V.now())
            for h in range(8):
                k.ld.start(Pm[64 * (h % 2):64 * (h % 2) + 64, h // 2, :], pp[:, h, :])
            fence(k)
        bo = bcast_row(k, es, a['L0_ffn_b_out'], D)
        V.wait(k.ld.all())
        wT = sb("wT", [128, 2, 4, 128])
        x3 = x.rearrange("p (b c) -> p b c", b=NB)
        for b in range(NB):
            bk = b % 2
            P.wait(k.pst[bk])
            for i in range(4):
                P.do(nc.tensor.transpose(k.ps[bk][:, 128 * i:128 * (i + 1)], sw[:, b, 128 * i:128 * (i + 1)],
                                         k.ident[:, :]))
            A.wait(P.now())
            k.pst[bk] = A.do(nc.scalar.copy(wT[:, bk, :, :].rearrange("p a b -> p (a b)"), k.ps[bk][:, :]))
            P.wait(A.now(), k.pst[2 + bk])
            for i in range(4):
                mm(k, k.ps[2 + bk][:, 0:D], wT[:, bk, i, :], Pm[:, i, :], start=(i == 0), stop=(i == 3))
            V.wait(P.now())
            k.pst[2 + bk] = V.do(vec.tensor_tensor(x3[:, b, :], x3[:, b, :], k.ps[2 + bk][:, 0:D], ALU.add))
            V.wait(V.now())
            V.do(vec.tensor_tensor(x3[:, b, :], x3[:, b, :], bo[:, :], ALU.add))
            A.wait(P.now())
        fence(k)


def stage_l1_gnn(k, x, a):
    nc, V, A, P = k.nc, k.V, k.A, k.P
    vec = nc.vector
    s = float(np.sqrt(np.float32(0.5)))
    table = nc.dram_tensor("hx_rel", (8 * 3200, D), F).ap()
    with ExitStack() as es:
        def sb(n, shape, dt=F):
            return es.enter_context(nc.sbuf_tensor(k.nm(n), shape, dt))
        h = sb("h", [128, NB * D])
        with ExitStack() as e2:
            xT = e2.enter_context(nc.sbuf_tensor(k.nm("xT"), [128, 2, 3200], F))
            layernorm(k, x, h[:, :])
            transpose_rows(k, h, xT)
            fence(k)
            w = e2.enter_context(nc.sbuf_tensor(k.nm("w"), [128, 2, 2048], F))
            wl = e2.enter_context(nc.sbuf_tensor(k.nm("wl"), [128, 2, D], F))
            for r in range(8):
                for c in range(2):
                    k.ld.start(w[:, c, D * r:D * (r + 1)], a['L1_gnn_weight'][r, 128 * c:128 * (c + 1), :])
            P.wait(load_w(k, wl, a['L1_gnn_loop_weight']))
            project(k, xT, w, 2048, dram_sink(k, e2, table, D))
            x3 = x.rearrange("p (b c) -> p b c", b=NB)

            def sink(b, m0, mw, ps):
                V.wait(P.now())
                return V.do(vec.scalar_tensor_tensor(out=x3[:, b, :], in0=ps, scalar=s, in1=x3[:, b, :],
                                                     op0=ALU.mult, op1=ALU.add))
            project(k, xT, wl, D, sink)
            fence(k)
        seg_sum(k, k.T, table, 8 * 3200, k.xtyp, k.dlR, k.off256, h)
        add_bias(k, x, a['L1_gnn_h_bias'])
        V.do(vec.scalar_tensor_tensor(out=x, in0=h[:, :], scalar=s, in1=x, op0=ALU.mult, op1=ALU.add))
        fence(k)


def top2_gates(k, sc, E, gates):
    nc, V, A = k.nc, k.V, k.A
    vec = nc.vector
    with ExitStack() as es:
        def sb(n, shape, dt=F):
            return es.enter_context(nc.sbuf_tensor(k.nm(n), shape, dt))
        mv = sb("mv", [128, NB, 8])
        mi = sb("mi", [128, NB, 8], U32)
        mf = sb("mf", [128, NB, 2])
        w = sb("w", [128, NB, 2])
        dn = sb("dn", [128, NB])
        t1 = sb("t1", [128, NB, E])

        def vs(op, *args, **kw):
            V.wait(V.now())
            V.do(op(*args, **kw))
        V.wait(V.now())
        for b in range(NB):
            V.do(vec.max(mv[:, b, :], sc[:, b, :]))
        V.wait(V.now())
        for b in range(NB):
            V.do(vec.max_index(mi[:, b, :], mv[:, b, :], sc[:, b, :]))
        vs(vec.tensor_copy, mf[:, :, :], mi[:, :, 0:2])
        vs(vec.tensor_tensor, dn[:, :], mv[:, :, 1], mv[:, :, 0], ALU.subtract)
        A.wait(V.now())
        A.do(nc.scalar.activation(w[:, :, 1], dn[:, :], ACT.Exp))
        V.wait(A.now())
        vs(vec.tensor_scalar, dn[:, :], w[:, :, 1], 1.0, None, ALU.add)
        vs(vec.reciprocal, w[:, :, 0], dn[:, :])
        vs(vec.tensor_tensor, w[:, :, 1], w[:, :, 1], w[:, :, 0], ALU.mult)
        io = bc(k.iof[:, 0:E].unsqueeze(1), [128, NB, E])
        vs(vec.tensor_tensor, gates, io, bc(mf[:, :, 0:1], [128, NB, E]), ALU.is_equal)
        vs(vec.tensor_tensor, gates, gates, bc(w[:, :, 0:1], [128, NB, E]), ALU.mult)
        vs(vec.tensor_tensor, t1[:, :, :], io, bc(mf[:, :, 1:2], [128, NB, E]), ALU.is_equal)
        vs(vec.tensor_tensor, t1[:, :, :], t1[:, :, :], bc(w[:, :, 1:2], [128, NB, E]), ALU.mult)
        vs(vec.tensor_tensor, gates, gates, t1[:, :, :], ALU.add)
        fence(k)


def moe(k, x, xT, gates, E, Hd, W1, b1, W2, b2):
    nc, V, A, P = k.nc, k.V, k.A, k.P
    vec = nc.vector
    HC = Hd // 128
    x3 = x.rearrange("p (b c) -> p b c", b=NB)
    with ExitStack() as es:
        def sb(n, shape, dt=F):
            return es.enter_context(nc.sbuf_tensor(k.nm(n), shape, dt))
        w1 = sb("w1", [128, 2, 2, Hd])
        w2 = sb("w2", [128, 2, HC, D])
        bb = sb("bb", [128, E, HC])
        b2s = sb("b2s", [E, D])
        gT = sb("gT", [E, 3200])
        hT = sb("hT", [128, 4, 512])
        k.ld.start(bb[:, :, :], b1.rearrange("e (c p) -> p e c", p=128), small=True)
        k.ld.start(b2s[:, :], b2)
        free = [None, None]

        def fetch(e):
            k.S.wait(free[e % 2])
            t = [k.ld.start(w1[:, e % 2, c, :], W1[e, 128 * c:128 * (c + 1), :]) for c in range(2)]
            t.append(k.ld.start(w2[:, e % 2, :, :], W2[e].rearrange("(c p) n -> p c n", p=128)))
            return t
        small = k.ld.all()
        tw = [fetch(0), fetch(1)]
        P.wait(small)
        A.wait(small)
        for b in range(NB):
            bk = b % 2
            P.wait(k.pst[bk])
            P.do(nc.tensor.transpose(k.ps[bk][0:E, 0:128], gates[:, b, :], k.ident[:, :]))
            A.wait(P.now())
            k.pst[bk] = A.do(nc.scalar.copy(gT[:, 128 * b:128 * (b + 1)], k.ps[bk][0:E, 0:128]))
            P.wait(A.now(), k.pst[2 + bk])
            mm(k, k.ps[2 + bk][:, 0:D], gT[:, 128 * b:128 * (b + 1)], b2s[:, :])
            V.wait(P.now())
            k.pst[2 + bk] = V.do(vec.tensor_tensor(x3[:, b, :], x3[:, b, :], k.ps[2 + bk][:, 0:D], ALU.add))
        hfree = [None] * 4
        hn = 0
        cn = 0
        for e in range(E):
            P.wait(tw[e])
            for ch in range(7):
                t0, tw_ = 512 * ch, min(512, 3200 - 512 * ch)
                oa = (4, 5) if cn % 2 == 0 else (6, 7)
                cn += 1
                pend = []

                def second(hc, slot, ta):
                    P.wait(ta)
                    if hc == 0:
                        P.wait(k.pst[oa[0]], k.pst[oa[1]])
                    for j in range(tw_ // 128):
                        hfree[slot] = mm(k, k.ps[oa[j // 2]][:, D * (j % 2):D * (j % 2 + 1)],
                                         hT[:, slot, 128 * j:128 * (j + 1)], w2[:, e % 2, hc, :],
                                         start=(hc == 0 and j % 2 == 0), stop=(hc == HC - 1))
                for hc in range(HC):
                    bk = hn % 4
                    slot = hn % 4
                    hn += 1
                    P.wait(k.pst[bk])
                    for c in range(2):
                        mm(k, k.ps[bk][:, 0:tw_], w1[:, e % 2, c, 128 * hc:128 * (hc + 1)], xT[:, c, t0:t0 + tw_],
                           start=(c == 0), stop=(c == 1))
                    A.wait(P.now(), hfree[slot])
                    ta = k.pst[bk] = A.do(nc.scalar.activation(hT[:, slot, 0:tw_], k.ps[bk][:, 0:tw_], ACT.Gelu,
                                                               bias=bb[:, e, hc:hc + 1]))
                    pend.append((hc, slot, ta))
                    if len(pend) > 1:
                        second(*pend.pop(0))
                for q in pend:
                    second(*q)
                tp = P.now()
                V.wait(tp)
                for j in range(tw_ // 128):
                    b = 4 * ch + j
                    V.wait(V.now())
                    k.pst[oa[j // 2]] = V.do(vec.scalar_tensor_tensor(
                        out=x3[:, b, :], in0=k.ps[oa[j // 2]][:, D * (j % 2):D * (j % 2 + 1)],
                        scalar=gates[:, b, e:e + 1], in1=x3[:, b, :], op0=ALU.mult, op1=ALU.add))
            free[e % 2] = P.now()
            if e + 2 < E:
                tw.append(fetch(e + 2))
        fence(k)


def finish_second(k, es):
    nc, V = k.nc, k.V
    vec = nc.vector
    e = k.second
    T = e.T

    def sb(n, shape, dt):
        return es.enter_context(nc.sbuf_tensor(k.nm(n), shape, dt))
    k.dl2 = sb("dl2", [128, T], F)
    k.xs2 = sb("xs2", [128, T], U32)
    k.n4 = sb("n4", [1, T], I32)
    k.n16 = sb("n16", [1, T], I32)
    blk = sb("blk", [128, T], F)
    tile_blocks(k, "n", T, e.st, blk, ((4, k.n4), (16, k.n16)))
    k.n_flags = edge_flags_dram(k, "n", T)
    with ExitStack() as e2:
        p = e2.enter_context(nc.sbuf_tensor("sorted_n", [128, T, 2], F))
        k.S.wait(k.late.all())
        V.wait(k.ld.start(p[:, :, :].rearrange("p a b -> p (a b)"), e.tab.rearrange("(p r) w -> p (r w)", p=128)))
        V.do(vec.tensor_copy(k.xs2[:, :], p[:, :, 1]))
        V.do(vec.scalar_tensor_tensor(out=k.dl2[:, :], in0=blk[:, :], scalar=-128.0, in1=p[:, :, 0],
                                      op0=ALU.mult, op1=ALU.add))
        V.wait(V.now())
        to_rows(k, "nf", p[:, :, 0], T, k.n_flags[128:128 + T * 128])
        fence(k)


def stage_l1_ffn(k, x, a):
    nc, V, A, P, G = k.nc, k.V, k.A, k.P, k.G
    vec = nc.vector
    T = k.T2
    table = nc.dram_tensor("gat_rows", (3200, 20), F).ap()
    with ExitStack() as es:
        def sb(n, shape, dt=F):
            return es.enter_context(nc.sbuf_tensor(k.nm(n), shape, dt))

        def vs(op, *args, **kw):
            V.wait(V.now())
            return V.do(op(*args, **kw))
        xT = sb("xT", [128, 2, 3200])
        gates = sb("gates", [128, NB, 4])
        with ExitStack() as e2:
            finish_second(k, e2)

            def s2(n, shape, dt=F):
                return e2.enter_context(nc.sbuf_tensor(k.nm(n), shape, dt))
            with ExitStack() as e3:
                xn = e3.enter_context(nc.sbuf_tensor(k.nm("xn"), [128, NB * D], F))
                layernorm(k, x, xn[:, :])
                transpose_rows(k, xn, xT)
                fence(k)
            wg = s2("wg", [128, 2, 16])
            h = s2("h", [128, NB, 20])
            ad = s2("ad", [128, NB, 4])
            load_w(k, wg, a['L1_ffn_W_gat'])
            asr = bcast_row(k, e2, a['L1_ffn_att_src'].rearrange("h c -> (h c)"), 16)
            adr = bcast_row(k, e2, a['L1_ffn_att_dst'].rearrange("h c -> (h c)"), 16)
            bg = bcast_row(k, e2, a['L1_ffn_b_gat'], 16)
            lg = bcast_row(k, e2, a['L1_ffn_ln_gamma'], 16)
            lb = bcast_row(k, e2, a['L1_ffn_ln_beta'], 16)
            P.wait(k.ld.all())
            V.wait(k.ld.all())

            def sink(b, m0, mw, ps):
                V.wait(P.now())
                return V.do(vec.tensor_copy(h[:, b, 0:16], ps))
            project(k, xT, wg, 16, sink)
            tmp = s2("tmp", [128, NB, 16])
            for r, o in ((asr, h[:, :, 16:20]), (adr, ad[:, :, :])):
                vs(vec.tensor_tensor, tmp[:, :, :], h[:, :, 0:16], bc(r[:, :].unsqueeze(1), [128, NB, 16]), ALU.mult)
                vs(vec.tensor_reduce, o, tmp[:, :, :].rearrange("p b (h c) -> p b h c", h=4), AX, ALU.add)
            k.S.wait(V.now())
            k.ld.start(table.rearrange("(b p) c -> p b c", p=128), h[:, :, :])
            fence(k)
            gs = s2("gs", [128, T, 20])
            L = s2("L", [128, 4 * T])
            tg = [k.ind.gather(gs[:, t, :], table, k.xs2[:, t:t + 1], 3200) for t in range(T)]
            adf = ad[:, :, :].rearrange("p b c -> p (b c)")
            e4 = ExitStack()
            rows = DstRows(k, e4, k.dl2, k.n4, adf, 4, 4)
            Lv = L[:, :].rearrange("p (h t) -> p h t", h=4)
            te = [None] * T

            def spread(t):
                bk = 2 + (t // 32) % 4
                if t % 32 == 0:
                    P.wait(k.pst[bk])
                te[t] = rows.spread(t, k.ps[bk][:, 4 * (t % 32):4 * (t % 32) + 4])

            def collect(t):
                if t % 32 != 31:
                    return
                bk = 2 + (t // 32) % 4
                V.wait(te[t])
                k.pst[bk] = V.do(vec.tensor_copy(Lv[:, :, t - 31:t + 1],
                                                 k.ps[bk][:, 0:128].rearrange("p (t h) -> p h t", h=4)))
            pipeline(T, (0, rows.mark), (2, rows.turn), (5, spread), (7, collect))
            V.wait(tg, V.now())
            V.do(vec.tensor_tensor(Lv, Lv, gs[:, :, 16:20].rearrange("p t h -> p h t"), ALU.add))
            vs(vec.scalar_tensor_tensor, out=L[:, :], in0=L[:, :], scalar=0.2, in1=L[:, :], op0=ALU.mult, op1=ALU.max)
            fence(k)
            e4.close()
            seg_softmax(k, "n1", L[:, :], 4, 32, T, k.n_flags, ALU.add, 1e-16)
            g4 = gs[:, :, 0:16].rearrange("p t (h c) -> p t h c", h=4)
            for c in range(4):
                vs(vec.tensor_tensor, gs[:, :, 0:16].rearrange("p t (h c) -> p h t c", h=4)[:, :, :, c],
                                     gs[:, :, 0:16].rearrange("p t (h c) -> p h t c", h=4)[:, :, :, c],
                                     Lv, ALU.mult)
            acc = s2("acc", [128, NB * 16])
            oh = s2("oh", [128, 6, 128])
            vs(vec.memset, acc[:, :], 0.0)
            free = [None] * 6
            off = Offsets(k, mybir.EngineType.DVE, k.n16, 24 * 16)
            to, tp = {}, {}

            def mark(t):
                V.wait(free[t % 6])
                to[t] = onehot(k, oh[:, t % 6, :], k.dl2, t)

            def product(t):
                P.wait(to.pop(t), k.pst[t % 6])
                tp[t] = free[t % 6] = mm(k, k.ps[t % 6][:, 0:16], oh[:, t % 6, :], gs[:, t, 0:16])

            def add(t):
                d = acc[:, bass.ds(off(t), 16)]
                V.wait(tp.pop(t), V.now())
                k.pst[t % 6] = V.do(vec.tensor_tensor(d, d, k.ps[t % 6][:, 0:16], ALU.add))
            pipeline(T, (0, mark), (2, product), (4, add))
            c3 = acc[:, :].rearrange("p (b c) -> p b c", b=NB)
            mu = s2("mu", [128, NB])

            def row16(r):
                return bc(r[:, :].unsqueeze(1), [128, NB, 16])
            vs(vec.tensor_tensor, c3, c3, row16(bg), ALU.add)
            vs(vec.tensor_reduce, mu[:, :], c3, AX, ALU.add)
            vs(vec.tensor_scalar, mu[:, :], mu[:, :], 1.0 / 16, None, ALU.mult)
            vs(vec.tensor_tensor, c3, c3, bc(mu[:, :].unsqueeze(2), [128, NB, 16]), ALU.subtract)
            vs(vec.tensor_tensor, tmp[:, :, :], c3, c3, ALU.mult)
            vs(vec.tensor_reduce, mu[:, :], tmp[:, :, :], AX, ALU.add)
            vs(vec.tensor_scalar, mu[:, :], mu[:, :], 1.0 / 16, 1e-5, ALU.mult, ALU.add)
            A.wait(V.now())
            A.do(nc.scalar.activation(mu[:, :], mu[:, :], ACT.Sqrt))
            V.wait(A.now())
            vs(vec.reciprocal, mu[:, :], mu[:, :])
            vs(vec.tensor_tensor, c3, c3, bc(mu[:, :].unsqueeze(2), [128, NB, 16]), ALU.mult)
            vs(vec.tensor_tensor, c3, c3, row16(lg), ALU.mult)
            vs(vec.tensor_tensor, c3, c3, row16(lb), ALU.add)
            sc = s2("sc", [128, NB, 8])
            vs(vec.memset, sc[:, :, :], NEG)
            vs(vec.tensor_reduce, sc[:, :, 0:4], c3.rearrange("p b (h e) -> p b e h", h=4), AX, ALU.add)
            vs(vec.tensor_scalar, sc[:, :, 0:4], sc[:, :, 0:4], 0.25, None, ALU.mult)
            fence(k)
            top2_gates(k, sc, 4, gates[:, :, :])
        moe(k, x, xT, gates, 4, 512, a['L1_ffn_W1'], a['L1_ffn_b1'], a['L1_ffn_W2'], a['L1_ffn_b2'])


def stage_l2_gnn(k, x, a):
    nc, V, A, P = k.nc, k.V, k.A, k.P
    vec = nc.vector
    with ExitStack() as es:
        def sb(n, shape, dt=F):
            return es.enter_context(nc.sbuf_tensor(k.nm(n), shape, dt))

        def vs(op, *args, **kw):
            V.wait(V.now())
            return V.do(op(*args, **kw))
        h = sb("h", [128, NB * D])
        h3 = h[:, :].rearrange("p (b c) -> p b c", b=NB)
        xT = sb("xT", [128, 2, 3200])
        dinv = sb("dinv", [128, NB])
        pos = sb("pos", [128, NB])
        xn = sb("xn", [128, NB * D])
        layernorm(k, x, xn[:, :])
        transpose_rows(k, xn, xT)
        fence(k)
        vs(vec.tensor_scalar, pos[:, :], k.deg[:, :], 0.5, None, ALU.is_gt)
        vs(vec.tensor_scalar, dinv[:, :], k.deg[:, :], 1e-12, None, ALU.max)
        A.wait(V.now())
        A.do(nc.scalar.activation(dinv[:, :], dinv[:, :], ACT.Sqrt))
        V.wait(A.now())
        vs(vec.reciprocal, dinv[:, :], dinv[:, :])
        vs(vec.tensor_tensor, dinv[:, :], dinv[:, :], pos[:, :], ALU.mult)
        w = sb("w", [128, 2, D])
        for i in range(2):
            table = nc.dram_tensor(f"gcn{i}", (3200, D), F).ap()
            with ExitStack() as e2:
                P.wait(load_w(k, w, a[f'L2_gnn_W{i + 1}']), V.now())
                buf = e2.enter_context(nc.sbuf_tensor(k.nm("tb"), [128, 6, D], F))
                free = [None] * 6

                def sink(b, m0, mw, ps):
                    V.wait(P.now(), free[b % 6])
                    t = V.do(vec.tensor_scalar(buf[:, b % 6, :], ps, dinv[:, b:b + 1], None, ALU.mult))
                    k.S.wait(t)
                    free[b % 6] = k.ld.start(table[128 * b:128 * (b + 1), :], buf[:, b % 6, :])
                    return t
                V.wait(V.now())
                project(k, xT, w, D, sink)
                fence(k)
            seg_sum(k, k.T, table, 3200, k.xsrc, k.dlA, k.off256, h)
            vs(vec.tensor_tensor, h3, h3, bc(dinv[:, :].unsqueeze(2), [128, NB, D]), ALU.mult)
            fence(k)
            add_bias(k, h[:, :], a[f'L2_gnn_b{i + 1}'])
            if i == 0:
                nr = sb("nr", [128, NB])
                junk = sb("junk", [128, D])
                for b in range(NB):
                    A.wait(A.now())
                    A.do(nc.scalar.activation(junk[:, :], h3[:, b, :], ACT.Square, accum_out=nr[:, b:b + 1]))
                A.wait(A.now())
                A.do(nc.scalar.activation(nr[:, :], nr[:, :], ACT.Sqrt))
                V.wait(A.now())
                vs(vec.tensor_scalar, nr[:, :], nr[:, :], 1e-12, None, ALU.max)
                vs(vec.reciprocal, nr[:, :], nr[:, :])
                vs(vec.tensor_tensor, h3, h3, bc(nr[:, :].unsqueeze(2), [128, NB, D]), ALU.mult)
                transpose_rows(k, h, xT)
                fence(k)
        vs(vec.tensor_tensor, h[:, :], h[:, :], xn[:, :], ALU.add)
        vs(vec.tensor_tensor, x, x, h[:, :], ALU.add)
        fence(k)


def stage_l2_ffn(k, x, a):
    nc, V, A, P, G = k.nc, k.V, k.A, k.P, k.G
    vec = nc.vector
    x3 = x.rearrange("p (b c) -> p b c", b=NB)
    with ExitStack() as es:
        def sb(n, shape, dt=F):
            return es.enter_context(nc.sbuf_tensor(k.nm(n), shape, dt))

        def vs(op, *args, **kw):
            V.wait(V.now())
            return V.do(op(*args, **kw))
        xT = sb("xT", [128, 2, 3200])
        with ExitStack() as e3:
            xn = e3.enter_context(nc.sbuf_tensor(k.nm("xn"), [128, NB * D], F))
            layernorm(k, x, xn[:, :])
            transpose_rows(k, xn, xT)
            fence(k)
        rw = sb("rw", [32, D])
        rwT = sb("rwT", [128, 2, 32])
        k.ld.start(rw[:, :], a['L2_ffn_router_w'])
        rb = bcast_row(k, es, a['L2_ffn_router_b'], 32)
        w1 = sb("w1", [128, 2, 32, 64])
        for c in range(2):
            k.ld.start(w1[:, c, :, :], a['L2_ffn_W1'][:, 128 * c:128 * (c + 1), :].rearrange("e p h -> p e h"))
        b1 = sb("b1", [128, 16])
        k.ld.start(b1[:, :], a['L2_ffn_b1'].rearrange("(i e) h -> (e h) i", e=2), small=True)
        w2 = sb("w2", [128, 16, D])
        k.ld.start(w2[:, :, :], a['L2_ffn_W2'].rearrange("(i e) h n -> (e h) i n", e=2))
        b2 = sb("b2", [32, D])
        k.ld.start(b2[:, :], a['L2_ffn_b2'])
        P.wait(k.ld.all())
        V.wait(k.ld.all())
        A.wait(k.ld.all())
        for c in range(2):
            P.do(nc.tensor.transpose(k.ps[0][:, 32 * c:32 * c + 32], rw[:, 128 * c:128 * (c + 1)], k.ident[0:32, 0:32]))
        V.wait(P.now())
        vs(vec.tensor_copy, rwT[:, :, :], k.ps[0][:, 0:64].rearrange("p (c e) -> p c e", c=2))
        k.pst[0] = V.now()
        lg = sb("lg", [128, NB, 32])

        def sink(b, m0, mw, ps):
            V.wait(P.now())
            return V.do(vec.tensor_tensor(lg[:, b, :], ps, rb[:, :], ALU.add))
        P.wait(V.now())
        project(k, xT, rwT, 32, sink)
        mv = sb("mv", [128, NB, 8])
        mi = sb("mi", [128, NB, 8], U32)
        mf = sb("mf", [128, NB, 1])
        oh = sb("oh", [128, NB, 32])
        V.wait(V.now())
        for b in range(NB):
            V.do(vec.max(mv[:, b, :], lg[:, b, :]))
        V.wait(V.now())
        for b in range(NB):
            V.do(vec.max_index(mi[:, b, :], mv[:, b, :], lg[:, b, :]))
        vs(vec.tensor_copy, mf[:, :, :], mi[:, :, 0:1])
        vs(vec.tensor_tensor, oh[:, :, :], bc(k.iof[:, 0:32].unsqueeze(1), [128, NB, 32]),
                             bc(mf[:, :, :], [128, NB, 32]), ALU.is_equal)
        P.wait(V.now())
        ohT = sb("ohT", [32, 3200])
        nohT = sb("nohT", [32, 3200], BF)
        sel = sb("sel", [32, 32, 64], BF)
        vs(vec.tensor_scalar, sel[:, :, :], bc(k.ident[0:32, 0:32].unsqueeze(2), [32, 32, 64]), NEG, None, ALU.mult)
        for b in range(NB):
            bk = b % 2
            P.wait(k.pst[bk])
            P.do(nc.tensor.transpose(k.ps[bk][0:32, 0:128], oh[:, b, :], k.ident[:, :]))
            A.wait(P.now())
            k.pst[bk] = A.do(nc.scalar.copy(ohT[:, 128 * b:128 * (b + 1)], k.ps[bk][0:32, 0:128]))
        V.wait(A.now())
        vs(vec.tensor_scalar, nohT[:, :], ohT[:, :], -1.0, 1.0, ALU.mult, ALU.add)
        P.wait(V.now(), A.now())
        hT = sb("hT", [128, 4, 512])
        hfree = [None] * 4
        hn = 0
        for ch in range(7):
            t0, tw = 512 * ch, min(512, 3200 - 512 * ch)
            oa = (4, 5) if ch % 2 == 0 else (6, 7)
            pend = []

            def second(i, slot, ta):
                P.wait(ta)
                for j in range(tw // 128):
                    hfree[slot] = mm(k, k.ps[oa[j // 2]][:, D * (j % 2):D * (j % 2 + 1)],
                                     hT[:, slot, 128 * j:128 * (j + 1)], w2[:, i, :], start=False, stop=(i == 15))
            P.wait(k.pst[oa[0]], k.pst[oa[1]])
            for j in range(tw // 128):
                mm(k, k.ps[oa[j // 2]][:, D * (j % 2):D * (j % 2 + 1)],
                   ohT[:, t0 + 128 * j:t0 + 128 * (j + 1)], b2[:, :], start=(j % 2 == 0), stop=False)
            for i in range(16):
                bk = slot = hn % 4
                hn += 1
                P.wait(k.pst[bk])
                for c in range(2):
                    mm(k, k.ps[bk][:, 0:tw], w1[:, c, 2 * i:2 * i + 2, :].rearrange("p e h -> p (e h)"),
                       xT[:, c, t0:t0 + tw], start=(c == 0), stop=False)
                mm(k, k.ps[bk][:, 0:tw], sel[:, 2 * i:2 * i + 2, :].rearrange("p e h -> p (e h)"),
                   nohT[:, t0:t0 + tw], start=False, stop=True)
                A.wait(P.now(), hfree[slot])
                ta = k.pst[bk] = A.do(nc.scalar.activation(hT[:, slot, 0:tw], k.ps[bk][:, 0:tw], ACT.Relu,
                                                           bias=b1[:, i:i + 1]))
                pend.append((i, slot, ta))
                if len(pend) > 1:
                    second(*pend.pop(0))
            for q in pend:
                second(*q)
            V.wait(P.now())
            for j in range(tw // 128):
                b = 4 * ch + j
                k.pst[oa[j // 2]] = V.do(vec.scalar_tensor_tensor(
                    out=x3[:, b, :], in0=k.ps[oa[j // 2]][:, D * (j % 2):D * (j % 2 + 1)],
                    scalar=0.0, in1=x3[:, b, :], op0=ALU.max, op1=ALU.add))
        fence(k)


def stage_l3_gnn(k, x, a):
    nc, V, A, P, G = k.nc, k.V, k.A, k.P, k.G
    vec = nc.vector
    T = k.T
    table = nc.dram_tensor("h3", (3200, D), F).ap()
    tabs = nc.dram_tensor("as3", (3200, 8), F).ap()
    with ExitStack() as es:
        def sb(n, shape, dt=F):
            return es.enter_context(nc.sbuf_tensor(k.nm(n), shape, dt))

        def vs(op, *args, **kw):
            V.wait(V.now())
            return V.do(op(*args, **kw))
        L = sb("L", [128, 8 * T])
        Lv = L[:, :].rearrange("p (h t) -> p h t", h=8)
        with ExitStack() as e2:
            def s2(n, shape, dt=F):
                return e2.enter_context(nc.sbuf_tensor(k.nm(n), shape, dt))
            ha = s2("ha", [128, NB, 264])
            with ExitStack() as e3:
                xn = e3.enter_context(nc.sbuf_tensor(k.nm("xn"), [128, NB * D], F))
                xT = e3.enter_context(nc.sbuf_tensor(k.nm("xT"), [128, 2, 3200], F))
                w = e3.enter_context(nc.sbuf_tensor(k.nm("w"), [128, 2, D], F))
                wT = e3.enter_context(nc.sbuf_tensor(k.nm("wT"), [128, 2, D], F))
                asb = e3.enter_context(nc.sbuf_tensor(k.nm("as"), [128, NB, 8], F))
                tmp = e3.enter_context(nc.sbuf_tensor(k.nm("tmp"), [128, NB, D], F))
                layernorm(k, x, xn[:, :])
                transpose_rows(k, xn, xT)
                load_w(k, w, a['L3_gnn_W'])
                asr = bcast_row(k, e3, a['L3_gnn_a_src'].rearrange("h c -> (h c)"), D)
                adr = bcast_row(k, e3, a['L3_gnn_a_dst'].rearrange("h c -> (h c)"), D)
                P.wait(k.ld.all(), k.pst[2], k.pst[3])
                V.wait(k.ld.all())
                for i in range(2):
                    for j in range(2):
                        P.do(nc.tensor.transpose(k.ps[2][:, 256 * i + 128 * j:256 * i + 128 * j + 128],
                                                 w[:, j, 128 * i:128 * (i + 1)], k.ident[:, :]))
                V.wait(P.now())
                k.pst[2] = vs(vec.tensor_copy, wT[:, :, :].rearrange("p a b -> p (a b)"), k.ps[2][:, :])
                P.wait(V.now())

                def sink(b, m0, mw, ps):
                    V.wait(P.now())
                    return V.do(vec.tensor_copy(ha[:, b, 0:D], ps))
                project(k, xT, wT, D, sink)
                k.S.wait(V.now())
                k.ld.start(table.rearrange("(b p) c -> p b c", p=128), ha[:, :, 0:D])
                for r, o in ((asr, asb[:, :, :]), (adr, ha[:, :, D:D + 8])):
                    vs(vec.tensor_tensor, tmp[:, :, :], ha[:, :, 0:D], bc(r[:, :].unsqueeze(1), [128, NB, D]), ALU.mult)
                    vs(vec.tensor_reduce, o, tmp[:, :, :].rearrange("p b (h c) -> p b h c", h=8), AX, ALU.add)
                k.S.wait(V.now())
                k.ld.start(tabs.rearrange("(b p) c -> p b c", p=128), asb[:, :, :])
                fence(k)
            ew = s2("ew", [4, D])
            k.ld.start(ew[0:3, :], a['L3_gnn_edge_W'].rearrange("n f -> f n"), small=True)
            k.ld.start(ew[3:4, :], rows_of(a['L3_gnn_edge_b']))
            P.wait(k.ld.all())
            AS = s2("AS", [128, T, 8])
            tg = [k.ind.gather(AS[:, t, :], tabs, k.xsrc[:, t:t + 1], 3200) for t in range(T)]
            rows = DstRows(k, e2, k.dlA, k.off264, ha[:, :, :].rearrange("p b c -> p (b c)"), 264, 264)
            aT = s2("aT", [4, 4, 4, 128])
            en = s2("en", [128, 6, D])
            lin = s2("lin", [128, T, 8])
            af = [None] * 4
            ta = [None] * 4
            ef = [None] * 6
            th, te, tx = {}, {}, {}

            def attrs(t):
                if t % 4:
                    return
                i = (t // 4) % 4
                P.wait(k.pst[7])
                for u in range(4):
                    P.do(nc.tensor.transpose(k.ps[7][0:4, 128 * u:128 * (u + 1)], k.attr[:, t + u, :], k.ident[:, :]))
                A.wait(P.now(), af[i])
                k.pst[7] = ta[i] = A.do(nc.scalar.copy(aT[:, i, :, :].rearrange("p a b -> p (a b)"), k.ps[7][0:4, :]))

            def spread(t):
                i = (t // 4) % 4
                bk = 2 + t % 3
                eb = 5 + t % 2
                P.wait(ta[i], k.pst[eb])
                af[i] = te[t] = mm(k, k.ps[eb][:, 0:D], aT[:, i, t % 4, :], ew[:, :])
                P.wait(k.pst[bk])
                th[t] = rows.spread(t, k.ps[bk][:, 0:264])

            def relu(t):
                eb = 5 + t % 2
                A.wait(te.pop(t), ef[t % 6])
                k.pst[eb] = te[t] = A.do(nc.scalar.activation(en[:, t % 6, :], k.ps[eb][:, 0:D], ACT.Relu))

            def weigh(t):
                bk = 2 + t % 3
                V.wait(te.pop(t), th.pop(t))
                tx[t] = V.do(vec.tensor_tensor(en[:, t % 6, :], en[:, t % 6, :], k.ps[bk][:, 0:D], ALU.mult))
                A.wait(tx[t])
                k.pst[bk] = A.do(nc.scalar.copy(lin[:, t, :], k.ps[bk][:, D:D + 8]))

            def total(t):
                V.wait(tx.pop(t))
                ef[t % 6] = V.do(vec.tensor_reduce(Lv[:, :, t], en[:, t % 6, :].rearrange("p (h c) -> p h c", h=8),
                                                   AX, ALU.add))
            pipeline(T, (0, attrs), (0, rows.mark), (2, rows.turn), (5, spread), (6, relu), (7, weigh), (9, total))
            V.wait(tg, A.now(), V.now())
            V.do(vec.tensor_tensor(Lv, Lv, lin[:, :, :].rearrange("p t h -> p h t"), ALU.add))
            vs(vec.tensor_tensor, Lv, Lv, AS[:, :, :].rearrange("p t h -> p h t"), ALU.add)
            vs(vec.scalar_tensor_tensor, out=L[:, :], in0=L[:, :], scalar=0.2, in1=L[:, :], op0=ALU.mult, op1=ALU.max)
            vs(vec.tensor_tensor, Lv, Lv, bc(k.loopneg[:, :].unsqueeze(1), [128, 8, T]), ALU.add)
            fence(k)
        seg_softmax(k, "g3", L[:, :], 8, 16, T, k.m_flags, ALU.max, 1e-10)
        h = sb("h", [128, NB * D])
        seg_sum(k, T, table, 3200, k.xsrc, k.dlR, k.off256, h, alpha=L[:, :], H=8)
        add_bias(k, h[:, :], a['L3_gnn_bias'])
        vs(vec.tensor_tensor, x, x, h[:, :], ALU.add)
        fence(k)


def stage_l3_ffn(k, x, a):
    nc, V, A, P, G, S = k.nc, k.V, k.A, k.P, k.G, k.S
    vec = nc.vector
    T, E, Hd = 56, 8, 1024
    x3 = x.rearrange("p (b c) -> p b c", b=NB)
    xs = nc.dram_tensor("moe_in", (128 * T, D), F).ap()
    ys = nc.dram_tensor("moe_out", (128 * T, D), F).ap()
    with ExitStack() as es:
        def sb(n, shape, dt=F):
            return es.enter_context(nc.sbuf_tensor(k.nm(n), shape, dt))

        def vs(op, *args, **kw):
            V.wait(V.now())
            return V.do(op(*args, **kw))
        w1 = sb("w1", [128, 2, E * Hd])
        w2 = sb("w2", [128, 8, E * D])
        b1 = sb("b1", [E, Hd])
        b2 = sb("b2", [E, D])
        wt = sb("wt", [128, NB, 2])
        pos = sb("pos", [128, 2, NB], U32)
        ohE = sb("ohE", [E, T])
        o1 = sb("o1", [1, T], I32)
        o2 = sb("o2", [1, T], I32)
        with ExitStack() as e2:
            def s2(n, shape, dt=F):
                return e2.enter_context(nc.sbuf_tensor(k.nm(n), shape, dt))
            zero = s2("zero", [128, D])
            wg = s2("wg", [128, 2, 8])
            sc = s2("sc", [128, NB, 8])
            V.do(vec.memset(zero[:, :], 0.0))
            load_w(k, wg, a['L3_ffn_Wg'])
            bg = bcast_row(k, e2, a['L3_ffn_bg'], 8)
            tsmall = k.ld.all()
            tb = [k.ld.start(b1[:, :], a['L3_ffn_b1']), k.ld.start(b2[:, :], a['L3_ffn_b2'])]
            S.wait(V.now())
            zt = [k.ld.start(xs[128 * t:128 * (t + 1), :], zero[:, :]) for t in range(T)]
            tw = [[k.ld.start(w1[:, c, Hd * e:Hd * (e + 1)], a['L3_ffn_W1'][e, 128 * c:128 * (c + 1), :])
                   for c in range(2)] for e in range(E)]
            xn = s2("xn", [128, NB * D])
            xT = w2[:, 0:4, :].rearrange("p c n -> p (c n)")[:, 0:6400].rearrange("p (c n) -> p c n", c=2)
            layernorm(k, x, xn[:, :])
            transpose_rows(k, xn, xT)
            P.wait(tsmall)
            V.wait(tsmall)

            def sink(b, m0, mw, ps):
                V.wait(P.now())
                return V.do(vec.tensor_tensor(sc[:, b, :], ps, bg[:, :], ALU.add))
            project(k, xT, wg, 8, sink)
            S.wait(P.now())
            for e in range(E):
                tw[e].append(k.ld.start(w2[:, :, D * e:D * (e + 1)],
                                        a['L3_ffn_W2'][e].rearrange("(c p) n -> p c n", p=128)))
            V.wait(V.now())
            mv = s2("mv", [128, NB, 8])
            mi = s2("mi", [128, NB, 8], U32)
            mf = s2("mf", [128, 2, NB])
            dn = s2("dn", [128, NB])
            C = 2 * NB
            O = s2("O", [128, C, E], BF)
            rk = s2("rk", [128, C, E])
            tot = s2("tot", [128, C, E])
            cm = s2("cm", [128, C + 1, E])
            nt = s2("nt", [128, E])
            ni = s2("ni", [128, E], I32)
            st = s2("st", [128, E])
            pf = s2("pf", [128, C])
            iv = s2("iv", [128, 1])
            pid = s2("pid", [128, 1])
            bt = s2("bt", [128, T])
            tf = s2("tf", [1, T])
            for b in range(NB):
                V.do(vec.max(mv[:, b, :], sc[:, b, :]))
            V.wait(V.now())
            for b in range(NB):
                V.do(vec.max_index(mi[:, b, :], mv[:, b, :], sc[:, b, :]))
            vs(vec.tensor_copy, mf[:, :, :], mi[:, :, 0:2].rearrange("p b k -> p k b"))
            vs(vec.tensor_tensor, dn[:, :], mv[:, :, 1], mv[:, :, 0], ALU.subtract)
            A.wait(V.now())
            A.do(nc.scalar.activation(wt[:, :, 1], dn[:, :], ACT.Exp))
            V.wait(A.now())
            vs(vec.tensor_scalar, dn[:, :], wt[:, :, 1], 1.0, None, ALU.add)
            vs(vec.reciprocal, wt[:, :, 0], dn[:, :])
            vs(vec.tensor_tensor, wt[:, :, 1], wt[:, :, 1], wt[:, :, 0], ALU.mult)
            V.wait(G.do(nc.gpsimd.iota(pid[:, :], pattern=[[0, 1]], base=0, channel_multiplier=1,
                                       allow_small_or_imprecise_dtypes=True)))
            vs(vec.tensor_scalar, iv[:, :], pid[:, :], LASTP - 0.5, 1.0e6, ALU.is_gt, ALU.mult)
            for i in range(2):
                vs(vec.tensor_tensor, mf[:, i, 24:25], mf[:, i, 24:25], iv[:, :], ALU.add)
            vs(vec.tensor_tensor, O[:, :, :], bc(k.iof[:, 0:E].unsqueeze(1), [128, C, E]),
               bc(mf[:, :, :].rearrange("p k b -> p (k b)").unsqueeze(2), [128, C, E]), ALU.is_equal)
            P.wait(V.now())
            Of = O[:, :, :].rearrange("p c e -> p (c e)")
            mm(k, k.ps[0][:, 0:C * E], k.ltrib[:, :], Of)
            mm(k, k.ps[1][:, 0:C * E], k.onesb[:, :], Of)
            V.wait(P.now())
            vs(vec.tensor_copy, rk[:, :, :].rearrange("p c e -> p (c e)"), k.ps[0][:, 0:C * E])
            vs(vec.tensor_copy, tot[:, :, :].rearrange("p c e -> p (c e)"), k.ps[1][:, 0:C * E])
            vs(vec.tensor_reduce, nt[:, :], tot[:, :, :].rearrange("p c e -> p e c"), AX, ALU.add)
            vs(vec.tensor_scalar, ni[:, :], nt[:, :], 1.0, 127.0, ALU.max, ALU.add)
            vs(vec.tensor_scalar, ni[:, :], ni[:, :], 7, None, ALU.arith_shift_right)
            vs(vec.tensor_copy, nt[:, :], ni[:, :])
            vs(vec.memset, st[:, 0:1], 0.0)
            vs(vec.tensor_tensor_scan, st[:, 1:E], k.ones[:, 0:E - 1], nt[:, 0:E - 1], 0.0, ALU.mult, ALU.add)
            vs(vec.tensor_scalar, cm[:, 0, :], st[:, :], 128.0, None, ALU.mult)
            V.wait(V.now())
            for e in range(E):
                V.do(vec.tensor_tensor_scan(cm[:, 1:C + 1, e], k.ones[:, 0:C], tot[:, :, e], cm[:, 0, e:e + 1],
                                            ALU.mult, ALU.add))
            vs(vec.tensor_tensor, rk[:, :, :], rk[:, :, :], cm[:, 0:C, :], ALU.add)
            vs(vec.tensor_tensor, rk[:, :, :], rk[:, :, :], O[:, :, :], ALU.mult)
            vs(vec.tensor_reduce, pf[:, :], rk[:, :, :], AX, ALU.add)
            for i in range(2):
                vs(vec.tensor_tensor, pf[:, 25 * i + 24:25 * i + 25], pf[:, 25 * i + 24:25 * i + 25], iv[:, :], ALU.add)
            vs(vec.tensor_copy, pos[:, :, :].rearrange("p k b -> p (k b)"), pf[:, :])
            vs(vec.memset, bt[:, :], 0.0)
            for e in range(1, E):
                vs(vec.scalar_tensor_tensor, out=bt[:, :], in0=k.tiles[:, 0:T], scalar=st[:, e:e + 1], in1=bt[:, :],
                   op0=ALU.is_ge, op1=ALU.add)
            for w, o in ((float(Hd), o1), (float(D), o2)):
                vs(vec.tensor_scalar, tf[:, :], bt[0:1, :], w, None, ALU.mult)
                vs(vec.tensor_copy, o[:, :], tf[:, :])
            vs(vec.tensor_scalar, ohE[:, :], bt[0:E, :], pid[0:E, :], None, ALU.is_equal)
            G.wait(V.now(), zt)
            for i in range(2):
                for b in range(NB):
                    k.ind.scatter(xs, pos[:, i, b:b + 1], xn[:, D * b:D * (b + 1)], 128 * T)
            vs(vec.tensor_scalar, pf[:, :], pf[:, :], float(128 * T - 1), None, ALU.min)
            V.wait(G.now())
            G.wait(V.now())
            tind = k.ind.all()
            V.wait(tind)
            vs(vec.tensor_copy, pos[:, :, :].rearrange("p k b -> p (k b)"), pf[:, :])
            fence(k)
        xt = sb("xt", [128, 3, D])
        xTt = sb("xTt", [128, 3, D])
        hb = sb("hb", [128, 2, Hd])
        hT = sb("hT", [128, 2, Hd])
        yb = sb("yb", [128, 3, D])
        off1 = Offsets(k, mybir.EngineType.PE, o1, 7 * Hd)
        off2 = Offsets(k, mybir.EngineType.PE, o2, 7 * D)
        tx, tt, tg, th, tq = {}, {}, {}, {}, {}
        xfree = [None] * 3
        xtfree = [None] * 3
        hfree = [None] * 2
        htfree = [None] * 2
        yfree = [None] * 3
        P.wait(tb)

        def fetch(t):
            S.wait(xfree[t % 3])
            tx[t] = k.ld.start(xt[:, t % 3, :], xs[128 * t:128 * (t + 1), :])

        def turn(t):
            P.wait(tx.pop(t), k.pst[0])
            for c in range(2):
                xfree[t % 3] = P.do(nc.tensor.transpose(k.ps[0][:, 128 * c:128 * (c + 1)],
                                                        xt[:, t % 3, 128 * c:128 * (c + 1)], k.ident[:, :]))
            V.wait(xfree[t % 3], xtfree[t % 3])
            k.pst[0] = tt[t] = V.do(vec.tensor_copy(xTt[:, t % 3, :], k.ps[0][:, 0:D]))

        def hidden(t):
            P.wait(tt.pop(t), tw[min(t, E - 1)])
            o = off1(t)
            for h in range(2):
                bk = 1 + 2 * (t % 2) + h
                P.wait(k.pst[bk])
                mm(k, k.ps[bk][:, :], bc(ohE[:, t:t + 1], [E, 128]), b1[:, 512 * h:512 * (h + 1)], stop=False)
                for c in range(2):
                    view = w1[:, c, 512 * h:512 * h + 7 * Hd + 512]
                    xtfree[t % 3] = mm(k, k.ps[bk][:, :], xTt[:, t % 3, 128 * c:128 * (c + 1)],
                                       view[:, bass.ds(o, 512)], start=False, stop=(c == 1))
                A.wait(P.now(), hfree[t % 2])
                k.pst[bk] = tg[t] = A.do(nc.scalar.activation(hb[:, t % 2, 512 * h:512 * (h + 1)], k.ps[bk][:, :],
                                                              ACT.Gelu))

        def turn_hidden(t):
            P.wait(tg.pop(t))
            for h in range(2):
                bk = 5 + h
                P.wait(k.pst[bk])
                for c in range(4):
                    s = slice(512 * h + 128 * c, 512 * h + 128 * (c + 1))
                    hfree[t % 2] = P.do(nc.tensor.transpose(k.ps[bk][:, 128 * c:128 * (c + 1)], hb[:, t % 2, s],
                                                            k.ident[:, :]))
                V.wait(P.now(), htfree[t % 2])
                k.pst[bk] = th[t] = V.do(vec.tensor_copy(hT[:, t % 2, 512 * h:512 * (h + 1)], k.ps[bk][:, :]))

        def output(t):
            P.wait(th.pop(t), k.pst[7])
            o = off2(t)
            mm(k, k.ps[7][:, 0:D], bc(ohE[:, t:t + 1], [E, 128]), b2[:, :], stop=False)
            for c in range(8):
                htfree[t % 2] = mm(k, k.ps[7][:, 0:D], hT[:, t % 2, 128 * c:128 * (c + 1)],
                                   w2[:, c, bass.ds(o, D)], start=False, stop=(c == 7))
            V.wait(P.now(), yfree[t % 3])
            k.pst[7] = V.do(vec.tensor_copy(yb[:, t % 3, :], k.ps[7][:, 0:D]))
            S.wait(V.now())
            yfree[t % 3] = k.ld.start(ys[128 * t:128 * (t + 1), :], yb[:, t % 3, :])
        pipeline(T, (0, fetch), (2, turn), (3, hidden), (4, turn_hidden), (5, output))
        fence(k)
        back = sb("back", [128, 8, D])
        free = [None] * 8
        n = 0
        for b in range(NB):
            for i in range(2):
                G.wait(free[n % 8])
                V.wait(k.ind.gather(back[:, n % 8, :], ys, pos[:, i, b:b + 1], 128 * T), V.now())
                free[n % 8] = V.do(vec.scalar_tensor_tensor(out=x3[:, b, :], in0=back[:, n % 8, :],
                                                            scalar=wt[:, b, i:i + 1], in1=x3[:, b, :],
                                                            op0=ALU.mult, op1=ALU.add))
                n += 1
        fence(k)


STAGES = [stage_l0_gnn, stage_l0_ffn, stage_l1_gnn, stage_l1_ffn, stage_l2_gnn, stage_l2_ffn, stage_l3_gnn,
          stage_l3_ffn]


def build(nc, a, out, stages=tuple(range(8))):
    k = make_ctx(nc)
    n = [0]

    def nm(s):
        n[0] += 1
        return f"{s}_{n[0]}"
    k.nm = nm
    constants(k)
    x = nc.alloc_sbuf_tensor("x", [128, NB * D], F)
    both_graphs(k, a, x)
    if 1 not in stages:
        send(k, k.late, k.second, range(k.second.J))
    x3 = x[:, :].rearrange("p (b c) -> p b c", b=NB)
    k.V.do(nc.vector.memset(x[:, 24 * D:], 0.0))
    k.S.wait(k.V.now())
    k.ld.start(x3[:, 0:24, :], a['x'][0:3072, :].rearrange("(b p) c -> p b c", p=128))
    k.ld.start(x[0:LASTP, 24 * D:], a['x'][3072:N, :])
    fence(k)
    for i in stages:
        if i == 7:
            for q in (k.V, k.A, k.P, k.G, k.S):
                q.wait(k.late.all())
            fence(k)
            k.edges.close()
        STAGES[i](k, x[:, :], a)
    k.ld.start(out[0:3072, :].rearrange("(b p) c -> p b c", p=128), x3[:, 0:24, :])
    k.ld.start(out[3072:N, :], x[0:LASTP, 24 * D:])
    fence(k)
    k.S.wait(k.late.all())


_INS = ['x', 'src', 'dst', 'edge_attr_3', 'edge_type_8', 'L0_gnn_Wl1', 'L0_gnn_Wr1', 'L0_gnn_att1', 'L0_gnn_b1', 'L0_gnn_Wl2', 'L0_gnn_Wr2', 'L0_gnn_att2', 'L0_gnn_b2', 'L0_ffn_W_fx', 'L0_ffn_b_fx', 'L0_ffn_W_x', 'L0_ffn_b_x', 'L0_ffn_W_slice', 'L0_ffn_b_slice', 'L0_ffn_W_q', 'L0_ffn_W_k', 'L0_ffn_W_v', 'L0_ffn_W_out', 'L0_ffn_b_out', 'L0_ffn_temperature', 'L1_gnn_weight', 'L1_gnn_h_bias', 'L1_gnn_loop_weight', 'L1_ffn_W_gat', 'L1_ffn_att_src', 'L1_ffn_att_dst', 'L1_ffn_b_gat', 'L1_ffn_ln_gamma', 'L1_ffn_ln_beta', 'L1_ffn_W1', 'L1_ffn_b1', 'L1_ffn_W2', 'L1_ffn_b2', 'L1_ffn_edge_index', 'L2_gnn_W1', 'L2_gnn_b1', 'L2_gnn_W2', 'L2_gnn_b2', 'L2_ffn_router_w', 'L2_ffn_router_b', 'L2_ffn_W1', 'L2_ffn_b1', 'L2_ffn_W2', 'L2_ffn_b2', 'L3_gnn_W', 'L3_gnn_a_src', 'L3_gnn_a_dst', 'L3_gnn_edge_W', 'L3_gnn_edge_b', 'L3_gnn_bias', 'L3_ffn_Wg', 'L3_ffn_bg', 'L3_ffn_W1', 'L3_ffn_b1', 'L3_ffn_W2', 'L3_ffn_b2']


def kernel(**inputs):
    import numpy as _np
    import concourse.bacc as _bacc
    from concourse import mybir as _mybir
    from concourse.bass_utils import run_bass_kernel_spmd as _run

    nc = _bacc.Bacc("TRN2", target_bir_lowering=False, num_devices=1)
    arrays, args = {}, {}
    for name in _INS:
        v = _np.ascontiguousarray(inputs[name])
        arrays[f"in_{name}_dram"] = v
        args[name] = nc.dram_tensor(f"in_{name}_dram", v.shape, _mybir.dt.from_np(v.dtype), kind="ExternalInput").ap()
    out = nc.dram_tensor("out_0_dram", (3125, 256), _mybir.dt.float32, kind="ExternalOutput").ap()
    build(nc, args, out)
    r = _run(nc, [arrays], core_ids=[0])
    return r.results[0]["out_0_dram"]
```

```python
from contextlib import ExitStack

import numpy as np

import concourse.bass as bass
from concourse import mybir

F = mybir.dt.float32
BF = mybir.dt.bfloat16
I32 = mybir.dt.int32
U32 = mybir.dt.uint32
ALU = mybir.AluOpType
ACT = mybir.ActivationFunctionType
AX = mybir.AxisListType.X

N = 3125
NB = 25
D = 256
LASTP = N - 24 * 128
NEG = -1.0e30
FILL = -1000.0


class Queue:

    def __init__(self, nc, eng, name):
        self.nc, self.eng, self.sem, self.n = nc, eng, nc.alloc_semaphore(name), 0
        self.name = self.base = name
        self.gen = 0
        self.seen = {}

    def wait(self, *tokens):
        for tok in tokens:
            if tok is None:
                continue
            if isinstance(tok, list):
                self.wait(*tok)
                continue
            name, sem, value = tok
            if self.seen.get(name, 0) < value:
                self.eng.wait_ge(sem, value)
                self.seen[name] = value

    def do(self, ins):
        ins.then_inc(self.sem, 1)
        self.n += 1
        return (self.name, self.sem, self.n)

    def renew(self):
        if self.n > 4000:
            self.gen += 1
            self.name = f"{self.base}_{self.gen}"
            self.sem, self.n = self.nc.alloc_semaphore(self.name), 0

    def now(self):
        return (self.name, self.sem, self.n) if self.n else None


class Dmas:

    def __init__(self, nc, queue, name, ring):
        self.q, self.name = queue, name
        self.sems = [nc.alloc_semaphore(f"{name}{i}") for i in range(ring)]
        self.count = [0] * ring
        self.k = 0

    def slot(self):
        i = self.k % len(self.sems)
        self.k += 1
        self.q.wait(self.token(i))
        return i

    def token(self, i):
        return (f"{self.name}{i}", self.sems[i], 16 * self.count[i]) if self.count[i] else None

    def start(self, out, in_, small=False):
        i = self.slot()
        self.q.eng.dma_start(out, in_, allow_slow_non_contiguous=small).then_inc(self.sems[i], 16)
        self.count[i] += 1
        return self.token(i)

    def gather(self, out, table, index, rows):
        i = self.slot()
        self.q.eng.indirect_dma_start(
            out=out, out_offset=None, in_=table,
            in_offset=bass.IndirectOffsetOnAxis(ap=index, axis=0),
            bounds_check=rows - 1, oob_is_err=False).then_inc(self.sems[i], 16)
        self.count[i] += 1
        return self.token(i)

    def scatter(self, table, index, in_, rows):
        i = self.slot()
        self.q.eng.indirect_dma_start(
            out=table, out_offset=bass.IndirectOffsetOnAxis(ap=index, axis=0),
            in_=in_, in_offset=None,
            bounds_check=rows - 1, oob_is_err=False).then_inc(self.sems[i], 16)
        self.count[i] += 1
        return self.token(i)

    def all(self):
        return [self.token(i) for i in range(len(self.sems))]


class Ctx:
    pass


def bc(ap, shape):
    return ap.to_broadcast(shape)


def make_ctx(nc):
    k = Ctx()
    k.nc = nc
    k.edges = ExitStack()
    k.V = Queue(nc, nc.vector, "qv")
    k.A = Queue(nc, nc.scalar, "qa")
    k.P = Queue(nc, nc.tensor, "qp")
    k.G = Queue(nc, nc.gpsimd, "qg")
    k.S = Queue(nc, nc.sync, "qs")
    k.ld = Dmas(nc, k.S, "dl", 12)
    k.st = Dmas(nc, k.A, "da", 8)
    k.ind = Dmas(nc, k.G, "dg", 24)
    k.late = Dmas(nc, k.G, "dt", 16)
    k.ps = [nc.alloc_psum_tensor(f"ps{i}", [128, 512], F) for i in range(8)]
    k.pst = [None] * 8
    return k


def fence_but_pool(k):
    toks = [q.now() for q in (k.V, k.A, k.P)] + k.ld.all() + k.st.all()
    for q in (k.V, k.A, k.P, k.S):
        q.wait(toks)
    k.pst = [None] * 8


def fence(k):
    toks = [q.now() for q in (k.V, k.A, k.P, k.G)] + k.ld.all() + k.st.all() + k.ind.all()
    for q in (k.V, k.A, k.P, k.G, k.S):
        q.wait(toks)
    k.pst = [None] * 8
    for q in (k.V, k.A, k.P, k.G):
        q.renew()


def pipeline(n, *steps):
    top = max(lag for lag, _ in steps)
    for i in range(n + top):
        for lag, fn in sorted(steps, key=lambda s: -s[0]):
            if 0 <= i - lag < n:
                fn(i - lag)


class Offsets:

    def __init__(self, k, engine, offs, top):
        self.k, self.engine, self.offs, self.top = k, engine, offs, top
        self.at = None

    def __call__(self, t):
        if self.at != t // 8:
            self.at = t // 8
            n = min(8, self.offs.shape[1] - 8 * self.at)
            _, self.regs = self.k.nc.values_load_multi_w_load_instructions(
                self.offs[0:1, 8 * self.at:8 * self.at + n], engines=[self.engine], min_val=0, max_val=self.top,
                skip_runtime_bounds_check_because="a tile's block is at most 24 by construction")
        return self.regs[t % 8]


def mm(k, out, lhsT, rhs, start=True, stop=True):
    return k.P.do(k.nc.tensor.matmul(out, lhsT, rhs, start=start, stop=stop, skip_group_check=True))


def constants(k):
    nc, V, G = k.nc, k.V, k.G
    al = nc.alloc_sbuf_tensor
    k.ident = al("ident", [128, 128], F)
    k.identb = al("identb", [128, 128], BF)
    k.ltri = al("ltri", [128, 128], F)
    k.lmask = al("lmask", [128, 128], F)
    k.ones = al("ones", [128, 128], F)
    k.iof = al("iof", [128, 128], F)
    k.iob = al("iob", [128, 128], BF)
    k.ltrib = al("ltrib", [128, 128], BF)
    k.onesb = al("onesb", [128, 128], BF)
    a = V.do(nc.vector.memset(k.ones[:, :], 1.0))
    V.do(nc.vector.memset(k.ident[:, :], 0.0))
    b = V.do(nc.vector.memset(k.identb[:, :], 0.0))
    G.wait(a, b)
    t0 = G.do(nc.gpsimd.affine_select(out=k.ident[:, :], in_=k.ident[:, :], compare_op=ALU.not_equal, fill=1.0,
                                      base=0, pattern=[[-1, 128]], channel_multiplier=1))
    t2 = G.do(nc.gpsimd.affine_select(out=k.ltri[:, :], in_=k.ones[:, :], compare_op=ALU.is_gt, fill=0.0,
                                 base=0, pattern=[[1, 128]], channel_multiplier=-1))
    G.do(nc.gpsimd.affine_select(out=k.lmask[:, :], in_=k.ones[:, :], compare_op=ALU.is_gt, fill=0.0,
                                 base=0, pattern=[[-1, 128]], channel_multiplier=1))
    t1 = G.do(nc.gpsimd.iota(k.iof[:, :], pattern=[[1, 128]], base=0, channel_multiplier=0,
                             allow_small_or_imprecise_dtypes=True))
    k.tiles = al("tiles", [128, 576], F)
    G.do(nc.gpsimd.iota(k.tiles[:, :], pattern=[[1, 576]], base=0, channel_multiplier=0,
                        allow_small_or_imprecise_dtypes=True))
    V.wait(t0, t1, t2)
    V.do(nc.vector.tensor_copy(k.ltrib[:, :], k.ltri[:, :]))
    V.do(nc.vector.tensor_copy(k.onesb[:, :], k.ones[:, :]))
    V.do(nc.vector.tensor_copy(k.identb[:, :], k.ident[:, :]))
    V.do(nc.vector.tensor_copy(k.iob[:, :], k.iof[:, :]))
    fence(k)


class EdgeList:

    def __init__(self, k, es, name, J, T, Wd):
        nc = k.nc
        self.name, self.J, self.T, self.Wd = name, J, T, Wd
        self.tab = nc.dram_tensor(f"tab_{name}", (128 * T, Wd), F).ap()

        def al(n, shape, dt):
            return k.edges.enter_context(nc.sbuf_tensor(n, shape, dt))

        def sb(n, shape, dt):
            return es.enter_context(nc.sbuf_tensor(f"{name}_{n}", shape, dt))
        self.st = al(f"st_{name}", [128, 26], F)
        self.cnt = al(f"cnt_{name}", [128, NB], F)
        keep = al if name == "n" else None
        self.pay = keep("n_pay", [128, J, Wd], F) if keep else None
        self.addr = keep("n_addr", [128, J], U32) if keep else None
        self.sb = sb

    def place(self, x, at):
        sb, J = self.sb, self.J
        if self.pay is None:
            self.pay = x[:, at:at + J * self.Wd].rearrange("p (j w) -> p j w", w=self.Wd)
            self.addr = sb("addr", [128, J], U32)
            at += J * self.Wd
        self.lo, self.hi = x[:, at:at + J], x[:, at + J:at + 2 * J]
        at += 2 * J
        if at + J <= x.shape[1]:
            self.inv = x[:, at:at + J]
            return at + J
        self.inv = sb("inv", [128, J], F)
        return at


def split_digits(k, e, load):
    nc, V = k.nc, k.V
    vec = nc.vector
    with ExitStack() as es:
        def sb(n, shape, dt):
            return es.enter_context(nc.sbuf_tensor(f"{e.name}_{n}", shape, dt))
        filla = sb("fill", [128, e.T, e.Wd], F)
        V.do(vec.memset(filla[:, :, :], 0.0))
        V.wait(V.now())
        V.do(vec.memset(filla[:, :, 0], FILL))
        k.S.wait(V.now())
        k.ld.start(e.tab.rearrange("(p r) w -> p (r w)", p=128), filla[:, :, :].rearrange("p a b -> p (a b)"))
        dst = load(sb, e.pay)
        ti = sb("ti", [128, e.J], I32)
        V.wait(V.now())
        V.do(vec.tensor_scalar(ti[:, :], dst[:, :], 127, None, ALU.bitwise_and))
        V.wait(V.now())
        V.do(vec.tensor_copy(e.lo[:, :], ti[:, :]))
        V.wait(V.now())
        V.do(vec.tensor_scalar(ti[:, :], dst[:, :], 7, None, ALU.arith_shift_right))
        V.wait(V.now())
        V.do(vec.tensor_copy(e.hi[:, :], ti[:, :]))
        V.do(vec.tensor_scalar(e.inv[:, :], e.pay[:, :, 0], float(N) - 0.5, 1.0e6, ALU.is_gt, ALU.mult))
        V.wait(V.now())
        V.do(vec.tensor_tensor(e.hi[:, :], e.hi[:, :], e.inv[:, :], ALU.add))
        V.wait(V.now())
        fence(k)


def low_onehots(k, out, lo, t, m):
    return k.nc.vector.tensor_tensor(out, bc(k.iob[:, :].unsqueeze(1), [128, m, 128]),
                                     bc(lo[:, t:t + m].unsqueeze(2), [128, m, 128]), ALU.is_equal)


def sort_edges(k, e, dmas, sent):
    nc, V, A, P, G = k.nc, k.V, k.A, k.P, k.G
    vec = nc.vector
    name, J, T, st, cnt = e.name, e.J, e.T, e.st, e.cnt
    pay, lo, hi, inv, addr = e.pay, e.lo, e.hi, e.inv, e.addr
    with ExitStack() as es:
        def sb(n, shape, dt):
            return es.enter_context(nc.sbuf_tensor(f"{name}_{n}", shape, dt))
        NG = (J + 15) // 16
        ohi = sb("ohi", [128, NG, 16, NB], BF)
        hist = sb("hist", [128, J, NB], BF)
        cum = sb("cum", [128, NB, J + 1], F)
        olo = sb("olo", [128, 12, 128], BF)
        use = [None] * 3
        tko = []
        for g in range(NG):
            w = min(16, J - 16 * g)
            h = ohi[:, g, 0:w, :]
            tko.append(V.do(vec.tensor_tensor(h, bc(k.iof[:, 0:NB].unsqueeze(1), [128, w, NB]),
                                              bc(hi[:, 16 * g:16 * g + w].unsqueeze(2), [128, w, NB]), ALU.is_equal)))
        for g in range(NG):
            w = min(16, J - 16 * g)
            bank = g % 2
            for c in range(w):
                t = 16 * g + c
                b = t % 12
                if t % 4 == 0:
                    m = min(4, J - t)
                    V.wait(use[b // 4])
                    tlo = V.do(low_onehots(k, olo[:, b:b + m, :], lo, t, m))
                P.wait(tlo, tko[g])
                if c == 0:
                    P.wait(k.pst[bank])
                use[b // 4] = mm(k, k.ps[bank][:, c * NB:(c + 1) * NB], olo[:, b, :], ohi[:, g, c, :])
            A.wait(P.now())
            k.pst[bank] = A.do(nc.scalar.copy(hist[:, 16 * g:16 * g + w, :],
                                              k.ps[bank][:, 0:w * NB].rearrange("p (a b) -> p a b", b=NB)))
        V.wait(A.now())
        hv = hist[:, :, :].rearrange("p t b -> p b t")
        V.do(vec.tensor_reduce(cnt[:, :], hv, AX, ALU.add))
        P.wait(V.now(), k.pst[2])
        mm(k, k.ps[2][:, 0:NB], k.ltri[:, :], cnt[:, :])
        mm(k, k.ps[2][:, 32:32 + NB], k.ones[:, :], cnt[:, :])
        V.wait(P.now())
        tot = sb("tot", [128, NB], F)
        toti = sb("toti", [128, NB], I32)
        V.do(vec.tensor_scalar(tot[:, :], k.ps[2][:, 32:32 + NB], 1.0, 127.0, ALU.max, ALU.add))
        V.wait(V.now())
        V.do(vec.tensor_copy(toti[:, :], tot[:, :]))
        V.wait(V.now())
        V.do(vec.tensor_scalar(toti[:, :], toti[:, :], 7, None, ALU.arith_shift_right))
        V.wait(V.now())
        V.do(vec.tensor_copy(tot[:, :], toti[:, :]))
        V.do(vec.memset(st[:, 0:1], 0.0))
        V.wait(V.now())
        V.do(vec.tensor_tensor_scan(st[:, 1:26], k.ones[:, 0:25], tot[:, :], 0.0, ALU.mult, ALU.add))
        V.wait(V.now())
        V.do(vec.scalar_tensor_tensor(out=cum[:, :, 0], in0=st[:, 0:25], scalar=128.0, in1=k.ps[2][:, 0:NB],
                                      op0=ALU.mult, op1=ALU.add))
        V.wait(V.now())
        k.pst[2] = V.now()
        one = sb("one", [128, J], F)
        V.do(vec.memset(one[:, :], 1.0))
        V.wait(V.now())
        for b in range(NB):
            V.do(vec.tensor_tensor_scan(cum[:, b, 1:J + 1], one[:, :], hist[:, :, b], cum[:, b, 0:1],
                                        ALU.mult, ALU.add))
        tcum = V.now()
        NT = (J + 127) // 128
        dT = sb("dT", [128, NT, 128], F)
        P.wait(k.pst[2])
        P.wait(V.now())
        for a in range(NT):
            w = min(128, J - 128 * a)
            P.wait(k.pst[2 + a % 2])
            P.do(nc.tensor.transpose(k.ps[2 + a % 2][0:w, 0:128], pay[:, 128 * a:128 * a + w, 0], k.ident[:, :]))
            A.wait(P.now())
            k.pst[2 + a % 2] = A.do(nc.scalar.copy(dT[0:w, a, :], k.ps[2 + a % 2][0:w, 0:128]))
        tdT = A.now()
        olt = sb("olt", [128, 3, 512], F)
        rank = sb("rank", [128, J], F)
        junk = sb("junk", [128, 4, 128], F)
        prod = sb("prod", [128, 2, 16, NB], F)
        negd = sb("negd", [128, J], F)
        far = sb("far", [128, 4, 128], BF)
        junka = sb("junka", [128, 4, 128], F)
        V.do(vec.tensor_scalar(negd[:, :], pay[:, :, 0], -1.0, None, ALU.mult))
        V.do(vec.tensor_scalar(far[:, :, :], bc(k.lmask[:, :].unsqueeze(1), [128, 4, 128]), -16384.0, 16384.0,
                               ALU.mult, ALU.add))
        P.wait(V.now())
        A.wait(V.now())
        fa = sb("fa", [128, J], F)
        fi = sb("fi", [128, J], I32)
        fj = sb("fj", [128, J], I32)
        fb = sb("fb", [128, J], F)
        use = [None] * 3
        uselt = [None] * 3
        junkt = [None] * 8
        trank = [None]
        tolt = {}
        ready = {}
        tv = {}
        dest = (2, 3, 6, 7)

        def group(g):
            return range(4 * g, min(4 * g + 4, J))

        def first(g):
            V.wait(use[g % 3])
            m = len(group(g))
            tv[g] = V.do(low_onehots(k, olo[:, 4 * (g % 3):4 * (g % 3) + m, :], lo, 4 * g, m))

        def spread(g):
            rb = dest[g % 4]
            P.wait(tdT, k.pst[rb])
            act = g % 3 == 1
            w = 128 * len(group(g))
            if act:
                mm(k, k.ps[rb][:, 0:w], k.identb[:, :], far[:, :, :].rearrange("p a b -> p (a b)")[:, 0:w], stop=False)
            for t in group(g):
                kk = min(128, J - 128 * (t // 128))
                ready[g] = mm(k, k.ps[rb][:, 128 * (t % 4):128 * (t % 4) + 128],
                              bc(k.ident[0:kk, t % 128:t % 128 + 1], [kk, 128]), dT[0:kk, t // 128, :], start=not act)
            P.wait(tv.pop(g), k.pst[g % 2])
            for t in group(g):
                use[g % 3] = P.do(nc.tensor.transpose(k.ps[g % 2][:, 64 * (t % 4):64 * (t % 4) + 64].bitcast(BF),
                                                      olo[:, 4 * (g % 3) + t % 4, :], k.identb[:, :]))

        def second(g):
            w = len(group(g))
            A.wait(use[g % 3], uselt[g % 3])
            k.pst[g % 2] = tolt[g] = A.do(nc.scalar.copy(
                olt[:, g % 3, 0:128 * w], k.ps[g % 2][:, 0:64 * w].bitcast(BF)))

        def compare(g):
            if g % 3 == 1:
                A.wait(ready.pop(g))
                for t in group(g):
                    A.wait(junkt[4 + t % 4])
                    k.pst[dest[g % 4]] = A.do(nc.scalar.activation(
                        junka[:, t % 4, :], k.ps[dest[g % 4]][:, 128 * (t % 4):128 * (t % 4) + 128], ACT.Abs,
                        bias=negd[:, t:t + 1]))
                A.wait(A.now())
                for t in group(g):
                    junkt[4 + t % 4] = trank[0] = A.do(nc.scalar.activation(
                        junka[:, t % 4, :], junka[:, t % 4, :], ACT.Relu, bias=k.ones[:, 0:1], scale=-1.0,
                        accum_out=rank[:, t:t + 1]))
                return
            V.wait(ready.pop(g))
            for t in group(g):
                V.wait(junkt[t % 4])
                k.pst[dest[g % 4]] = junkt[t % 4] = V.do(vec.scalar_tensor_tensor(
                    out=junk[:, t % 4, :], in0=k.ps[dest[g % 4]][:, 128 * (t % 4):128 * (t % 4) + 128],
                    scalar=pay[:, t, 0:1], in1=k.lmask[:, :],
                    op0=ALU.is_equal, op1=ALU.mult, accum_out=rank[:, t:t + 1]))

        def third(g):
            P.wait(tolt.pop(g), tcum)
            for t in group(g):
                lb = 4 + (t // 16) % 2
                c = t % 16
                if c == 0:
                    P.wait(k.pst[lb])
                uselt[g % 3] = mm(k, k.ps[lb][:, c * NB:(c + 1) * NB], olt[:, g % 3, 128 * (t % 4):128 * (t % 4) + 128],
                                  cum[:, :, t])

        def fourth(g4):
            t = group(g4)[-1]
            if t % 16 != 15 and t != J - 1:
                return
            g = t // 16
            w = t % 16 + 1
            lb = 4 + g % 2
            s = slice(16 * g, 16 * g + w)
            V.wait(uselt[g4 % 3], V.now(), trank[0])
            k.pst[lb] = V.do(vec.tensor_tensor(prod[:, g % 2, 0:w, :],
                                               k.ps[lb][:, 0:w * NB].rearrange("p (a b) -> p a b", b=NB),
                                               ohi[:, g, 0:w, :], ALU.mult))
            V.wait(V.now())
            V.do(vec.tensor_reduce(fa[:, s], prod[:, g % 2, 0:w, :], AX, ALU.add))
            V.wait(V.now())
            V.do(vec.tensor_tensor(fi[:, s], fa[:, s], rank[:, s], ALU.add))
            V.wait(V.now())
            V.do(vec.tensor_scalar(fj[:, s], fi[:, s], 7, None, ALU.arith_shift_right))
            V.do(vec.tensor_scalar(fi[:, s], fi[:, s], 127, None, ALU.bitwise_and))
            V.wait(V.now())
            V.do(vec.scalar_tensor_tensor(out=fb[:, s], in0=fi[:, s], scalar=float(T), in1=fj[:, s],
                                          op0=ALU.mult, op1=ALU.add))
            V.wait(V.now())
            tad = V.do(vec.tensor_tensor(addr[:, s], fb[:, s], inv[:, s], ALU.add))
            if 16 * g < sent:
                G.wait(tad)
                send(k, dmas, e, range(16 * g, min(16 * g + w, sent)))
        pipeline((J + 3) // 4, (0, first), (1, spread), (2, second), (3, compare), (3, third), (4, fourth))
        fence_but_pool(k)


def send(k, dmas, e, tiles):
    for u in tiles:
        dmas.scatter(e.tab, e.addr[:, u:u + 1], e.pay[:, u, :], 128 * e.T)


def tile_blocks(k, name, T, st, blk, offsets):
    nc, V = k.nc, k.V
    vec = nc.vector
    with ExitStack() as es:
        io = k.tiles
        tmp = es.enter_context(nc.sbuf_tensor(f"tmp_{name}", [128, T], F))
        V.do(vec.memset(blk[:, :], 0.0))
        for b in range(1, 25):
            V.wait(V.now())
            V.do(vec.scalar_tensor_tensor(out=blk[:, :], in0=io[:, 0:T], scalar=st[:, b:b + 1], in1=blk[:, :],
                                          op0=ALU.is_ge, op1=ALU.add))
        for w, o in offsets:
            V.wait(V.now())
            V.do(vec.tensor_scalar(tmp[:, :], blk[:, :], float(w), None, ALU.mult))
            V.wait(V.now())
            V.do(vec.tensor_copy(o[:, :], tmp[0:1, :]))
        fence(k)


def load_int(k, sb, name, J, src, fill):
    nc, V = k.nc, k.V
    t = sb(name, [128, J], I32)
    V.do(nc.vector.memset(t[:, :], fill))
    k.S.wait(V.now())
    E = src.shape[0]
    c = (E + 127) // 128
    full = E // c
    toks = [k.ld.start(t[0:full, 0:c], src[0:full * c].rearrange("(p c) -> p c", c=c))]
    if E > full * c:
        toks.append(k.ld.start(t[full:full + 1, 0:E - full * c],
                               src[full * c:E].rearrange("(a c) -> a c", a=1)))
    return t, toks


def main_loader(k, src, dst, attr, typ):
    nc, V, G = k.nc, k.V, k.G
    vec = nc.vector
    J = 441

    def load(sb, pay):
        d, t1 = load_int(k, sb, "d", J, dst, 4095)
        s, t2 = load_int(k, sb, "s", J, src, 0)
        y, t3 = load_int(k, sb, "y", J, typ, 0)
        at = sb("at", [128, 416, 3], F)
        V.do(vec.memset(at[:, :, :], 0.0))
        k.S.wait(V.now())
        t4 = [k.ld.start(at[0:127, :, :].rearrange("p a b -> p (a b)"),
                         attr[0:127 * 416, :].rearrange("(p c) w -> p (c w)", c=416)),
              k.ld.start(at[127:128, 0:293, :].rearrange("p a b -> p (a b)"),
                         attr[127 * 416:53125, :].rearrange("(p c) w -> p (c w)", p=1))]
        G.wait(t1, t2, V.now())
        lp = [G.do(nc.gpsimd.iota(x[:, 416:441], pattern=[[1, 25]], base=0, channel_multiplier=25)) for x in (d, s)]
        V.wait(lp, t1, t2, t3, t4)
        V.do(vec.tensor_copy(pay[:, :, 0], d[:, :]))
        V.do(vec.tensor_scalar(pay[:, :, 1], s[:, :], float(N - 1), None, ALU.min))
        V.wait(V.now())
        V.do(vec.scalar_tensor_tensor(out=pay[:, :, 2], in0=y[:, :], scalar=3200.0, in1=pay[:, :, 1],
                                      op0=ALU.mult, op1=ALU.add))
        V.do(vec.memset(pay[:, 0:416, 3], 1.0))
        V.do(vec.memset(pay[:, 416:441, 3:8], 0.0))
        V.do(vec.memset(pay[:, 0:416, 7], 0.0))
        V.do(vec.tensor_copy(pay[:, 0:416, 4:7], at[:, :, :]))
        return d

    return load


def second_loader(k, ei):
    nc, V, G = k.nc, k.V, k.G
    vec = nc.vector
    J = 537

    def load(sb, pay):
        d, t1 = load_int(k, sb, "d", J, ei[1, :], 4095)
        s, t2 = load_int(k, sb, "s", J, ei[0, :], 0)
        G.wait(t1, t2, V.now())
        lp = [G.do(nc.gpsimd.iota(z[:, 512:537], pattern=[[1, 25]], base=0, channel_multiplier=25)) for z in (d, s)]
        V.wait(lp, t1, t2)
        V.do(vec.tensor_copy(pay[:, :, 0], d[:, :]))
        V.do(vec.tensor_scalar(pay[:, :, 1], s[:, :], float(N - 1), None, ALU.min))
        return d
    return load


def both_graphs(k, a, x):

    def al(n, shape, dt):
        return k.edges.enter_context(k.nc.sbuf_tensor(n, shape, dt))
    with ExitStack() as es:
        m = EdgeList(k, es, "m", 441, 464, 8)
        n = EdgeList(k, es, "n", 537, 576, 2)
        k.T, k.T2 = m.T, n.T
        k.second = n
        k.deg = m.cnt
        k.blk = al("blk_m", [128, m.T], F)
        k.off256 = al("off_m256", [1, m.T], I32)
        k.off264 = al("off_m264", [1, m.T], I32)
        k.dlA = al("dlA", [128, m.T], F)
        k.dlR = al("dlR", [128, m.T], F)
        k.xsrc = al("xsrc", [128, m.T], U32)
        k.xtyp = al("xtyp", [128, m.T], U32)
        k.attr = al("attr", [128, m.T, 4], F)
        k.loopneg = al("loopneg", [128, m.T], F)
        n.place(x, m.place(x, 0))
        split_digits(k, m, main_loader(k, a['src'], a['dst'], a['edge_attr_3'], a['edge_type_8']))
        split_digits(k, n, second_loader(k, a['L1_ffn_edge_index']))
        sort_edges(k, m, k.ind, m.J)
        n.sent = 304
        sort_edges(k, n, k.late, n.sent)
        fence(k)
        finish_main(k, m)


def finish_main(k, e):
    nc, V = k.nc, k.V
    vec = nc.vector
    T, tab = e.T, e.tab
    tile_blocks(k, "m", T, e.st, k.blk, ((256, k.off256), (264, k.off264)))
    k.m_flags = edge_flags_dram(k, "m", T)
    with ExitStack() as es:
        p = es.enter_context(nc.sbuf_tensor("sorted_m", [128, T, 8], F))
        V.wait(k.ld.start(p[:, :, :].rearrange("p a b -> p (a b)"), tab.rearrange("(p r) w -> p (r w)", p=128)))
        V.do(vec.tensor_copy(k.xsrc[:, :], p[:, :, 1]))
        V.do(vec.tensor_copy(k.xtyp[:, :], p[:, :, 2]))
        V.do(vec.tensor_copy(k.attr[:, :, 0:3], p[:, :, 4:7]))
        V.do(vec.memset(k.attr[:, :, 3:4], 1.0))
        V.do(vec.scalar_tensor_tensor(out=k.dlA[:, :], in0=k.blk[:, :], scalar=-128.0, in1=p[:, :, 0],
                                      op0=ALU.mult, op1=ALU.add))
        V.do(vec.tensor_scalar(k.loopneg[:, :], p[:, :, 3], 1.0, -NEG, ALU.subtract, ALU.mult))
        V.wait(V.now())
        V.do(vec.tensor_tensor(k.dlR[:, :], k.dlA[:, :], k.loopneg[:, :], ALU.add))
        V.wait(V.now())
        to_rows(k, "mf", p[:, :, 0], T, k.m_flags[128:128 + T * 128])
        fence(k)


def edge_flags_dram(k, name, T):
    nc, V = k.nc, k.V
    d = nc.dram_tensor(f"dsts_{name}", (128 * (T + 2),), F).ap()
    with ExitStack() as es:
        s = es.enter_context(nc.sbuf_tensor(f"sent_{name}", [2, 128], F))
        V.do(nc.vector.memset(s[:, :], -7.0))
        k.S.wait(V.now())
        k.ld.start(d[0:128].rearrange("(a b) -> a b", a=1), s[0:1, :])
        k.ld.start(d[128 * (T + 1):128 * (T + 2)].rearrange("(a b) -> a b", a=1), s[1:2, :])
        fence(k)
    return d


def to_rows(k, name, src, C, dram):
    nc, P, A = k.nc, k.P, k.A
    with ExitStack() as es:
        buf = es.enter_context(nc.sbuf_tensor(f"rows_{name}", [128, 4, 128], F))
        free = [None] * 4
        P.wait(k.V.now())
        for a in range((C + 127) // 128):
            w = min(128, C - 128 * a)
            b = a % 2
            P.wait(k.pst[b])
            P.do(nc.tensor.transpose(k.ps[b][0:w, 0:128], src[:, 128 * a:128 * a + w], k.ident[:, :]))
            A.wait(P.now(), free[a % 4])
            k.pst[b] = A.do(nc.scalar.copy(buf[0:w, a % 4, :], k.ps[b][0:w, 0:128]))
            k.S.wait(A.now())
            free[a % 4] = k.ld.start(dram[128 * 128 * a:128 * (128 * a + w)].rearrange("(q e) -> q e", e=128),
                                     buf[0:w, a % 4, :])
        fence(k)


def from_rows(k, name, dram, C, dst):
    nc, P, A = k.nc, k.P, k.A
    with ExitStack() as es:
        buf = es.enter_context(nc.sbuf_tensor(f"fr_{name}", [128, 4, 128], F))
        free = [None] * 4
        for a in range((C + 127) // 128):
            w = min(128, C - 128 * a)
            b = a % 2
            k.S.wait(free[a % 4])
            t = k.ld.start(buf[0:w, a % 4, :],
                           dram[128 * 128 * a:128 * (128 * a + w)].rearrange("(q e) -> q e", e=128))
            P.wait(t, k.pst[b])
            free[a % 4] = P.do(nc.tensor.transpose(k.ps[b][:, 0:w], buf[0:w, a % 4, :], k.ident[0:w, 0:w]))
            A.wait(P.now())
            k.pst[b] = A.do(nc.scalar.copy(dst[:, 128 * a:128 * a + w], k.ps[b][:, 0:w]))
        fence(k)


def rev(ap):
    return ap[:, ::-1]


def seg_softmax(k, name, L, H, C, T, flags, eps_op, eps):
    nc, V, P, A = k.nc, k.V, k.P, k.A
    vec = nc.vector
    Q = H * C
    r = T // C
    n = r * 128
    dram = nc.dram_tensor(f"soft_{name}", (H * T * 128,), F).ap()
    dram2 = nc.dram_tensor(f"softo_{name}", (H * T * 128,), F).ap()
    to_rows(k, name + "i", L, H * T, dram)
    with ExitStack() as es:
        def sb(nm, shape, dt=F):
            return es.enter_context(nc.sbuf_tensor(f"{name}_{nm}", shape, dt))
        x = sb("x", [128, n])
        d = sb("d", [128, n + 2])
        ks = sb("ks", [128, n], BF)
        ke = sb("ke", [128, n], BF)
        a = sb("a", [128, n])
        b = sb("b", [128, n])
        row = sb("row", [1, 4, 128])
        col = sb("col", [128, 2])
        toks = [k.ld.start(x[0:Q, :], dram.rearrange("(q e) -> q e", q=Q))]
        for h in range(H):
            win = flags[127:127 + C * n].rearrange("(c e) -> c e", c=C)
            toks.append(k.ld.start(d[h * C:(h + 1) * C, 0:n], win))
            win = flags[129:129 + C * n].rearrange("(c e) -> c e", c=C)
            toks.append(k.ld.start(d[h * C:(h + 1) * C, n:n + 2], win[:, n - 2:n]))
        V.wait(toks)
        V.do(vec.tensor_tensor(ks[0:Q, :], d[0:Q, 1:n + 1], d[0:Q, 0:n], ALU.not_equal))
        V.do(vec.tensor_tensor(ke[0:Q, :], d[0:Q, 1:n + 1], d[0:Q, 2:n + 2], ALU.not_equal))
        V.wait(V.now())
        V.do(vec.tensor_reduce(col[0:Q, 0:1], ks[0:Q, :], AX, ALU.max))
        V.do(vec.tensor_reduce(col[0:Q, 1:2], ke[0:Q, :], AX, ALU.max))
        V.wait(V.now())
        anys = sb("anys", [1, 2, 128])
        cc = sb("cc", [128, 4])
        for i in range(2):
            P.wait(V.now(), k.pst[0])
            P.do(nc.tensor.transpose(k.ps[0][0:1, 128 * i:128 * i + Q], col[0:Q, i:i + 1], k.ident[0:Q, 0:Q]))
        V.wait(P.now())
        V.do(vec.tensor_copy(anys[0:1, :, 0:Q], k.ps[0][0:1, 0:256].rearrange("p (a b) -> p a b", a=2)[:, :, 0:Q]))
        V.wait(V.now())
        k.pst[0] = V.now()

        def scans(out, gate, inp, back, op_gate, op_in, init, any_row):
            o, g, i_ = out[0:Q, 0:n], gate[0:Q, 0:n], inp[0:Q, 0:n]
            if back:
                o, g, i_ = rev(o), rev(g), rev(i_)
            V.wait(V.now())
            V.do(vec.tensor_tensor_scan(o, g, i_, init, op_gate, op_in))
            V.wait(V.now())
            last = out[0:Q, 0:1] if back else out[0:Q, n - 1:n]
            P.wait(V.now(), k.pst[0])
            P.do(nc.tensor.transpose(k.ps[0][0:1, 0:Q], last, k.ident[0:Q, 0:Q]))
            V.wait(P.now())
            v = row[0:1, 0, 0:Q]
            V.do(vec.tensor_copy(v, k.ps[0][0:1, 0:Q]))
            gt = row[0:1, 1, 0:Q]
            if op_gate == ALU.add:
                V.do(vec.tensor_scalar(gt, any_row, NEG, None, ALU.mult))
            else:
                V.do(vec.tensor_scalar(gt, any_row, -1.0, 1.0, ALU.mult, ALU.add))
            V.wait(V.now())
            res = row[0:1, 2, 0:Q]
            V.do(vec.memset(res, init))
            V.wait(V.now())
            for h in range(H):
                s = slice(h * C, (h + 1) * C)
                vo, vg, vi = row[0:1, 3, s], row[0:1, 1, s], row[0:1, 0, s]
                if back:
                    vo, vg, vi = rev(vo), rev(vg), rev(vi)
                V.do(vec.tensor_tensor_scan(vo, vg, vi, init, op_gate, op_in))
            V.wait(V.now())
            for h in range(H):
                if back:
                    V.do(vec.tensor_copy(row[0:1, 2, h * C:(h + 1) * C - 1], row[0:1, 3, h * C + 1:(h + 1) * C]))
                else:
                    V.do(vec.tensor_copy(row[0:1, 2, h * C + 1:(h + 1) * C], row[0:1, 3, h * C:(h + 1) * C - 1]))
            P.wait(V.now())
            P.do(nc.tensor.transpose(k.ps[0][0:Q, 0:1], res, k.ident[0:1, 0:1]))
            V.wait(P.now(), V.now())
            V.do(vec.tensor_copy(cc[0:Q, 0:1], k.ps[0][0:Q, 0:1]))
            k.pst[0] = V.now()
            V.wait(V.now())
            V.do(vec.tensor_tensor_scan(o, g, i_, cc[0:Q, 0:1], op_gate, op_in))
            V.wait(V.now())

        aS, aE = anys[0:1, 0, 0:Q], anys[0:1, 1, 0:Q]
        V.do(vec.tensor_scalar(b[0:Q, :], ks[0:Q, :], NEG, None, ALU.mult))
        scans(a, b, x, False, ALU.add, ALU.max, NEG, aS)
        V.do(vec.tensor_scalar(b[0:Q, :], ke[0:Q, :], NEG, None, ALU.mult))
        V.wait(V.now())
        g2 = d
        scans(g2, b, a, True, ALU.add, ALU.max, NEG, aE)
        V.do(vec.tensor_tensor(x[0:Q, :], x[0:Q, :], g2[0:Q, 0:n], ALU.subtract))
        A.wait(V.now())
        V.wait(A.do(nc.scalar.activation(x[0:Q, :], x[0:Q, :], ACT.Exp)))
        V.do(vec.tensor_scalar(b[0:Q, :], ks[0:Q, :], -1.0, 1.0, ALU.mult, ALU.add))
        scans(a, b, x, False, ALU.mult, ALU.add, 0.0, aS)
        V.do(vec.tensor_tensor(a[0:Q, :], a[0:Q, :], ke[0:Q, :], ALU.mult))
        V.do(vec.tensor_scalar(b[0:Q, :], ke[0:Q, :], -1.0, 1.0, ALU.mult, ALU.add))
        scans(g2, b, a, True, ALU.mult, ALU.add, 0.0, aE)
        if eps_op is not None:
            V.do(vec.tensor_scalar(g2[0:Q, 0:n], g2[0:Q, 0:n], eps, None, eps_op))
            V.wait(V.now())
        V.do(vec.reciprocal(g2[0:Q, 0:n], g2[0:Q, 0:n]))
        V.wait(V.now())
        V.do(vec.tensor_tensor(x[0:Q, :], x[0:Q, :], g2[0:Q, 0:n], ALU.mult))
        k.S.wait(V.now())
        k.ld.start(dram2.rearrange("(q e) -> q e", q=Q), x[0:Q, :])
        fence(k)
    from_rows(k, name + "o", dram2, H * T, L)


def rows_of(ap):
    return ap[:].rearrange("(a c) -> a c", a=1)


def layernorm(k, x, out):
    nc, V, A = k.nc, k.V, k.A
    vec = nc.vector
    x3 = x.rearrange("p (b c) -> p b c", b=NB)
    o3 = out.rearrange("p (b c) -> p b c", b=NB)
    with ExitStack() as es:
        mu = es.enter_context(nc.sbuf_tensor(k.nm("mu"), [128, NB], F))
        va = es.enter_context(nc.sbuf_tensor(k.nm("va"), [128, NB], F))
        junk = es.enter_context(nc.sbuf_tensor(k.nm("junk"), [128, 2, D], F))
        V.do(vec.tensor_reduce(mu[:, :], x3, AX, ALU.add))
        V.wait(V.now())
        V.do(vec.tensor_scalar(mu[:, :], mu[:, :], 1.0 / D, None, ALU.mult))
        V.wait(V.now())
        for b in range(NB):
            t = V.do(vec.tensor_scalar(o3[:, b, :], x3[:, b, :], mu[:, b:b + 1], None, ALU.subtract))
            A.wait(t)
            A.wait(A.now())
            A.do(nc.scalar.activation(junk[:, b % 2, :], o3[:, b, :], ACT.Square, accum_out=va[:, b:b + 1]))
        V.wait(A.now())
        V.do(vec.tensor_scalar(va[:, :], va[:, :], 1.0 / D, 1e-5, ALU.mult, ALU.add))
        A.wait(V.now())
        A.do(nc.scalar.activation(va[:, :], va[:, :], ACT.Sqrt))
        V.wait(A.now())
        V.do(vec.reciprocal(va[:, :], va[:, :]))
        V.wait(V.now())
        for b in range(NB):
            V.do(vec.tensor_scalar(o3[:, b, :], o3[:, b, :], va[:, b:b + 1], None, ALU.mult))
        fence(k)


def transpose_rows(k, x, xT, banks=(0, 1)):
    nc, P, A, V = k.nc, k.P, k.A, k.V
    P.wait(V.now(), A.now())
    i = 0
    for c in range(2):
        for b0 in range(0, NB, 4):
            w = min(4, NB - b0)
            bk = banks[i % len(banks)]
            P.wait(k.pst[bk])
            for j in range(w):
                b = b0 + j
                P.do(nc.tensor.transpose(k.ps[bk][:, 128 * j:128 * (j + 1)],
                                         x[:, b * D + c * 128:b * D + c * 128 + 128], k.ident[:, :]))
            E, f = (A, nc.scalar.copy) if i % 2 else (V, nc.vector.tensor_copy)
            E.wait(P.now())
            k.pst[bk] = E.do(f(xT[:, c, 128 * b0:128 * (b0 + w)], k.ps[bk][:, 0:128 * w]))
            i += 1
    P.wait(A.now(), V.now())


def load_w(k, dst, src):
    for c in range(2):
        k.ld.start(dst[:, c, :], src[128 * c:128 * (c + 1), :])
    return k.ld.all()


def project(k, xT, w, M, sink, banks=(2, 3, 4, 5)):
    i = 0
    for b in range(NB):
        for m0 in range(0, M, 512):
            mw = min(512, M - m0)
            bk = banks[i % len(banks)]
            i += 1
            k.P.wait(k.pst[bk])
            for c in range(2):
                mm(k, k.ps[bk][:, 0:mw], xT[:, c, 128 * b:128 * (b + 1)], w[:, c, m0:m0 + mw],
                   start=(c == 0), stop=(c == 1))
            k.pst[bk] = sink(b, m0, mw, k.ps[bk][:, 0:mw])


def copy_sink(k, dst, M):
    n = [0]

    def sink(b, m0, mw, ps):
        E, f = (k.A, k.nc.scalar.copy) if n[0] % 2 else (k.V, k.nc.vector.tensor_copy)
        n[0] += 1
        E.wait(k.P.now())
        return E.do(f(dst[:, b * M + m0:b * M + m0 + mw], ps))
    return sink


def dram_sink(k, es, dram, M):
    buf = es.enter_context(k.nc.sbuf_tensor(k.nm("tb"), [128, 6, 512], F))
    free = [None] * 6
    n = [0]

    def sink(b, m0, mw, ps):
        i = n[0] % 6
        E, f = (k.A, k.nc.scalar.copy) if n[0] % 2 else (k.V, k.nc.vector.tensor_copy)
        n[0] += 1
        E.wait(k.P.now(), free[i])
        t = E.do(f(buf[:, i, 0:mw], ps))
        k.S.wait(t)
        free[i] = []
        for j in range(0, mw, D):
            r = 3200 * ((m0 + j) // D) + 128 * b
            free[i].append(k.ld.start(dram[r:r + 128, :], buf[:, i, j:j + min(D, mw)]))
        return t
    return sink


def bcast_row(k, es, vecap, M):
    t = es.enter_context(k.nc.sbuf_tensor(k.nm("bc"), [128, M], F))
    k.ld.start(t[:, :], vecap.partition_broadcast(128))
    return t


def onehot(k, buf, dl, t, weight=None):
    if weight is None:
        return k.V.do(k.nc.vector.tensor_scalar(buf, k.iof[:, :], dl[:, t:t + 1], None, ALU.is_equal))
    return k.V.do(k.nc.vector.tensor_scalar(buf, k.iof[:, :], dl[:, t:t + 1], weight, ALU.is_equal, ALU.mult))


def onehots(k, buf, dl, t):
    return k.V.do(k.nc.vector.tensor_tensor(buf, bc(k.iof[:, :].unsqueeze(1), [128, 4, 128]),
                                            bc(dl[:, t:t + 4].unsqueeze(2), [128, 4, 128]), ALU.is_equal))


def is_kept(t):
    return t % 4 >= 2


def seg_sum(k, T, table, rows, idx, dl, offs, acc, Rw=D, alpha=None, H=1, kept=None):
    nc, V, P, G, A = k.nc, k.V, k.P, k.G, k.A
    vec = nc.vector
    R = 16
    with ExitStack() as es:
        g = es.enter_context(nc.sbuf_tensor(k.nm("g"), [128, R, Rw], F))
        oh = es.enter_context(nc.sbuf_tensor(k.nm("oh"), [128, 8, 128], F))
        V.do(vec.memset(acc[:, :], 0.0))
        freeg = [None] * R
        freeo = [None] * 8
        tg, to, tp = {}, {}, {}
        tadd = [V.now()]
        off = Offsets(k, mybir.EngineType.DVE, offs, 24 * D)
        if alpha is not None:
            av = alpha.rearrange("p (h t) -> p h t", h=H)

        def fetch(t):
            if kept is not None and is_kept(t):
                if not is_kept(t - 1):
                    k.S.wait(freeg[t % R], freeg[t % R + 1])
                    tg[t] = tg[t + 1] = k.ld.start(g[:, t % R:t % R + 2, :], kept[t // 4])
                return
            G.wait(freeg[t % R])
            tg[t] = k.ind.gather(g[:, t % R, :], table, idx[:, t:t + 1], rows)

        def mark(t):
            if alpha is not None and H == 1:
                V.wait(freeo[t % 8])
                to[t] = onehot(k, oh[:, t % 8, :], dl, t, alpha[:, t:t + 1])
            elif t % 4 == 0:
                V.wait(freeo[t % 8 + 3])
                to[t] = to[t + 1] = to[t + 2] = to[t + 3] = onehots(k, oh[:, t % 8:t % 8 + 4, :], dl, t)

        def weigh(t):
            if t % (2 if H == 4 else 3):
                V.wait(tg[t])
                gv = g[:, t % R, 0:D].rearrange("p (h c) -> p h c", h=H)
                tg[t] = V.do(vec.tensor_tensor(gv, gv, bc(av[:, :, t:t + 1], [128, H, D // H]), ALU.mult))
            else:
                A.wait(tg[t])
                for h in range(H):
                    gh = g[:, t % R, D // H * h:D // H * (h + 1)]
                    tg[t] = A.do(nc.scalar.mul(gh, gh, alpha[:, T * h + t:T * h + t + 1]))

        def product(t):
            P.wait(to.pop(t), tg.pop(t), k.pst[t % 6])
            tp[t] = freeg[t % R] = freeo[t % 8] = mm(k, k.ps[t % 6][:, 0:D], oh[:, t % 8, :], g[:, t % R, 0:D])

        def add(t):
            d = acc[:, bass.ds(off(t), D)]
            V.wait(tp.pop(t), tadd[0])
            k.pst[t % 6] = tadd[0] = V.do(vec.tensor_tensor(d, d, k.ps[t % 6][:, 0:D], ALU.add))
        steps = [(0, fetch), (0, mark), (1, product), (4, add)]
        if H > 1:
            steps.insert(1, (0, weigh))
        pipeline(T, *steps)
        fence(k)


class DstRows:

    def __init__(self, k, es, dl, offs, src, width, used):
        nc = k.nc
        self.k, self.dl, self.src, self.width, self.used = k, dl, src, width, used
        self.off = Offsets(k, mybir.EngineType.PE, offs, 24 * width)
        self.oh = es.enter_context(nc.sbuf_tensor(k.nm("oh"), [128, 8, 128], BF))
        self.ot = es.enter_context(nc.sbuf_tensor(k.nm("ot"), [128, 3, 512], F))
        self.fo = [None] * 2
        self.ft = [None] * 3
        self.tt = [None] * 3

    def mark(self, t):
        if t % 4:
            return
        k, nc, g = self.k, self.k.nc, t // 4
        b = g % 2
        k.V.wait(self.fo[b])
        to = onehots(k, self.oh[:, 4 * b:4 * b + 4, :], self.dl, t)
        k.P.wait(to, k.pst[b])
        for u in range(4):
            self.fo[b] = k.P.do(nc.tensor.transpose(k.ps[b][:, 64 * u:64 * u + 64].bitcast(BF),
                                                    self.oh[:, 4 * b + u, :], k.identb[:, :]))

    def turn(self, t):
        if t % 4:
            return
        k, nc, g = self.k, self.k.nc, t // 4
        k.A.wait(self.fo[g % 2], self.ft[g % 3])
        k.pst[g % 2] = self.tt[g % 3] = k.A.do(nc.scalar.copy(
            self.ot[:, g % 3, :], k.ps[g % 2][:, 0:256].bitcast(BF)))

    def spread(self, t, out, stop=True):
        k, i = self.k, (t // 4) % 3
        r = self.src[:, bass.ds(self.off(t), self.used)]
        k.P.wait(self.tt[i])
        self.ft[i] = mm(k, out, self.ot[:, i, 128 * (t % 4):128 * (t % 4) + 128], r, stop=stop)
        return self.ft[i]


def gatv2_logits(k, T, table, xr, att8, H, L, kept):
    nc, V, P, G, A = k.nc, k.V, k.P, k.G, k.A
    vec = nc.vector
    R = 16
    W = D + H
    with ExitStack() as es:
        def sb(n, shape, dt=F):
            return es.enter_context(nc.sbuf_tensor(k.nm(n), shape, dt))
        g = sb("g", [128, R, W])
        r = sb("r", [128, 6, D])
        lin = sb("lin", [128, T, H])
        rows = DstRows(k, es, k.dlA, k.off264, xr, 264, W)
        free = [None] * R
        stored = [None] * R
        rfree = [None] * 6
        tg, tm, tr, tx = {}, {}, {}, {}
        Lv = L.rearrange("p (h t) -> p h t", h=H)

        def fetch(t):
            G.wait(free[t % R], stored[t % R])
            tg[t] = k.ind.gather(g[:, t % R, :], table, k.xsrc[:, t:t + 1], 3200)
            if is_kept(t) and not is_kept(t + 1):
                k.S.wait(tg[t - 1], tg[t])
                s = k.ld.start(kept[t // 4], g[:, t % R - 1:t % R + 1, :])
                stored[t % R] = stored[t % R - 1] = s

        def join(t):
            bk = 2 + t % 6
            P.wait(k.pst[bk])
            rows.spread(t, k.ps[bk][:, 0:W], stop=False)
            P.wait(tg.pop(t))
            tm[t] = free[t % R] = mm(k, k.ps[bk][:, 0:W], k.ident[:, :], g[:, t % R, :], start=False)

        def relu(t):
            bk = 2 + t % 6
            A.wait(tm.pop(t), rfree[t % 6])
            tr[t] = A.do(nc.scalar.activation(r[:, t % 6, :], k.ps[bk][:, 0:D], ACT.Relu))
            k.pst[bk] = A.do(nc.scalar.copy(lin[:, t, :], k.ps[bk][:, D:W]))

        def weigh(t):
            V.wait(tr.pop(t))
            x = r[:, t % 6, :]
            if H == 1:
                rfree[t % 6] = V.do(vec.tensor_tensor_reduce(x, x, att8[:, :], 1.0, 0.0, ALU.mult, ALU.add,
                                                             L[:, t:t + 1]))
            else:
                tx[t] = V.do(vec.tensor_tensor(x, x, att8[:, :], ALU.mult))

        def total(t):
            V.wait(tx.pop(t))
            rfree[t % 6] = V.do(vec.tensor_reduce(Lv[:, :, t], r[:, t % 6, :].rearrange("p (h c) -> p h c", h=H),
                                                  AX, ALU.add))
        steps = [(0, fetch), (0, rows.mark), (2, rows.turn), (5, join), (6, relu), (8, weigh)]
        if H > 1:
            steps.append((9, total))
        pipeline(T, *steps)
        V.wait(A.now(), V.now())
        V.do(vec.tensor_tensor(Lv, Lv, lin[:, :, :].rearrange("p t h -> p h t"), ALU.add))
        fence(k)


def gat_layer(k, name, xT, Wl, Wr, att, H, acc):
    nc = k.nc
    T = k.T
    V, A, P = k.V, k.A, k.P
    vec = nc.vector
    W = D + H
    table = nc.dram_tensor("xl_" + name, (3200, W), F).ap()
    kept = nc.dram_tensor("kept_" + name, (T // 4, 128, 2, W), F).ap()
    with ExitStack() as es:
        def sb(n, shape, dt=F):
            return es.enter_context(nc.sbuf_tensor(k.nm(n), shape, dt))
        L = sb("L", [128, H * T])
        with ExitStack() as e2:
            def s2(n, shape, dt=F):
                return e2.enter_context(nc.sbuf_tensor(k.nm(n), shape, dt))
            xr = s2("xr", [128, NB * 264])
            att8 = bcast_row(k, e2, att, D)
            wl = e2.enter_context(nc.sbuf_tensor(k.nm("wl"), [128, 2, D], F))
            wr = e2.enter_context(nc.sbuf_tensor(k.nm("wr"), [128, 2, D], F))
            att2 = e2.enter_context(nc.sbuf_tensor(k.nm("att2"), [128, D], F))
            buf = e2.enter_context(nc.sbuf_tensor(k.nm("buf"), [128, 6, W], F))
            tmp = e2.enter_context(nc.sbuf_tensor(k.nm("tmp"), [128, 4, D], F))
            load_w(k, wl, Wl)
            P.wait(load_w(k, wr, Wr))
            V.wait(k.ld.all())
            V.do(vec.tensor_scalar(att2[:, :], att8[:, :], 0.2, None, ALU.mult))
            V.wait(V.now())
            V.do(vec.tensor_scalar(att8[:, :], att8[:, :], 0.8, None, ALU.mult))
            n = [0]
            tfree = [None] * 4

            def widen(dst, ps):
                i = n[0] % 4
                n[0] += 1
                A.wait(P.now())
                t = A.do(nc.scalar.copy(dst[:, 0:D], ps))
                V.wait(t)
                V.do(vec.tensor_tensor(tmp[:, i, :], dst[:, 0:D], att2[:, :], ALU.mult))
                V.wait(V.now())
                V.do(vec.tensor_reduce(dst[:, D:W], tmp[:, i, :].rearrange("p (h c) -> p h c", h=H), AX, ALU.add))
                return t
            free = [None] * 6
            stores = []

            def table_sink(b, m0, mw, ps):
                A.wait(free[b % 6])
                t = widen(buf[:, b % 6, :], ps)
                k.S.wait(t, V.now())
                free[b % 6] = k.ld.start(table[128 * b:128 * (b + 1), :], buf[:, b % 6, :])
                stores.append(free[b % 6])
                return t

            def xr_sink(b, m0, mw, ps):
                return widen(xr[:, 264 * b:264 * b + W], ps)
            project(k, xT, wl, D, table_sink)
            project(k, xT, wr, D, xr_sink)
            k.G.wait(stores)
            P.wait(V.now(), A.now())
            gatv2_logits(k, T, table, xr, att8, H, L[:, :], kept)
        seg_softmax(k, name, L[:, :], H, 29 if H == 4 else 116, T, k.m_flags, None, 0)
        seg_sum(k, T, table, 3200, k.xsrc, k.dlA, k.off256, acc, Rw=W, alpha=L[:, :], H=H,
                kept=kept)


def add_bias(k, acc, bias_ap):
    with ExitStack() as es:
        b = bcast_row(k, es, bias_ap, D)
        k.V.wait(k.ld.all(), k.V.now())
        a3 = acc.rearrange("p (b c) -> p b c", b=NB)
        k.V.do(k.nc.vector.tensor_tensor(a3, a3, bc(b[:, :].unsqueeze(1), [128, NB, D]), ALU.add))
        fence(k)


def stage_l0_gnn(k, x, a):
    nc, V, A = k.nc, k.V, k.A
    vec = nc.vector
    with ExitStack() as es:
        def sb(n, shape, dt=F):
            return es.enter_context(nc.sbuf_tensor(k.nm(n), shape, dt))
        h = sb("h", [128, NB * D])
        xT = sb("xT", [128, 2, 3200])
        layernorm(k, x, h[:, :])
        transpose_rows(k, h, xT)
        fence(k)
        gat_layer(k, "g1", xT, a['L0_gnn_Wl1'], a['L0_gnn_Wr1'],
                  a['L0_gnn_att1'].rearrange("h c -> (h c)"), 4, h)
        add_bias(k, h[:, :], a['L0_gnn_b1'])
        with ExitStack() as e2:
            t = e2.enter_context(nc.sbuf_tensor(k.nm("t"), [128, NB * D], F))
            V.do(vec.tensor_scalar(t[:, :], h[:, :], 0.0, None, ALU.min))
            A.wait(V.now())
            A.do(nc.scalar.activation(t[:, :], t[:, :], ACT.Exp))
            V.wait(A.now())
            V.do(vec.tensor_scalar(t[:, :], t[:, :], -1.0, None, ALU.add))
            V.wait(V.now())
            V.do(vec.scalar_tensor_tensor(out=h[:, :], in0=h[:, :], scalar=0.0, in1=t[:, :],
                                          op0=ALU.max, op1=ALU.add))
            fence(k)
        transpose_rows(k, h, xT)
        fence(k)
        gat_layer(k, "g2", xT, a['L0_gnn_Wl2'], a['L0_gnn_Wr2'],
                  a['L0_gnn_att2'].rearrange("h c -> (h c)"), 1, h)
        add_bias(k, h[:, :], a['L0_gnn_b2'])
        V.do(vec.tensor_tensor(x, x, h[:, :], ALU.add))
        fence(k)


def stage_l0_ffn(k, x, a):
    nc, V, A, P = k.nc, k.V, k.A, k.P
    vec = nc.vector
    send(k, k.late, k.second, range(k.second.sent, k.second.J))
    with ExitStack() as es:
        def sb(n, shape, dt=F):
            return es.enter_context(nc.sbuf_tensor(k.nm(n), shape, dt))
        sw = sb("sw", [128, NB, 512])
        Pm = sb("Pm", [128, 4, D])
        with ExitStack() as e2:
            def s2(n, shape, dt=F):
                return e2.enter_context(nc.sbuf_tensor(k.nm(n), shape, dt))
            xT = s2("xT", [128, 2, 3200])
            with ExitStack() as e3:
                xn = e3.enter_context(nc.sbuf_tensor(k.nm("xn"), [128, NB * D], F))
                layernorm(k, x, xn[:, :])
                transpose_rows(k, xn, xT)
                fence(k)
            wfx = s2("wfx", [128, 2, 512])
            wx = s2("wx", [128, 2, 512])
            load_w(k, wfx, a['L0_ffn_W_fx'])
            load_w(k, wx, a['L0_ffn_W_x'])
            bfx = bcast_row(k, e2, a['L0_ffn_b_fx'], 512)
            bxc = s2("bxc", [128, 4])
            k.ld.start(bxc[:, :], a['L0_ffn_b_x'].rearrange("(c p) -> p c", p=128), small=True)
            ws = s2("ws", [128, 128])
            V.do(vec.memset(ws[:, :], 0.0))
            k.S.wait(V.now())
            k.ld.start(ws[0:64, 0:64], a['L0_ffn_W_slice'])
            k.ld.start(ws[64:128, 64:128], a['L0_ffn_W_slice'])
            bs = bcast_row(k, e2, a['L0_ffn_b_slice'], 64)
            tp = bcast_row(k, e2, a['L0_ffn_temperature'].rearrange("a h b c -> (a h b c)"), 8)
            V.wait(k.ld.all())
            P.wait(k.ld.all())
            A.wait(k.ld.all())
            V.do(vec.tensor_scalar(tp[:, :], tp[:, :], 0.1, 5.0, ALU.max, ALU.min))
            V.wait(V.now())
            V.do(vec.reciprocal(tp[:, :], tp[:, :]))
            xm = s2("xm", [128, 2, 4, 512])
            fx = s2("fx", [128, 4, 8, 65])
            V.do(vec.memset(fx[:, :, :, :], 1.0))
            mx = s2("mx", [128, 4, 8])
            V.wait(V.now())
            pst = k.pst
            tok8 = [k.ps[6][0:64, :], k.ps[7][0:64, :]]
            fxfree = [None] * 4
            xmfree = [None] * 2
            txm, tex, tfx, tsw = {}, {}, {}, {}

            def step(ins):
                V.do(ins)
                V.wait(V.now())

            def middle(b):
                if b % 4:
                    return
                ch = b // 4
                t0, tw = 512 * ch, min(512, 3200 - 512 * ch)
                for i in range(4):
                    bk = i % 2
                    P.wait(pst[bk])
                    for c in range(2):
                        mm(k, k.ps[bk][:, 0:tw], wx[:, c, 128 * i:128 * (i + 1)], xT[:, c, t0:t0 + tw],
                           start=(c == 0), stop=(c == 1))
                    A.wait(P.now(), xmfree[ch % 2])
                    pst[bk] = txm[ch] = A.do(nc.scalar.activation(xm[:, ch % 2, i, 0:tw], k.ps[bk][:, 0:tw],
                                                                  ACT.Identity, bias=bxc[:, i:i + 1]))

            def scores(b):
                ch, j, bk = b // 4, b % 4, 2 + b % 2
                P.wait(txm[ch], pst[bk])
                for i in range(4):
                    xmfree[ch % 2] = mm(k, k.ps[bk][:, 128 * i:128 * (i + 1)],
                                        xm[:, ch % 2, i, 128 * j:128 * (j + 1)], ws[:, :])
                w3 = sw[:, b, :].rearrange("p (h g) -> p h g", h=8)
                m = mx[:, b % 4, :]
                V.wait(P.now())
                pst[bk] = V.do(vec.tensor_tensor(w3, k.ps[bk][:, :].rearrange("p (h g) -> p h g", h=8),
                                                 bc(bs[:, :].unsqueeze(1), [128, 8, 64]), ALU.add))
                V.wait(V.now())
                step(vec.tensor_tensor(w3, w3, bc(tp[:, :].unsqueeze(2), [128, 8, 64]), ALU.mult))
                step(vec.tensor_reduce(m, w3, AX, ALU.max))
                step(vec.tensor_tensor(w3, w3, bc(m.unsqueeze(2), [128, 8, 64]), ALU.subtract))
                A.wait(V.now())
                tex[b] = A.do(nc.scalar.activation(sw[:, b, :], sw[:, b, :], ACT.Exp))

            def values(b):
                fk = 4 + b % 2
                P.wait(pst[fk])
                for c in range(2):
                    mm(k, k.ps[fk][:, :], xT[:, c, 128 * b:128 * (b + 1)], wfx[:, c, :],
                       start=(c == 0), stop=(c == 1))
                V.wait(P.now(), fxfree[b % 4])
                pst[fk] = tfx[b] = V.do(vec.tensor_tensor(fx[:, b % 4, :, 0:64],
                                                          k.ps[fk][:, :].rearrange("p (h g) -> p h g", h=8),
                                                          bfx[:, :].rearrange("p (h g) -> p h g", h=8), ALU.add))

            def weights(b):
                w3 = sw[:, b, :].rearrange("p (h g) -> p h g", h=8)
                m = mx[:, b % 4, :]
                V.wait(tex.pop(b))
                step(vec.tensor_reduce(m, w3, AX, ALU.add))
                step(vec.reciprocal(m, m))
                step(vec.tensor_tensor(w3, w3, bc(m.unsqueeze(2), [128, 8, 64]), ALU.mult))
                tsw[b] = V.now()

            def pool(b):
                P.wait(tsw.pop(b), tfx.pop(b))
                kp = 128 if b < 24 else LASTP
                for h in range(8):
                    fxfree[b % 4] = mm(k, tok8[h // 4][:, 65 * (h % 4):65 * (h % 4) + 65],
                                       sw[0:kp, b, 64 * h:64 * h + 64], fx[0:kp, b % 4, h, :],
                                       start=(b == 0 and h % 4 == 0), stop=(b == 24))
            pipeline(NB, (0, middle), (1, scores), (1, values), (2, weights), (3, pool))
            fence(k)
            wq = s2("wq", [64, 64])
            wk = s2("wk", [64, 64])
            wv = s2("wv", [64, 64])
            wo = s2("wo", [64, 8, D])
            for t, n in ((wq, 'q'), (wk, 'k'), (wv, 'v')):
                k.ld.start(t[:, :], a['L0_ffn_W_' + n])
            k.ld.start(wo[:, :, :], a['L0_ffn_W_out'].rearrange("(h c) n -> c h n", c=64))
            P.wait(k.ld.all())
            st = s2("st", [64, 8, 65])
            nr = s2("nr", [64, 8])
            stT = s2("stT", [64, 8, 64])
            qT = s2("qT", [64, 8, 64])
            kT = s2("kT", [64, 8, 64])
            vv = s2("vv", [64, 8, 64])
            at = s2("at", [64, 8, 64])
            atT = s2("atT", [64, 8, 64])
            oT = s2("oT", [64, 8, 64])
            am = s2("am", [64, 8])

            def vs(op, *args, **kw):
                V.wait(V.now())
                V.do(op(*args, **kw))
                V.wait(V.now())
            for i in range(2):
                vs(vec.tensor_copy, st[:, 4 * i:4 * i + 4, :],
                                   tok8[i][:, 0:260].rearrange("p (h c) -> p h c", h=4))
            vs(vec.tensor_scalar, nr[:, :], st[:, :, 64], 1e-5, None, ALU.add)
            vs(vec.reciprocal, nr[:, :], nr[:, :])
            vs(vec.tensor_tensor, st[:, :, 0:64], st[:, :, 0:64], bc(nr[:, :].unsqueeze(2), [64, 8, 64]), ALU.mult)

            def heads(fn, dst, bank):
                P.wait(V.now(), A.now())
                for h in range(8):
                    fn(h, k.ps[bank][0:64, 64 * h:64 * h + 64])
                vs_wait = P.now()
                V.wait(vs_wait)
                vs(vec.tensor_copy, dst[:, :, :], k.ps[bank][0:64, :].rearrange("p (h c) -> p h c", h=8))
            i64 = k.ident[0:64, 0:64]
            heads(lambda h, o: P.do(nc.tensor.transpose(o, st[:, h, 0:64], i64)), stT, 0)
            heads(lambda h, o: mm(k, o, wq[:, :], stT[:, h, :]), qT, 1)
            heads(lambda h, o: mm(k, o, wk[:, :], stT[:, h, :]), kT, 2)
            heads(lambda h, o: mm(k, o, stT[:, h, :], wv[:, :]), vv, 3)
            heads(lambda h, o: mm(k, o, qT[:, h, :], kT[:, h, :]), at, 4)
            vs(vec.tensor_scalar, at[:, :, :], at[:, :, :], 0.125, None, ALU.mult)
            vs(vec.tensor_reduce, am[:, :], at[:, :, :], AX, ALU.max)
            vs(vec.tensor_tensor, at[:, :, :], at[:, :, :], bc(am[:, :].unsqueeze(2), [64, 8, 64]), ALU.subtract)
            A.wait(V.now())
            A.do(nc.scalar.activation(at[:, :, :], at[:, :, :], ACT.Exp))
            V.wait(A.now())
            vs(vec.tensor_reduce, am[:, :], at[:, :, :], AX, ALU.add)
            vs(vec.reciprocal, am[:, :], am[:, :])
            vs(vec.tensor_tensor, at[:, :, :], at[:, :, :], bc(am[:, :].unsqueeze(2), [64, 8, 64]), ALU.mult)
            heads(lambda h, o: P.do(nc.tensor.transpose(o, at[:, h, :], i64)), atT, 0)
            heads(lambda h, o: mm(k, o, vv[:, h, :], atT[:, h, :]), oT, 1)
            P.wait(V.now())
            pp = s2("pp", [64, 8, D])
            for h in range(8):
                bk = h % 2
                P.wait(k.pst[bk])
                mm(k, k.ps[bk][0:64, 0:D], oT[:, h, :], wo[:, h, :])
                V.wait(P.now())
                k.pst[bk] = V.do(vec.tensor_copy(pp[:, h, :], k.ps[bk][0:64, 0:D]))
            k.S.wait(V.now())
            for h in range(8):
                k.ld.start(Pm[64 * (h % 2):64 * (h % 2) + 64, h // 2, :], pp[:, h, :])
            fence(k)
        bo = bcast_row(k, es, a['L0_ffn_b_out'], D)
        V.wait(k.ld.all())
        wT = sb("wT", [128, 3, 4, 128])
        x3 = x.rearrange("p (b c) -> p b c", b=NB)
        wfree = [None] * 3
        tw = {}

        def turn(b):
            bk = b % 2
            P.wait(k.pst[bk])
            for i in range(4):
                P.do(nc.tensor.transpose(k.ps[bk][:, 128 * i:128 * (i + 1)], sw[:, b, 128 * i:128 * (i + 1)],
                                         k.ident[:, :]))
            A.wait(P.now(), wfree[b % 3])
            k.pst[bk] = tw[b] = A.do(nc.scalar.copy(wT[:, b % 3, :, :].rearrange("p a b -> p (a b)"),
                                                    k.ps[bk][:, :]))

        def apply(b):
            bk = 2 + b % 2
            P.wait(tw.pop(b), k.pst[bk])
            for i in range(4):
                wfree[b % 3] = mm(k, k.ps[bk][:, 0:D], wT[:, b % 3, i, :], Pm[:, i, :], start=(i == 0),
                                  stop=(i == 3))
            V.wait(P.now())
            k.pst[bk] = V.do(vec.tensor_tensor(x3[:, b, :], x3[:, b, :], k.ps[bk][:, 0:D], ALU.add))
            V.wait(V.now())
            V.do(vec.tensor_tensor(x3[:, b, :], x3[:, b, :], bo[:, :], ALU.add))
        pipeline(NB, (0, turn), (1, apply))
        fence(k)


def stage_l1_gnn(k, x, a):
    nc, V, A, P = k.nc, k.V, k.A, k.P
    vec = nc.vector
    s = float(np.sqrt(np.float32(0.5)))
    table = nc.dram_tensor("hx_rel", (8 * 3200, D), F).ap()
    with ExitStack() as es:
        def sb(n, shape, dt=F):
            return es.enter_context(nc.sbuf_tensor(k.nm(n), shape, dt))
        h = sb("h", [128, NB * D])
        with ExitStack() as e2:
            xT = e2.enter_context(nc.sbuf_tensor(k.nm("xT"), [128, 2, 3200], F))
            layernorm(k, x, h[:, :])
            transpose_rows(k, h, xT)
            fence(k)
            w = e2.enter_context(nc.sbuf_tensor(k.nm("w"), [128, 2, 2048], F))
            wl = e2.enter_context(nc.sbuf_tensor(k.nm("wl"), [128, 2, D], F))
            for r in range(8):
                for c in range(2):
                    k.ld.start(w[:, c, D * r:D * (r + 1)], a['L1_gnn_weight'][r, 128 * c:128 * (c + 1), :])
            P.wait(load_w(k, wl, a['L1_gnn_loop_weight']))
            project(k, xT, w, 2048, dram_sink(k, e2, table, D))
            x3 = x.rearrange("p (b c) -> p b c", b=NB)

            def sink(b, m0, mw, ps):
                V.wait(P.now())
                return V.do(vec.scalar_tensor_tensor(out=x3[:, b, :], in0=ps, scalar=s, in1=x3[:, b, :],
                                                     op0=ALU.mult, op1=ALU.add))
            project(k, xT, wl, D, sink)
            fence(k)
        seg_sum(k, k.T, table, 8 * 3200, k.xtyp, k.dlR, k.off256, h)
        add_bias(k, x, a['L1_gnn_h_bias'])
        V.do(vec.scalar_tensor_tensor(out=x, in0=h[:, :], scalar=s, in1=x, op0=ALU.mult, op1=ALU.add))
        fence(k)


def top2_gates(k, sc, E, gates):
    nc, V, A = k.nc, k.V, k.A
    vec = nc.vector
    with ExitStack() as es:
        def sb(n, shape, dt=F):
            return es.enter_context(nc.sbuf_tensor(k.nm(n), shape, dt))
        mv = sb("mv", [128, NB, 8])
        mi = sb("mi", [128, NB, 8], U32)
        mf = sb("mf", [128, NB, 2])
        w = sb("w", [128, NB, 2])
        dn = sb("dn", [128, NB])
        t1 = sb("t1", [128, NB, E])

        def vs(op, *args, **kw):
            V.wait(V.now())
            V.do(op(*args, **kw))
        V.wait(V.now())
        for b in range(NB):
            V.do(vec.max(mv[:, b, :], sc[:, b, :]))
        V.wait(V.now())
        for b in range(NB):
            V.do(vec.max_index(mi[:, b, :], mv[:, b, :], sc[:, b, :]))
        vs(vec.tensor_copy, mf[:, :, :], mi[:, :, 0:2])
        vs(vec.tensor_tensor, dn[:, :], mv[:, :, 1], mv[:, :, 0], ALU.subtract)
        A.wait(V.now())
        A.do(nc.scalar.activation(w[:, :, 1], dn[:, :], ACT.Exp))
        V.wait(A.now())
        vs(vec.tensor_scalar, dn[:, :], w[:, :, 1], 1.0, None, ALU.add)
        vs(vec.reciprocal, w[:, :, 0], dn[:, :])
        vs(vec.tensor_tensor, w[:, :, 1], w[:, :, 1], w[:, :, 0], ALU.mult)
        io = bc(k.iof[:, 0:E].unsqueeze(1), [128, NB, E])
        vs(vec.tensor_tensor, gates, io, bc(mf[:, :, 0:1], [128, NB, E]), ALU.is_equal)
        vs(vec.tensor_tensor, gates, gates, bc(w[:, :, 0:1], [128, NB, E]), ALU.mult)
        vs(vec.tensor_tensor, t1[:, :, :], io, bc(mf[:, :, 1:2], [128, NB, E]), ALU.is_equal)
        vs(vec.tensor_tensor, t1[:, :, :], t1[:, :, :], bc(w[:, :, 1:2], [128, NB, E]), ALU.mult)
        vs(vec.tensor_tensor, gates, gates, t1[:, :, :], ALU.add)
        fence(k)


def moe(k, x, xT, gates, E, Hd, W1, b1, W2, b2):
    nc, V, A, P = k.nc, k.V, k.A, k.P
    vec = nc.vector
    HC = Hd // 128
    x3 = x.rearrange("p (b c) -> p b c", b=NB)
    with ExitStack() as es:
        def sb(n, shape, dt=F):
            return es.enter_context(nc.sbuf_tensor(k.nm(n), shape, dt))
        w1 = sb("w1", [128, 2, 2, Hd])
        w2 = sb("w2", [128, 2, HC, D])
        bb = sb("bb", [128, E, HC])
        b2s = sb("b2s", [E, D])
        gT = sb("gT", [E, 3200])
        hT = sb("hT", [128, 4, 512])
        k.ld.start(bb[:, :, :], b1.rearrange("e (c p) -> p e c", p=128), small=True)
        k.ld.start(b2s[:, :], b2)
        free = [None, None]

        def fetch(e):
            k.S.wait(free[e % 2])
            t = [k.ld.start(w1[:, e % 2, c, :], W1[e, 128 * c:128 * (c + 1), :]) for c in range(2)]
            t.append(k.ld.start(w2[:, e % 2, :, :], W2[e].rearrange("(c p) n -> p c n", p=128)))
            return t
        small = k.ld.all()
        tw = [fetch(0), fetch(1)]
        P.wait(small)
        A.wait(small)
        for b in range(NB):
            bk = b % 2
            P.wait(k.pst[bk])
            P.do(nc.tensor.transpose(k.ps[bk][0:E, 0:128], gates[:, b, :], k.ident[:, :]))
            A.wait(P.now())
            k.pst[bk] = A.do(nc.scalar.copy(gT[:, 128 * b:128 * (b + 1)], k.ps[bk][0:E, 0:128]))
            P.wait(A.now(), k.pst[2 + bk])
            mm(k, k.ps[2 + bk][:, 0:D], gT[:, 128 * b:128 * (b + 1)], b2s[:, :])
            V.wait(P.now())
            k.pst[2 + bk] = V.do(vec.tensor_tensor(x3[:, b, :], x3[:, b, :], k.ps[2 + bk][:, 0:D], ALU.add))
        hfree = [None] * 4
        hn = 0
        cn = 0
        for e in range(E):
            P.wait(tw[e])
            for ch in range(7):
                t0, tw_ = 512 * ch, min(512, 3200 - 512 * ch)
                oa = (4, 5) if cn % 2 == 0 else (6, 7)
                cn += 1
                pend = []

                def second(hc, slot, ta):
                    P.wait(ta)
                    if hc == 0:
                        P.wait(k.pst[oa[0]], k.pst[oa[1]])
                    for j in range(tw_ // 128):
                        hfree[slot] = mm(k, k.ps[oa[j // 2]][:, D * (j % 2):D * (j % 2 + 1)],
                                         hT[:, slot, 128 * j:128 * (j + 1)], w2[:, e % 2, hc, :],
                                         start=(hc == 0 and j % 2 == 0), stop=(hc == HC - 1))
                for hc in range(HC):
                    bk = hn % 4
                    slot = hn % 4
                    hn += 1
                    P.wait(k.pst[bk])
                    for c in range(2):
                        mm(k, k.ps[bk][:, 0:tw_], w1[:, e % 2, c, 128 * hc:128 * (hc + 1)], xT[:, c, t0:t0 + tw_],
                           start=(c == 0), stop=(c == 1))
                    A.wait(P.now(), hfree[slot])
                    ta = k.pst[bk] = A.do(nc.scalar.activation(hT[:, slot, 0:tw_], k.ps[bk][:, 0:tw_], ACT.Gelu,
                                                               bias=bb[:, e, hc:hc + 1]))
                    pend.append((hc, slot, ta))
                    if len(pend) > 1:
                        second(*pend.pop(0))
                for q in pend:
                    second(*q)
                tp = P.now()
                V.wait(tp)
                for j in range(tw_ // 128):
                    b = 4 * ch + j
                    V.wait(V.now())
                    k.pst[oa[j // 2]] = V.do(vec.scalar_tensor_tensor(
                        out=x3[:, b, :], in0=k.ps[oa[j // 2]][:, D * (j % 2):D * (j % 2 + 1)],
                        scalar=gates[:, b, e:e + 1], in1=x3[:, b, :], op0=ALU.mult, op1=ALU.add))
            free[e % 2] = P.now()
            if e + 2 < E:
                tw.append(fetch(e + 2))
        fence(k)


def finish_second(k, es):
    nc, V = k.nc, k.V
    vec = nc.vector
    e = k.second
    T = e.T

    def sb(n, shape, dt):
        return es.enter_context(nc.sbuf_tensor(k.nm(n), shape, dt))
    k.dl2 = sb("dl2", [128, T], F)
    k.xs2 = sb("xs2", [128, T], U32)
    k.n4 = sb("n4", [1, T], I32)
    blk = sb("blk", [128, T], F)
    tile_blocks(k, "n", T, e.st, blk, ((4, k.n4),))
    k.same = sb("same", [128, T], F)
    k.nend = sb("nend", [1, NB], I32)
    V.do(vec.memset(k.same[:, 0:1], 0.0))
    V.do(vec.tensor_tensor(k.same[:, 1:T], blk[:, 1:T], blk[:, 0:T - 1], ALU.is_equal))
    V.do(vec.tensor_scalar(k.nend[:, :], e.st[0:1, 1:NB + 1], 20.0, -20.0, ALU.mult, ALU.add))
    k.n_flags = edge_flags_dram(k, "n", T)
    with ExitStack() as e2:
        p = e2.enter_context(nc.sbuf_tensor("sorted_n", [128, T, 2], F))
        k.S.wait(k.late.all())
        V.wait(k.ld.start(p[:, :, :].rearrange("p a b -> p (a b)"), e.tab.rearrange("(p r) w -> p (r w)", p=128)))
        V.do(vec.tensor_copy(k.xs2[:, :], p[:, :, 1]))
        V.do(vec.scalar_tensor_tensor(out=k.dl2[:, :], in0=blk[:, :], scalar=-128.0, in1=p[:, :, 0],
                                      op0=ALU.mult, op1=ALU.add))
        V.wait(V.now())
        to_rows(k, "nf", p[:, :, 0], T, k.n_flags[128:128 + T * 128])
        fence(k)


def stage_l1_ffn(k, x, a):
    nc, V, A, P, G = k.nc, k.V, k.A, k.P, k.G
    vec = nc.vector
    T = k.T2
    table = nc.dram_tensor("gat_rows", (3200, 20), F).ap()
    with ExitStack() as es:
        def sb(n, shape, dt=F):
            return es.enter_context(nc.sbuf_tensor(k.nm(n), shape, dt))

        def vs(op, *args, **kw):
            V.wait(V.now())
            return V.do(op(*args, **kw))
        xT = sb("xT", [128, 2, 3200])
        gates = sb("gates", [128, NB, 4])
        with ExitStack() as e2:
            finish_second(k, e2)

            def s2(n, shape, dt=F):
                return e2.enter_context(nc.sbuf_tensor(k.nm(n), shape, dt))
            with ExitStack() as e3:
                xn = e3.enter_context(nc.sbuf_tensor(k.nm("xn"), [128, NB * D], F))
                layernorm(k, x, xn[:, :])
                transpose_rows(k, xn, xT)
                fence(k)
            wg = s2("wg", [128, 2, 16])
            h = s2("h", [128, NB, 20])
            ad = s2("ad", [128, NB, 4])
            load_w(k, wg, a['L1_ffn_W_gat'])
            asr = bcast_row(k, e2, a['L1_ffn_att_src'].rearrange("h c -> (h c)"), 16)
            adr = bcast_row(k, e2, a['L1_ffn_att_dst'].rearrange("h c -> (h c)"), 16)
            bg = bcast_row(k, e2, a['L1_ffn_b_gat'], 16)
            lg = bcast_row(k, e2, a['L1_ffn_ln_gamma'], 16)
            lb = bcast_row(k, e2, a['L1_ffn_ln_beta'], 16)
            P.wait(k.ld.all())
            V.wait(k.ld.all())

            def sink(b, m0, mw, ps):
                V.wait(P.now())
                return V.do(vec.tensor_copy(h[:, b, 0:16], ps))
            project(k, xT, wg, 16, sink)
            tmp = s2("tmp", [128, NB, 16])
            for r, o in ((asr, h[:, :, 16:20]), (adr, ad[:, :, :])):
                vs(vec.tensor_tensor, tmp[:, :, :], h[:, :, 0:16], bc(r[:, :].unsqueeze(1), [128, NB, 16]), ALU.mult)
                vs(vec.tensor_reduce, o, tmp[:, :, :].rearrange("p b (h c) -> p b h c", h=4), AX, ALU.add)
            k.S.wait(V.now())
            k.ld.start(table.rearrange("(b p) c -> p b c", p=128), h[:, :, :])
            fence(k)
            gs = s2("gs", [128, T, 20])
            L = s2("L", [128, 4 * T])
            tg = [k.ind.gather(gs[:, t, :], table, k.xs2[:, t:t + 1], 3200) for t in range(T)]
            adf = ad[:, :, :].rearrange("p b c -> p (b c)")
            e4 = ExitStack()
            rows = DstRows(k, e4, k.dl2, k.n4, adf, 4, 4)
            Lv = L[:, :].rearrange("p (h t) -> p h t", h=4)
            te = [None] * T

            def spread(t):
                bk = 2 + (t // 32) % 4
                if t % 32 == 0:
                    P.wait(k.pst[bk])
                te[t] = rows.spread(t, k.ps[bk][:, 4 * (t % 32):4 * (t % 32) + 4])

            def collect(t):
                if t % 32 != 31:
                    return
                bk = 2 + (t // 32) % 4
                V.wait(te[t])
                k.pst[bk] = V.do(vec.tensor_copy(Lv[:, :, t - 31:t + 1],
                                                 k.ps[bk][:, 0:128].rearrange("p (t h) -> p h t", h=4)))
            pipeline(T, (0, rows.mark), (2, rows.turn), (5, spread), (7, collect))
            V.wait(tg, V.now())
            V.do(vec.tensor_tensor(Lv, Lv, gs[:, :, 16:20].rearrange("p t h -> p h t"), ALU.add))
            vs(vec.scalar_tensor_tensor, out=L[:, :], in0=L[:, :], scalar=0.2, in1=L[:, :], op0=ALU.mult, op1=ALU.max)
            fence(k)
            e4.close()
            seg_softmax(k, "n1", L[:, :], 4, 32, T, k.n_flags, ALU.add, 1e-16)
            g4 = gs[:, :, 0:16].rearrange("p t (h c) -> p t h c", h=4)
            for c in range(4):
                vs(vec.tensor_tensor, gs[:, :, 0:16].rearrange("p t (h c) -> p h t c", h=4)[:, :, :, c],
                                     gs[:, :, 0:16].rearrange("p t (h c) -> p h t c", h=4)[:, :, :, c],
                                     Lv, ALU.mult)
            acc = s2("acc", [128, NB * 16])
            Q = T // 4
            oh = s2("oh", [128, 16, 128], BF)
            parts = s2("parts", [128, 2, Q, 3, 16], BF)
            rest = s2("rest", [128, Q, 16])
            free = [None] * 4
            pfree = [None] * 2
            to, tp, ts = {}, {}, {}

            def split(t):
                if t % Q:
                    return
                q = t // Q
                p = parts[:, q % 2, :, :, :]
                V.wait(pfree[q % 2])
                vs(vec.tensor_copy, p[:, :, 0, :], gs[:, t:t + Q, 0:16])
                vs(vec.tensor_tensor, rest[:, :, :], gs[:, t:t + Q, 0:16], p[:, :, 0, :], ALU.subtract)
                vs(vec.tensor_copy, p[:, :, 1, :], rest[:, :, :])
                vs(vec.tensor_tensor, rest[:, :, :], rest[:, :, :], p[:, :, 1, :], ALU.subtract)
                ts[q] = vs(vec.tensor_copy, p[:, :, 2, :], rest[:, :, :])

            def mark(t):
                if t % 4 == 0:
                    V.wait(free[(t // 4) % 4])
                    to[t // 4] = onehots(k, oh[:, t % 16:t % 16 + 4, :], k.dl2, t)

            def product(t):
                bk = (t // 8) % 4
                q = t // Q
                if t % 4 == 0:
                    P.wait(to.pop(t // 4), ts[q])
                if t % 8 == 0:
                    P.wait(k.pst[bk])
                tp[t] = free[(t // 4) % 4] = pfree[q % 2] = mm(
                    k, k.ps[bk][:, 48 * (t % 8):48 * (t % 8) + 48], oh[:, t % 16, :],
                    parts[:, q % 2, t % Q, :, :].rearrange("p s c -> p (s c)"))

            def keep(t):
                if t % 8 == 7:
                    bk = (t // 8) % 4
                    V.wait(tp[t])
                    k.pst[bk] = V.do(vec.tensor_reduce(
                        gs[:, t - 7:t + 1, 0:16],
                        k.ps[bk][:, 0:384].rearrange("p (t s c) -> p t c s", s=3, c=16), AX, ALU.add))
            V.wait(V.now())
            pipeline(T, (0, split), (0, mark), (4, product), (8, keep))
            V.wait(V.now())
            for c in range(16):
                V.do(vec.tensor_tensor_scan(gs[:, :, c], k.same[:, :], gs[:, :, c], 0.0, ALU.mult, ALU.add))
            V.wait(V.now())
            off = Offsets(k, mybir.EngineType.DVE, k.nend, 20 * (T - 1))
            gf = gs[:, :, :].rearrange("p t c -> p (t c)")
            for b in range(NB):
                V.do(vec.tensor_copy(acc[:, 16 * b:16 * (b + 1)], gf[:, bass.ds(off(b), 16)]))
            c3 = acc[:, :].rearrange("p (b c) -> p b c", b=NB)
            mu = s2("mu", [128, NB])

            def row16(r):
                return bc(r[:, :].unsqueeze(1), [128, NB, 16])
            vs(vec.tensor_tensor, c3, c3, row16(bg), ALU.add)
            vs(vec.tensor_reduce, mu[:, :], c3, AX, ALU.add)
            vs(vec.tensor_scalar, mu[:, :], mu[:, :], 1.0 / 16, None, ALU.mult)
            vs(vec.tensor_tensor, c3, c3, bc(mu[:, :].unsqueeze(2), [128, NB, 16]), ALU.subtract)
            vs(vec.tensor_tensor, tmp[:, :, :], c3, c3, ALU.mult)
            vs(vec.tensor_reduce, mu[:, :], tmp[:, :, :], AX, ALU.add)
            vs(vec.tensor_scalar, mu[:, :], mu[:, :], 1.0 / 16, 1e-5, ALU.mult, ALU.add)
            A.wait(V.now())
            A.do(nc.scalar.activation(mu[:, :], mu[:, :], ACT.Sqrt))
            V.wait(A.now())
            vs(vec.reciprocal, mu[:, :], mu[:, :])
            vs(vec.tensor_tensor, c3, c3, bc(mu[:, :].unsqueeze(2), [128, NB, 16]), ALU.mult)
            vs(vec.tensor_tensor, c3, c3, row16(lg), ALU.mult)
            vs(vec.tensor_tensor, c3, c3, row16(lb), ALU.add)
            sc = s2("sc", [128, NB, 8])
            vs(vec.memset, sc[:, :, :], NEG)
            vs(vec.tensor_reduce, sc[:, :, 0:4], c3.rearrange("p b (h e) -> p b e h", h=4), AX, ALU.add)
            vs(vec.tensor_scalar, sc[:, :, 0:4], sc[:, :, 0:4], 0.25, None, ALU.mult)
            fence(k)
            top2_gates(k, sc, 4, gates[:, :, :])
        moe(k, x, xT, gates, 4, 512, a['L1_ffn_W1'], a['L1_ffn_b1'], a['L1_ffn_W2'], a['L1_ffn_b2'])


def stage_l2_gnn(k, x, a):
    nc, V, A, P = k.nc, k.V, k.A, k.P
    vec = nc.vector
    with ExitStack() as es:
        def sb(n, shape, dt=F):
            return es.enter_context(nc.sbuf_tensor(k.nm(n), shape, dt))
        clear_rows(k, es)

        def vs(op, *args, **kw):
            V.wait(V.now())
            return V.do(op(*args, **kw))
        h = sb("h", [128, NB * D])
        h3 = h[:, :].rearrange("p (b c) -> p b c", b=NB)
        xT = sb("xT", [128, 2, 3200])
        dinv = sb("dinv", [128, NB])
        pos = sb("pos", [128, NB])
        xn = sb("xn", [128, NB * D])
        layernorm(k, x, xn[:, :])
        transpose_rows(k, xn, xT)
        fence(k)
        vs(vec.tensor_scalar, pos[:, :], k.deg[:, :], 0.5, None, ALU.is_gt)
        vs(vec.tensor_scalar, dinv[:, :], k.deg[:, :], 1e-12, None, ALU.max)
        A.wait(V.now())
        A.do(nc.scalar.activation(dinv[:, :], dinv[:, :], ACT.Sqrt))
        V.wait(A.now())
        vs(vec.reciprocal, dinv[:, :], dinv[:, :])
        vs(vec.tensor_tensor, dinv[:, :], dinv[:, :], pos[:, :], ALU.mult)
        w = sb("w", [128, 2, D])
        for i in range(2):
            table = nc.dram_tensor(f"gcn{i}", (3200, D), F).ap()
            with ExitStack() as e2:
                P.wait(load_w(k, w, a[f'L2_gnn_W{i + 1}']), V.now())
                buf = e2.enter_context(nc.sbuf_tensor(k.nm("tb"), [128, 6, D], F))
                free = [None] * 6

                def sink(b, m0, mw, ps):
                    V.wait(P.now(), free[b % 6])
                    t = V.do(vec.tensor_scalar(buf[:, b % 6, :], ps, dinv[:, b:b + 1], None, ALU.mult))
                    k.S.wait(t)
                    free[b % 6] = k.ld.start(table[128 * b:128 * (b + 1), :], buf[:, b % 6, :])
                    return t
                V.wait(V.now())
                project(k, xT, w, D, sink)
                fence(k)
            seg_sum(k, k.T, table, 3200, k.xsrc, k.dlA, k.off256, h)
            vs(vec.tensor_tensor, h3, h3, bc(dinv[:, :].unsqueeze(2), [128, NB, D]), ALU.mult)
            fence(k)
            add_bias(k, h[:, :], a[f'L2_gnn_b{i + 1}'])
            if i == 0:
                nr = sb("nr", [128, NB])
                junk = sb("junk", [128, D])
                for b in range(NB):
                    A.wait(A.now())
                    A.do(nc.scalar.activation(junk[:, :], h3[:, b, :], ACT.Square, accum_out=nr[:, b:b + 1]))
                A.wait(A.now())
                A.do(nc.scalar.activation(nr[:, :], nr[:, :], ACT.Sqrt))
                V.wait(A.now())
                vs(vec.tensor_scalar, nr[:, :], nr[:, :], 1e-12, None, ALU.max)
                vs(vec.reciprocal, nr[:, :], nr[:, :])
                vs(vec.tensor_tensor, h3, h3, bc(nr[:, :].unsqueeze(2), [128, NB, D]), ALU.mult)
                transpose_rows(k, h, xT)
                fence(k)
        vs(vec.tensor_tensor, h[:, :], h[:, :], xn[:, :], ALU.add)
        vs(vec.tensor_tensor, x, x, h[:, :], ALU.add)
        fence(k)


def split_biases(k, es, bs, b1, b2):
    nc, V = k.nc, k.V
    vec = nc.vector
    (E, M1), M2 = b1.shape, b2.shape[1]
    bf = es.enter_context(nc.sbuf_tensor(k.nm("bf"), [96, 2, M1 + M2], F))

    def vs(op, *args, **kw):
        V.wait(V.now())
        return V.do(op(*args, **kw))
    k.S.wait(V.do(vec.memset(bf[:, :, :], 0.0)))
    for i in range(3):
        k.ld.start(bf[32 * i:32 * i + E, 0, 0:M1], b1)
        k.ld.start(bf[32 * i:32 * i + E, 0, M1:M1 + M2], b2)
    V.wait(k.ld.all())
    vs(vec.tensor_copy, bs[:, :], bf[:, 0, :])
    vs(vec.tensor_tensor, bf[:, 1, :], bf[:, 0, :], bs[:, :], ALU.subtract)
    vs(vec.tensor_copy, bs[32:64, :], bf[32:64, 1, :])
    vs(vec.tensor_copy, bs[64:96, :], bf[64:96, 1, :])
    vs(vec.tensor_tensor, bf[64:96, 0, :], bf[64:96, 1, :], bs[64:96, :], ALU.subtract)
    vs(vec.tensor_copy, bs[64:96, :], bf[64:96, 0, :])


def route(k, es, mf, C, E, T, pos, ohE, offsets):
    nc, V, P, G = k.nc, k.V, k.P, k.G
    vec = nc.vector

    def sb(n, shape, dt=F):
        return es.enter_context(nc.sbuf_tensor(k.nm(n), shape, dt))

    def vs(op, *args, **kw):
        V.wait(V.now())
        return V.do(op(*args, **kw))
    O = sb("O", [128, C, E], BF)
    rk = sb("rk", [128, C, E])
    tot = sb("tot", [128, C, E])
    cm = sb("cm", [128, C + 1, E])
    nt = sb("nt", [128, E])
    ni = sb("ni", [128, E], I32)
    st = sb("st", [128, E])
    pf = sb("pf", [128, C])
    iv = sb("iv", [128, 1])
    pid = sb("pid", [128, 1])
    bt = sb("bt", [128, T])
    tf = sb("tf", [1, T])
    V.wait(G.do(nc.gpsimd.iota(pid[:, :], pattern=[[0, 1]], base=0, channel_multiplier=1,
                               allow_small_or_imprecise_dtypes=True)))
    vs(vec.tensor_scalar, iv[:, :], pid[:, :], LASTP - 0.5, 1.0e6, ALU.is_gt, ALU.mult)
    for c in range(NB - 1, C, NB):
        vs(vec.tensor_tensor, mf[:, c:c + 1], mf[:, c:c + 1], iv[:, :], ALU.add)
    vs(vec.tensor_tensor, O[:, :, :], bc(k.iof[:, 0:E].unsqueeze(1), [128, C, E]),
       bc(mf.unsqueeze(2), [128, C, E]), ALU.is_equal)
    P.wait(V.now())
    for i, c0 in enumerate(range(0, C, 512 // E)):
        c = slice(c0, min(c0 + 512 // E, C))
        w = (c.stop - c0) * E
        Of = O[:, c, :].rearrange("p c e -> p (c e)")
        P.wait(k.pst[2 * i], k.pst[2 * i + 1])
        mm(k, k.ps[2 * i][:, 0:w], k.ltrib[:, :], Of)
        mm(k, k.ps[2 * i + 1][:, 0:w], k.onesb[:, :], Of)
        V.wait(P.now())
        k.pst[2 * i] = vs(vec.tensor_copy, rk[:, c, :].rearrange("p c e -> p (c e)"), k.ps[2 * i][:, 0:w])
        k.pst[2 * i + 1] = vs(vec.tensor_copy, tot[:, c, :].rearrange("p c e -> p (c e)"),
                              k.ps[2 * i + 1][:, 0:w])
    vs(vec.tensor_reduce, nt[:, :], tot[:, :, :].rearrange("p c e -> p e c"), AX, ALU.add)
    vs(vec.tensor_scalar, ni[:, :], nt[:, :], 1.0, 127.0, ALU.max, ALU.add)
    vs(vec.tensor_scalar, ni[:, :], ni[:, :], 7, None, ALU.arith_shift_right)
    vs(vec.tensor_copy, nt[:, :], ni[:, :])
    vs(vec.memset, st[:, 0:1], 0.0)
    vs(vec.tensor_tensor_scan, st[:, 1:E], k.ones[:, 0:E - 1], nt[:, 0:E - 1], 0.0, ALU.mult, ALU.add)
    vs(vec.tensor_scalar, cm[:, 0, :], st[:, :], 128.0, None, ALU.mult)
    V.wait(V.now())
    for e in range(E):
        V.do(vec.tensor_tensor_scan(cm[:, 1:C + 1, e], k.ones[:, 0:C], tot[:, :, e], cm[:, 0, e:e + 1],
                                    ALU.mult, ALU.add))
    vs(vec.tensor_tensor, rk[:, :, :], rk[:, :, :], cm[:, 0:C, :], ALU.add)
    vs(vec.tensor_tensor, rk[:, :, :], rk[:, :, :], O[:, :, :], ALU.mult)
    vs(vec.tensor_reduce, pf[:, :], rk[:, :, :], AX, ALU.add)
    for c in range(NB - 1, C, NB):
        vs(vec.tensor_tensor, pf[:, c:c + 1], pf[:, c:c + 1], iv[:, :], ALU.add)
    vs(vec.tensor_copy, pos, pf[:, :])
    vs(vec.memset, bt[:, :], 0.0)
    for e in range(1, E):
        vs(vec.scalar_tensor_tensor, out=bt[:, :], in0=k.tiles[:, 0:T], scalar=st[:, e:e + 1], in1=bt[:, :],
           op0=ALU.is_ge, op1=ALU.add)
    for w, o in offsets:
        vs(vec.tensor_scalar, tf[:, :], bt[0:1, :], float(w), None, ALU.mult)
        vs(vec.tensor_copy, o[:, :], tf[:, :])
    for i in range(3):
        r = slice(32 * i, 32 * i + 32)
        vs(vec.tensor_scalar, pid[r, :], pid[r, :], -32.0 * i, None, ALU.add)
    vs(vec.tensor_scalar, ohE[:, :], bt[0:96, :], pid[0:96, :], None, ALU.is_equal)
    return pf


def clear_rows(k, es):
    nc = k.nc
    zero = es.enter_context(nc.sbuf_tensor(k.nm("zero"), [128, 7 * D], F))
    k.S.wait(k.V.do(nc.vector.memset(zero[:, :], 0.0)))
    k.one_in = nc.dram_tensor("one_in", (128 * 56, D), F).ap()
    k.moe_in = nc.dram_tensor("moe_in", (128 * 56, D), F).ap()
    for tab in (k.one_in, k.moe_in):
        for i in range(8):
            k.ld.start(tab[896 * i:896 * (i + 1), :].rearrange("(p r) n -> p (r n)", p=128), zero[:, :])


def stage_l2_ffn(k, x, a):
    nc, V, A, P, G, S = k.nc, k.V, k.A, k.P, k.G, k.S
    vec = nc.vector
    T, E, Hd = 56, 32, 64
    x3 = x.rearrange("p (b c) -> p b c", b=NB)
    xs = k.one_in
    ys = nc.dram_tensor("one_out", (128 * T, D), F).ap()
    with ExitStack() as es:
        def sb(n, shape, dt=F):
            return es.enter_context(nc.sbuf_tensor(k.nm(n), shape, dt))

        def vs(op, *args, **kw):
            V.wait(V.now())
            return V.do(op(*args, **kw))
        w1 = sb("w1", [128, 2, E * Hd])
        w2 = sb("w2", [Hd, E * D])
        bs = sb("bs", [96, Hd + D], BF)
        pos = sb("pos", [128, NB], U32)
        ohE = sb("ohE", [96, T], BF)
        o1 = sb("o1", [1, T], I32)
        o2 = sb("o2", [1, T], I32)
        with ExitStack() as e2:
            def s2(n, shape, dt=F):
                return e2.enter_context(nc.sbuf_tensor(k.nm(n), shape, dt))
            rw = s2("rw", [E, D])
            rwT = s2("rwT", [128, 2, E])
            k.ld.start(rw[:, :], a['L2_ffn_router_w'])
            rb = bcast_row(k, e2, a['L2_ffn_router_b'], E)
            split_biases(k, e2, bs, a['L2_ffn_b1'], a['L2_ffn_b2'])
            tsmall = k.ld.all()
            tw = [k.ld.start(w1[:, c, :].rearrange("p (e h) -> p e h", e=E),
                             a['L2_ffn_W1'][:, 128 * c:128 * (c + 1), :].rearrange("e p h -> p e h"))
                  for c in range(2)]
            tw.append(k.ld.start(w2[:, :].rearrange("h (e n) -> h e n", e=E),
                                 a['L2_ffn_W2'].rearrange("e h n -> h e n")))
            xn = s2("xn", [128, NB * D])
            xT = s2("xT", [128, 2, 3200])
            layernorm(k, x, xn[:, :])
            transpose_rows(k, xn, xT)
            P.wait(tsmall)
            V.wait(tsmall)
            P.wait(k.pst[2])
            for c in range(2):
                P.do(nc.tensor.transpose(k.ps[2][:, E * c:E * c + E], rw[:, 128 * c:128 * (c + 1)],
                                         k.ident[0:E, 0:E]))
            V.wait(P.now())
            k.pst[2] = vs(vec.tensor_copy, rwT[:, :, :], k.ps[2][:, 0:2 * E].rearrange("p (c e) -> p c e", c=2))
            lg = s2("lg", [128, NB, E])

            def sink(b, m0, mw, ps):
                V.wait(P.now())
                return V.do(vec.tensor_tensor(lg[:, b, :], ps, rb[:, :], ALU.add))
            P.wait(V.now())
            project(k, xT, rwT, E, sink)
            mv = s2("mv", [128, NB, 8])
            mi = s2("mi", [128, NB, 8], U32)
            mf = s2("mf", [128, NB])
            V.wait(V.now())
            for b in range(NB):
                V.do(vec.max(mv[:, b, :], lg[:, b, :]))
            V.wait(V.now())
            for b in range(NB):
                V.do(vec.max_index(mi[:, b, :], mv[:, b, :], lg[:, b, :]))
            vs(vec.tensor_copy, mf[:, :], mi[:, :, 0])
            pf = route(k, e2, mf[:, :], NB, E, T, pos[:, :], ohE, ((Hd, o1), (D, o2)))
            G.wait(V.now())
            for b in range(NB):
                k.ind.scatter(xs, pos[:, b:b + 1], xn[:, D * b:D * (b + 1)], 128 * T)
            vs(vec.tensor_scalar, pf[:, :], pf[:, :], float(128 * T - 1), None, ALU.min)
            V.wait(k.ind.all())
            vs(vec.tensor_copy, pos[:, :], pf[:, :])
            fence(k)
        R = 6
        xt = sb("xt", [128, R, D])
        xTt = sb("xTt", [128, R, D])
        hb = sb("hb", [128, R, Hd])
        hT = sb("hT", [Hd, R, 128])
        yb = sb("yb", [128, R, D])
        off1 = Offsets(k, mybir.EngineType.PE, o1, (E - 1) * Hd)
        off2 = Offsets(k, mybir.EngineType.PE, o2, (E - 1) * D)
        tx, tt, tg, th = {}, {}, {}, {}
        xfree, xtfree, hfree, htfree, yfree = ([None] * R for _ in range(5))

        def fetch(t):
            S.wait(xfree[t % R])
            tx[t] = k.ld.start(xt[:, t % R, :], xs[128 * t:128 * (t + 1), :])

        def turn(t):
            bk = t % 2
            P.wait(tx.pop(t), k.pst[bk])
            for c in range(2):
                xfree[t % R] = P.do(nc.tensor.transpose(k.ps[bk][:, 128 * c:128 * (c + 1)],
                                                        xt[:, t % R, 128 * c:128 * (c + 1)], k.ident[:, :]))
            V.wait(xfree[t % R], xtfree[t % R])
            k.pst[bk] = tt[t] = V.do(vec.tensor_copy(xTt[:, t % R, :], k.ps[bk][:, 0:D]))

        def hidden(t):
            bk = 2 + t % 2
            P.wait(tt.pop(t), k.pst[bk], tw)
            o = off1(t)
            mm(k, k.ps[bk][:, 0:Hd], bc(ohE[:, t:t + 1], [96, 128]), bs[:, 0:Hd], stop=False)
            for c in range(2):
                xtfree[t % R] = mm(k, k.ps[bk][:, 0:Hd], xTt[:, t % R, 128 * c:128 * (c + 1)],
                                   w1[:, c, bass.ds(o, Hd)], start=False, stop=(c == 1))
            A.wait(P.now(), hfree[t % R])
            k.pst[bk] = tg[t] = A.do(nc.scalar.activation(hb[:, t % R, :], k.ps[bk][:, 0:Hd], ACT.Relu))

        def turn_hidden(t):
            bk = 4 + t % 2
            P.wait(tg.pop(t), k.pst[bk])
            hfree[t % R] = P.do(nc.tensor.transpose(k.ps[bk][0:Hd, 0:128], hb[:, t % R, :], k.ident[:, :]))
            V.wait(P.now(), htfree[t % R])
            k.pst[bk] = th[t] = V.do(vec.tensor_copy(hT[:, t % R, :], k.ps[bk][0:Hd, 0:128]))

        def output(t):
            bk = 6 + t % 2
            P.wait(th.pop(t), k.pst[bk])
            o = off2(t)
            mm(k, k.ps[bk][:, 0:D], bc(ohE[:, t:t + 1], [96, 128]), bs[:, Hd:Hd + D], stop=False)
            htfree[t % R] = mm(k, k.ps[bk][:, 0:D], hT[:, t % R, :], w2[:, bass.ds(o, D)], start=False)
            A.wait(P.now(), yfree[t % R])
            k.pst[bk] = A.do(nc.scalar.activation(yb[:, t % R, :], k.ps[bk][:, 0:D], ACT.Relu))
            S.wait(A.now())
            yfree[t % R] = k.ld.start(ys[128 * t:128 * (t + 1), :], yb[:, t % R, :])
        pipeline(T, (0, fetch), (4, turn), (6, hidden), (8, turn_hidden), (10, output))
        fence(k)
        back = sb("back", [128, 8, D])
        free = [None] * 8
        for b in range(NB):
            G.wait(free[b % 8])
            V.wait(k.ind.gather(back[:, b % 8, :], ys, pos[:, b:b + 1], 128 * T))
            free[b % 8] = V.do(vec.tensor_tensor(x3[:, b, :], x3[:, b, :], back[:, b % 8, :], ALU.add))
        fence(k)


def stage_l3_gnn(k, x, a):
    nc, V, A, P, G = k.nc, k.V, k.A, k.P, k.G
    vec = nc.vector
    T = k.T
    table = nc.dram_tensor("h3", (3200, 264), F).ap()
    kept = nc.dram_tensor("kept_h3", (T // 4, 128, 2, 264), F).ap()
    tabs = nc.dram_tensor("as3", (3200, 8), F).ap()
    with ExitStack() as es:
        def sb(n, shape, dt=F):
            return es.enter_context(nc.sbuf_tensor(k.nm(n), shape, dt))

        def vs(op, *args, **kw):
            V.wait(V.now())
            return V.do(op(*args, **kw))
        L = sb("L", [128, 8 * T])
        Lv = L[:, :].rearrange("p (h t) -> p h t", h=8)
        with ExitStack() as e2:
            def s2(n, shape, dt=F):
                return e2.enter_context(nc.sbuf_tensor(k.nm(n), shape, dt))
            ha = s2("ha", [128, NB, 264])
            with ExitStack() as e3:
                xn = e3.enter_context(nc.sbuf_tensor(k.nm("xn"), [128, NB * D], F))
                xT = e3.enter_context(nc.sbuf_tensor(k.nm("xT"), [128, 2, 3200], F))
                w = e3.enter_context(nc.sbuf_tensor(k.nm("w"), [128, 2, D], F))
                wT = e3.enter_context(nc.sbuf_tensor(k.nm("wT"), [128, 2, D], F))
                asb = e3.enter_context(nc.sbuf_tensor(k.nm("as"), [128, NB, 8], F))
                tmp = e3.enter_context(nc.sbuf_tensor(k.nm("tmp"), [128, NB, D], F))
                layernorm(k, x, xn[:, :])
                transpose_rows(k, xn, xT)
                load_w(k, w, a['L3_gnn_W'])
                asr = bcast_row(k, e3, a['L3_gnn_a_src'].rearrange("h c -> (h c)"), D)
                adr = bcast_row(k, e3, a['L3_gnn_a_dst'].rearrange("h c -> (h c)"), D)
                P.wait(k.ld.all(), k.pst[2], k.pst[3])
                V.wait(k.ld.all())
                for i in range(2):
                    for j in range(2):
                        P.do(nc.tensor.transpose(k.ps[2][:, 256 * i + 128 * j:256 * i + 128 * j + 128],
                                                 w[:, j, 128 * i:128 * (i + 1)], k.ident[:, :]))
                V.wait(P.now())
                k.pst[2] = vs(vec.tensor_copy, wT[:, :, :].rearrange("p a b -> p (a b)"), k.ps[2][:, :])
                P.wait(V.now())

                def sink(b, m0, mw, ps):
                    V.wait(P.now())
                    return V.do(vec.tensor_copy(ha[:, b, 0:D], ps))
                project(k, xT, wT, D, sink)
                k.S.wait(V.now())
                wide = table.rearrange("(b p) c -> p b c", p=128)
                k.ld.start(wide[:, :, 0:D], ha[:, :, 0:D])
                for r, o in ((asr, asb[:, :, :]), (adr, ha[:, :, D:D + 8])):
                    vs(vec.tensor_tensor, tmp[:, :, :], ha[:, :, 0:D], bc(r[:, :].unsqueeze(1), [128, NB, D]), ALU.mult)
                    vs(vec.tensor_reduce, o, tmp[:, :, :].rearrange("p b (h c) -> p b h c", h=8), AX, ALU.add)
                k.S.wait(V.now())
                k.ld.start(tabs.rearrange("(b p) c -> p b c", p=128), asb[:, :, :])
                k.ld.start(wide[:, :, D:D + 8], asb[:, :, :])
                fence(k)
            ew = s2("ew", [4, D])
            k.ld.start(ew[0:3, :], a['L3_gnn_edge_W'].rearrange("n f -> f n"), small=True)
            k.ld.start(ew[3:4, :], rows_of(a['L3_gnn_edge_b']))
            P.wait(k.ld.all())
            AS = s2("AS", [128, T, 8])
            gk = s2("gk", [128, 8, 2, 264])
            stored = [None] * 8
            taken = [None] * 8
            tg = {}

            def fetch(t):
                i = (t // 4) % 8
                if not is_kept(t):
                    tg[t] = k.ind.gather(AS[:, t, :], tabs, k.xsrc[:, t:t + 1], 3200)
                    return
                G.wait(stored[i], taken[i])
                tg[t] = k.ind.gather(gk[:, i, t % 2, :], table, k.xsrc[:, t:t + 1], 3200)
                if t % 2:
                    k.S.wait(tg[t - 1], tg[t])
                    stored[i] = k.ld.start(kept[t // 4], gk[:, i, :, :])

            def take(t):
                if is_kept(t) and t % 2:
                    i = (t // 4) % 8
                    A.wait(tg[t - 1], tg[t])
                    taken[i] = A.do(nc.scalar.copy(AS[:, t - 1:t + 1, :], gk[:, i, :, D:D + 8]))
            rows = DstRows(k, e2, k.dlA, k.off264, ha[:, :, :].rearrange("p b c -> p (b c)"), 264, 264)
            aT = s2("aT", [4, 4, 4, 128])
            en = s2("en", [128, 6, D])
            lin = s2("lin", [128, T, 8])
            af = [None] * 4
            ta = [None] * 4
            ef = [None] * 6
            th, te, tx = {}, {}, {}

            def attrs(t):
                if t % 4:
                    return
                i = (t // 4) % 4
                P.wait(k.pst[7])
                for u in range(4):
                    P.do(nc.tensor.transpose(k.ps[7][0:4, 128 * u:128 * (u + 1)], k.attr[:, t + u, :], k.ident[:, :]))
                A.wait(P.now(), af[i])
                k.pst[7] = ta[i] = A.do(nc.scalar.copy(aT[:, i, :, :].rearrange("p a b -> p (a b)"), k.ps[7][0:4, :]))

            def spread(t):
                i = (t // 4) % 4
                bk = 2 + t % 3
                eb = 5 + t % 2
                P.wait(ta[i], k.pst[eb])
                af[i] = te[t] = mm(k, k.ps[eb][:, 0:D], aT[:, i, t % 4, :], ew[:, :])
                P.wait(k.pst[bk])
                th[t] = rows.spread(t, k.ps[bk][:, 0:264])

            def relu(t):
                eb = 5 + t % 2
                A.wait(te.pop(t), ef[t % 6])
                k.pst[eb] = te[t] = A.do(nc.scalar.activation(en[:, t % 6, :], k.ps[eb][:, 0:D], ACT.Relu))

            def weigh(t):
                bk = 2 + t % 3
                V.wait(te.pop(t), th.pop(t))
                tx[t] = V.do(vec.tensor_tensor(en[:, t % 6, :], en[:, t % 6, :], k.ps[bk][:, 0:D], ALU.mult))
                A.wait(tx[t])
                k.pst[bk] = A.do(nc.scalar.copy(lin[:, t, :], k.ps[bk][:, D:D + 8]))

            def total(t):
                V.wait(tx.pop(t))
                ef[t % 6] = V.do(vec.tensor_reduce(Lv[:, :, t], en[:, t % 6, :].rearrange("p (h c) -> p h c", h=8),
                                                   AX, ALU.add))
            pipeline(T, (0, fetch), (0, attrs), (0, rows.mark), (2, rows.turn), (5, spread), (6, relu), (7, weigh),
                     (9, total), (12, take))
            V.wait(list(tg.values()), A.now(), V.now())
            V.do(vec.tensor_tensor(Lv, Lv, lin[:, :, :].rearrange("p t h -> p h t"), ALU.add))
            vs(vec.tensor_tensor, Lv, Lv, AS[:, :, :].rearrange("p t h -> p h t"), ALU.add)
            vs(vec.scalar_tensor_tensor, out=L[:, :], in0=L[:, :], scalar=0.2, in1=L[:, :], op0=ALU.mult, op1=ALU.max)
            vs(vec.tensor_tensor, Lv, Lv, bc(k.loopneg[:, :].unsqueeze(1), [128, 8, T]), ALU.add)
            fence(k)
        seg_softmax(k, "g3", L[:, :], 8, 16, T, k.m_flags, ALU.max, 1e-10)
        h = sb("h", [128, NB * D])
        seg_sum(k, T, table, 3200, k.xsrc, k.dlR, k.off256, h, Rw=264, alpha=L[:, :], H=8, kept=kept)
        add_bias(k, h[:, :], a['L3_gnn_bias'])
        vs(vec.tensor_tensor, x, x, h[:, :], ALU.add)
        fence(k)


def stage_l3_ffn(k, x, a):
    nc, V, A, P, G, S = k.nc, k.V, k.A, k.P, k.G, k.S
    vec = nc.vector
    T, E, Hd = 56, 8, 1024
    x3 = x.rearrange("p (b c) -> p b c", b=NB)
    xs = k.moe_in
    ys = nc.dram_tensor("moe_out", (128 * T, D), F).ap()
    with ExitStack() as es:
        def sb(n, shape, dt=F):
            return es.enter_context(nc.sbuf_tensor(k.nm(n), shape, dt))

        def vs(op, *args, **kw):
            V.wait(V.now())
            return V.do(op(*args, **kw))
        w1 = sb("w1", [128, 2, E * Hd])
        w2 = sb("w2", [128, 8, E * D])
        bs = sb("bs", [96, Hd + D], BF)
        wt = sb("wt", [128, NB, 2])
        pos = sb("pos", [128, 2, NB], U32)
        ohE = sb("ohE", [96, T], BF)
        o1 = sb("o1", [1, T], I32)
        o2 = sb("o2", [1, T], I32)
        with ExitStack() as e2:
            def s2(n, shape, dt=F):
                return e2.enter_context(nc.sbuf_tensor(k.nm(n), shape, dt))
            wg = s2("wg", [128, 2, 8])
            sc = s2("sc", [128, NB, 8])
            load_w(k, wg, a['L3_ffn_Wg'])
            bg = bcast_row(k, e2, a['L3_ffn_bg'], 8)
            tsmall = k.ld.all()
            split_biases(k, e2, bs, a['L3_ffn_b1'], a['L3_ffn_b2'])
            tw = [[k.ld.start(w1[:, c, Hd * e:Hd * (e + 1)], a['L3_ffn_W1'][e, 128 * c:128 * (c + 1), :])
                   for c in range(2)] for e in range(E)]
            xn = s2("xn", [128, NB * D])
            xT = w2[:, 0:4, :].rearrange("p c n -> p (c n)")[:, 0:6400].rearrange("p (c n) -> p c n", c=2)
            layernorm(k, x, xn[:, :])
            transpose_rows(k, xn, xT)
            P.wait(tsmall)
            V.wait(tsmall)

            def sink(b, m0, mw, ps):
                V.wait(P.now())
                return V.do(vec.tensor_tensor(sc[:, b, :], ps, bg[:, :], ALU.add))
            project(k, xT, wg, 8, sink)
            S.wait(P.now())
            for e in range(E):
                tw[e].append(k.ld.start(w2[:, :, D * e:D * (e + 1)],
                                        a['L3_ffn_W2'][e].rearrange("(c p) n -> p c n", p=128)))
            V.wait(V.now())
            mv = s2("mv", [128, NB, 8])
            mi = s2("mi", [128, NB, 8], U32)
            mf = s2("mf", [128, 2, NB])
            dn = s2("dn", [128, NB])
            for b in range(NB):
                V.do(vec.max(mv[:, b, :], sc[:, b, :]))
            V.wait(V.now())
            for b in range(NB):
                V.do(vec.max_index(mi[:, b, :], mv[:, b, :], sc[:, b, :]))
            vs(vec.tensor_copy, mf[:, :, :], mi[:, :, 0:2].rearrange("p b k -> p k b"))
            vs(vec.tensor_tensor, dn[:, :], mv[:, :, 1], mv[:, :, 0], ALU.subtract)
            A.wait(V.now())
            A.do(nc.scalar.activation(wt[:, :, 1], dn[:, :], ACT.Exp))
            V.wait(A.now())
            vs(vec.tensor_scalar, dn[:, :], wt[:, :, 1], 1.0, None, ALU.add)
            vs(vec.reciprocal, wt[:, :, 0], dn[:, :])
            vs(vec.tensor_tensor, wt[:, :, 1], wt[:, :, 1], wt[:, :, 0], ALU.mult)
            pf = route(k, e2, mf[:, :, :].rearrange("p k b -> p (k b)"), 2 * NB, E, T,
                       pos[:, :, :].rearrange("p k b -> p (k b)"), ohE, ((Hd, o1), (D, o2)))
            G.wait(V.now())
            for i in range(2):
                for b in range(NB):
                    k.ind.scatter(xs, pos[:, i, b:b + 1], xn[:, D * b:D * (b + 1)], 128 * T)
            vs(vec.tensor_scalar, pf[:, :], pf[:, :], float(128 * T - 1), None, ALU.min)
            V.wait(G.now())
            G.wait(V.now())
            tind = k.ind.all()
            V.wait(tind)
            vs(vec.tensor_copy, pos[:, :, :].rearrange("p k b -> p (k b)"), pf[:, :])
            fence(k)
        xt = sb("xt", [128, 3, D])
        xTt = sb("xTt", [128, 3, D])
        hb = sb("hb", [128, 2, Hd])
        hT = sb("hT", [128, 2, Hd])
        yb = sb("yb", [128, 3, D])
        off1 = Offsets(k, mybir.EngineType.PE, o1, 7 * Hd)
        off2 = Offsets(k, mybir.EngineType.PE, o2, 7 * D)
        tx, tt, tg, th, tq = {}, {}, {}, {}, {}
        xfree = [None] * 3
        xtfree = [None] * 3
        hfree = [None] * 2
        htfree = [None] * 2
        yfree = [None] * 3
        def fetch(t):
            S.wait(xfree[t % 3])
            tx[t] = k.ld.start(xt[:, t % 3, :], xs[128 * t:128 * (t + 1), :])

        def turn(t):
            P.wait(tx.pop(t), k.pst[0])
            for c in range(2):
                xfree[t % 3] = P.do(nc.tensor.transpose(k.ps[0][:, 128 * c:128 * (c + 1)],
                                                        xt[:, t % 3, 128 * c:128 * (c + 1)], k.ident[:, :]))
            V.wait(xfree[t % 3], xtfree[t % 3])
            k.pst[0] = tt[t] = V.do(vec.tensor_copy(xTt[:, t % 3, :], k.ps[0][:, 0:D]))

        def hidden(t):
            P.wait(tt.pop(t), tw[min(t, E - 1)])
            o = off1(t)
            for h in range(2):
                bk = 1 + 2 * (t % 2) + h
                P.wait(k.pst[bk])
                mm(k, k.ps[bk][:, :], bc(ohE[:, t:t + 1], [96, 128]), bs[:, 512 * h:512 * (h + 1)], stop=False)
                for c in range(2):
                    view = w1[:, c, 512 * h:512 * h + 7 * Hd + 512]
                    xtfree[t % 3] = mm(k, k.ps[bk][:, :], xTt[:, t % 3, 128 * c:128 * (c + 1)],
                                       view[:, bass.ds(o, 512)], start=False, stop=(c == 1))
                A.wait(P.now(), hfree[t % 2])
                k.pst[bk] = tg[t] = A.do(nc.scalar.activation(hb[:, t % 2, 512 * h:512 * (h + 1)], k.ps[bk][:, :],
                                                              ACT.Gelu))

        def turn_hidden(t):
            P.wait(tg.pop(t))
            for h in range(2):
                bk = 5 + h
                P.wait(k.pst[bk])
                for c in range(4):
                    s = slice(512 * h + 128 * c, 512 * h + 128 * (c + 1))
                    hfree[t % 2] = P.do(nc.tensor.transpose(k.ps[bk][:, 128 * c:128 * (c + 1)], hb[:, t % 2, s],
                                                            k.ident[:, :]))
                V.wait(P.now(), htfree[t % 2])
                k.pst[bk] = th[t] = V.do(vec.tensor_copy(hT[:, t % 2, 512 * h:512 * (h + 1)], k.ps[bk][:, :]))

        def output(t):
            P.wait(th.pop(t), k.pst[7])
            o = off2(t)
            mm(k, k.ps[7][:, 0:D], bc(ohE[:, t:t + 1], [96, 128]), bs[:, Hd:Hd + D], stop=False)
            for c in range(8):
                htfree[t % 2] = mm(k, k.ps[7][:, 0:D], hT[:, t % 2, 128 * c:128 * (c + 1)],
                                   w2[:, c, bass.ds(o, D)], start=False, stop=(c == 7))
            V.wait(P.now(), yfree[t % 3])
            k.pst[7] = V.do(vec.tensor_copy(yb[:, t % 3, :], k.ps[7][:, 0:D]))
            S.wait(V.now())
            yfree[t % 3] = k.ld.start(ys[128 * t:128 * (t + 1), :], yb[:, t % 3, :])
        pipeline(T, (0, fetch), (2, turn), (3, hidden), (4, turn_hidden), (5, output))
        fence(k)
        back = sb("back", [128, 8, D])
        free = [None] * 8
        n = 0
        for b in range(NB):
            for i in range(2):
                G.wait(free[n % 8])
                V.wait(k.ind.gather(back[:, n % 8, :], ys, pos[:, i, b:b + 1], 128 * T), V.now())
                free[n % 8] = V.do(vec.scalar_tensor_tensor(out=x3[:, b, :], in0=back[:, n % 8, :],
                                                            scalar=wt[:, b, i:i + 1], in1=x3[:, b, :],
                                                            op0=ALU.mult, op1=ALU.add))
                n += 1
        fence(k)


STAGES = [stage_l0_gnn, stage_l0_ffn, stage_l1_gnn, stage_l1_ffn, stage_l2_gnn, stage_l2_ffn, stage_l3_gnn,
          stage_l3_ffn]


def build(nc, a, out, stages=tuple(range(8))):
    k = make_ctx(nc)
    n = [0]

    def nm(s):
        n[0] += 1
        return f"{s}_{n[0]}"
    k.nm = nm
    constants(k)
    x = nc.alloc_sbuf_tensor("x", [128, NB * D], F)
    both_graphs(k, a, x)
    if 1 not in stages:
        send(k, k.late, k.second, range(k.second.sent, k.second.J))
    x3 = x[:, :].rearrange("p (b c) -> p b c", b=NB)
    k.V.do(nc.vector.memset(x[:, 24 * D:], 0.0))
    k.S.wait(k.V.now())
    k.ld.start(x3[:, 0:24, :], a['x'][0:3072, :].rearrange("(b p) c -> p b c", p=128))
    k.ld.start(x[0:LASTP, 24 * D:], a['x'][3072:N, :])
    fence(k)
    for i in stages:
        if i in (5, 7) and i == stages[0]:
            with ExitStack() as es:
                clear_rows(k, es)
                fence(k)
        if i == 7:
            for q in (k.V, k.A, k.P, k.G, k.S):
                q.wait(k.late.all())
            fence(k)
            k.edges.close()
        STAGES[i](k, x[:, :], a)
    k.ld.start(out[0:3072, :].rearrange("(b p) c -> p b c", p=128), x3[:, 0:24, :])
    k.ld.start(out[3072:N, :], x[0:LASTP, 24 * D:])
    fence(k)
    k.S.wait(k.late.all())


_INS = ['x', 'src', 'dst', 'edge_attr_3', 'edge_type_8', 'L0_gnn_Wl1', 'L0_gnn_Wr1', 'L0_gnn_att1', 'L0_gnn_b1', 'L0_gnn_Wl2', 'L0_gnn_Wr2', 'L0_gnn_att2', 'L0_gnn_b2', 'L0_ffn_W_fx', 'L0_ffn_b_fx', 'L0_ffn_W_x', 'L0_ffn_b_x', 'L0_ffn_W_slice', 'L0_ffn_b_slice', 'L0_ffn_W_q', 'L0_ffn_W_k', 'L0_ffn_W_v', 'L0_ffn_W_out', 'L0_ffn_b_out', 'L0_ffn_temperature', 'L1_gnn_weight', 'L1_gnn_h_bias', 'L1_gnn_loop_weight', 'L1_ffn_W_gat', 'L1_ffn_att_src', 'L1_ffn_att_dst', 'L1_ffn_b_gat', 'L1_ffn_ln_gamma', 'L1_ffn_ln_beta', 'L1_ffn_W1', 'L1_ffn_b1', 'L1_ffn_W2', 'L1_ffn_b2', 'L1_ffn_edge_index', 'L2_gnn_W1', 'L2_gnn_b1', 'L2_gnn_W2', 'L2_gnn_b2', 'L2_ffn_router_w', 'L2_ffn_router_b', 'L2_ffn_W1', 'L2_ffn_b1', 'L2_ffn_W2', 'L2_ffn_b2', 'L3_gnn_W', 'L3_gnn_a_src', 'L3_gnn_a_dst', 'L3_gnn_edge_W', 'L3_gnn_edge_b', 'L3_gnn_bias', 'L3_ffn_Wg', 'L3_ffn_bg', 'L3_ffn_W1', 'L3_ffn_b1', 'L3_ffn_W2', 'L3_ffn_b2']


def kernel(**inputs):
    import numpy as _np
    import concourse.bacc as _bacc
    from concourse import mybir as _mybir
    from concourse.bass_utils import run_bass_kernel_spmd as _run

    nc = _bacc.Bacc("TRN2", target_bir_lowering=False, num_devices=1)
    arrays, args = {}, {}
    for name in _INS:
        v = _np.ascontiguousarray(inputs[name])
        arrays[f"in_{name}_dram"] = v
        args[name] = nc.dram_tensor(f"in_{name}_dram", v.shape, _mybir.dt.from_np(v.dtype), kind="ExternalInput").ap()
    out = nc.dram_tensor("out_0_dram", (3125, 256), _mybir.dt.float32, kind="ExternalOutput").ap()
    build(nc, args, out)
    r = _run(nc, [arrays], core_ids=[0])
    return r.results[0]["out_0_dram"]
```
